# Optimizing a Trainium2 kernel written in Bass

```python
import numpy as np
import jax
import jax.numpy as jnp

def _softmax(x, axis=-1):
    return jax.nn.softmax(x, axis=axis)

def _gelu(x):
    return jax.nn.gelu(x, approximate=True)

def _silu(x):
    return jax.nn.silu(x)

def _sigmoid(x):
    return jax.nn.sigmoid(x)

def _layernorm(x, axis=-1, eps=1e-05):
    m = jnp.mean(x, axis=axis, keepdims=True)
    v = jnp.var(x, axis=axis, keepdims=True)
    return (x - m) / jnp.sqrt(v + eps)

def _scatter_add(tgt, idx, src, axis=0):
    return tgt.at[idx].add(src)

def _segment_sum(src, seg, n):
    return jax.ops.segment_sum(src, seg, n)
kernel_name = 'mk_gnn_preln_d4_gnn_r8_7be420'

def setup_inputs(seed: int=0):
    np.random.seed(seed)
    _w = jnp.asarray

    def _rec_inputs():
        import jax
        import jax.numpy as jnp
        _gk = jax.random.key(seed)
        x = -0.000202 + 1 * jax.random.normal(jax.random.fold_in(_gk, 1), (12500, 64), jnp.float32)
        src = jax.random.randint(jax.random.fold_in(_gk, 2), (200000,), 0, 12500, jnp.int32)
        dst = jnp.minimum((12500 * jax.random.uniform(jax.random.fold_in(_gk, 3), (200000,)) ** 2.0).astype(jnp.int32), 99999)
        _o = jnp.argsort(dst, stable=True)
        src = src[_o]
        dst = dst[_o]
        return (x, src, dst)
    x, src, dst = _rec_inputs()

    def _L0_gnn_setup():
        import jax, jax.numpy as jnp
        import numpy as np
        N = 12500
        D = 64
        H = 128
        E = 200000
        key = jax.random.key(seed)
        k_nodes, k_edges, k_w1, k_w2 = jax.random.split(key, 4)
        nodes = jax.random.normal(k_nodes, (N, D), dtype=jnp.float32)
        edges = jax.random.randint(k_edges, (E, 2), 0, N, dtype=jnp.int32)
        W1 = jax.random.normal(k_w1, (2 * D, H), dtype=jnp.float32) * (1.0 / np.sqrt(2 * D))
        b1 = jnp.zeros((H,), dtype=jnp.float32)
        W2 = jax.random.normal(k_w2, (H, D), dtype=jnp.float32) * (1.0 / np.sqrt(H))
        b2 = jnp.zeros((D,), dtype=jnp.float32)
        return {'nodes': nodes, 'edges': edges, 'W1': W1, 'b1': b1, 'W2': W2, 'b2': b2}
    _L0_gnn_all = _L0_gnn_setup()
    _L0_gnn_in = {k: v for k, v in _L0_gnn_all.items() if k in ('W1', 'b1', 'W2', 'b2')}
    del _L0_gnn_all

    def _L1_gnn_setup():
        import jax, jax.numpy as jnp
        import numpy as np
        N_NODES = 12500
        N_EDGES = 125000
        D = 64

        def _graph_conv(h, src, dst, n, W_root, W_rel, b):
            agg = jax.ops.segment_sum(h[src], dst, num_segments=n)
            return h @ W_root.T + agg @ W_rel.T + b
        key = jax.random.key(seed)
        ks = jax.random.split(key, 8)
        s = 1.0 / np.sqrt(D)
        x = jax.random.normal(ks[0], (N_NODES, D), dtype=jnp.float32)
        edge_index = jax.random.randint(ks[1], (2, N_EDGES), 0, N_NODES, dtype=jnp.int64)
        W1_root = jax.random.uniform(ks[2], (D, D), jnp.float32, -s, s)
        W1_rel = jax.random.uniform(ks[3], (D, D), jnp.float32, -s, s)
        b1 = jax.random.uniform(ks[4], (D,), jnp.float32, -s, s)
        W2_root = jax.random.uniform(ks[5], (D, D), jnp.float32, -s, s)
        W2_rel = jax.random.uniform(ks[6], (D, D), jnp.float32, -s, s)
        b2 = jax.random.uniform(ks[7], (D,), jnp.float32, -s, s)
        return {'x': x, 'edge_index': edge_index, 'dropout': 0, 'W1_root': W1_root, 'W1_rel': W1_rel, 'b1': b1, 'W2_root': W2_root, 'W2_rel': W2_rel, 'b2': b2}
    _L1_gnn_all = _L1_gnn_setup()
    _L1_gnn_in = {k: v for k, v in _L1_gnn_all.items() if k in ('W1_root', 'W1_rel', 'b1', 'W2_root', 'W2_rel', 'b2')}
    del _L1_gnn_all

    def _L2_gnn_setup():
        import jax, jax.numpy as jnp
        import numpy as np
        N_NODES = 6250
        N_EDGES = 100000
        D_IN = 64
        D_OUT = 64
        ALPHA = 0.5

        def _dir_norm_spmm(x, row, col, n):
            ones = jnp.ones(row.shape[0], dtype=x.dtype)
            out_deg = jax.ops.segment_sum(ones, row, num_segments=n)
            in_deg = jax.ops.segment_sum(ones, col, num_segments=n)
            dinv_out = jnp.where(out_deg > 0, jax.lax.rsqrt(jnp.maximum(out_deg, 1.0)), 0.0)
            dinv_in = jnp.where(in_deg > 0, jax.lax.rsqrt(jnp.maximum(in_deg, 1.0)), 0.0)
            w = dinv_out[row] * dinv_in[col]
            msgs = w[:, None] * x[col]
            return jax.ops.segment_sum(msgs, row, num_segments=n)
        key = jax.random.key(seed)
        k1, k2, k3, k4, k5, k6 = jax.random.split(key, 6)
        x = jax.random.normal(k1, (N_NODES, D_IN), dtype=jnp.float32)
        edge_index = jax.random.randint(k2, (2, N_EDGES), 0, N_NODES, dtype=jnp.int64)
        s = 1.0 / np.sqrt(D_IN)
        W_src = jax.random.uniform(k3, (D_IN, D_OUT), dtype=jnp.float32, minval=-s, maxval=s)
        b_src = jax.random.uniform(k4, (D_OUT,), dtype=jnp.float32, minval=-s, maxval=s)
        W_dst = jax.random.uniform(k5, (D_IN, D_OUT), dtype=jnp.float32, minval=-s, maxval=s)
        b_dst = jax.random.uniform(k6, (D_OUT,), dtype=jnp.float32, minval=-s, maxval=s)
        return {'x': x, 'edge_index': edge_index, 'W_src': W_src, 'b_src': b_src, 'W_dst': W_dst, 'b_dst': b_dst}
    _L2_gnn_all = _L2_gnn_setup()
    _L2_gnn_in = {k: v for k, v in _L2_gnn_all.items() if k in ('W_src', 'b_src', 'W_dst', 'b_dst')}
    del _L2_gnn_all

    def _L3_gnn_setup():
        import jax, jax.numpy as jnp
        import numpy as np
        N_NODES = 12500
        N_EDGES = 200000
        IN_DIM = 64
        OUT_DIM = 64
        T_STEPS = 4
        W_SCALE = 0.01
        key = jax.random.key(seed)
        k0, k1, k2, k3, k4, k5 = jax.random.split(key, 6)
        Xv = jax.random.normal(k0, (N_NODES, IN_DIM), dtype=jnp.float32)
        edge_index = jax.random.randint(k1, (2, N_EDGES), 0, N_NODES, dtype=jnp.int64)
        W1 = jax.random.normal(k2, (OUT_DIM, IN_DIM), dtype=jnp.float32) * W_SCALE
        W2 = jax.random.normal(k3, (OUT_DIM, OUT_DIM), dtype=jnp.float32) * W_SCALE
        W3 = jax.random.normal(k4, (OUT_DIM, OUT_DIM), dtype=jnp.float32) * W_SCALE
        W4 = jax.random.normal(k5, (OUT_DIM, 1), dtype=jnp.float32) * W_SCALE
        return {'Xv': Xv, 'edge_index': edge_index, 'W1': W1, 'W2': W2, 'W3': W3, 'W4': W4}
    _L3_gnn_all = _L3_gnn_setup()
    _L3_gnn_in = {k: v for k, v in _L3_gnn_all.items() if k in ('W1', 'W2', 'W3', 'W4')}
    del _L3_gnn_all
    return {'x': x, 'src': src, 'dst': dst, 'L0_gnn_W1': _L0_gnn_in['W1'], 'L0_gnn_b1': _L0_gnn_in['b1'], 'L0_gnn_W2': _L0_gnn_in['W2'], 'L0_gnn_b2': _L0_gnn_in['b2'], 'L1_gnn_W1_root': _L1_gnn_in['W1_root'], 'L1_gnn_W1_rel': _L1_gnn_in['W1_rel'], 'L1_gnn_b1': _L1_gnn_in['b1'], 'L1_gnn_W2_root': _L1_gnn_in['W2_root'], 'L1_gnn_W2_rel': _L1_gnn_in['W2_rel'], 'L1_gnn_b2': _L1_gnn_in['b2'], 'L2_gnn_W_src': _L2_gnn_in['W_src'], 'L2_gnn_b_src': _L2_gnn_in['b_src'], 'L2_gnn_W_dst': _L2_gnn_in['W_dst'], 'L2_gnn_b_dst': _L2_gnn_in['b_dst'], 'L3_gnn_W1': _L3_gnn_in['W1'], 'L3_gnn_W2': _L3_gnn_in['W2'], 'L3_gnn_W3': _L3_gnn_in['W3'], 'L3_gnn_W4': _L3_gnn_in['W4']}

def reference(x, src, dst, L0_gnn_W1, L0_gnn_b1, L0_gnn_W2, L0_gnn_b2, L1_gnn_W1_root, L1_gnn_W1_rel, L1_gnn_b1, L1_gnn_W2_root, L1_gnn_W2_rel, L1_gnn_b2, L2_gnn_W_src, L2_gnn_b_src, L2_gnn_W_dst, L2_gnn_b_dst, L3_gnn_W1, L3_gnn_W2, L3_gnn_W3, L3_gnn_W4):
    import jax
    import jax.numpy as jnp

    def _L0_gnn_ref(nodes, edges, W1, b1, W2, b2):
        import jax, jax.numpy as jnp
        import numpy as np
        N = 12500
        D = 64
        H = 128
        E = 200000
        i = edges[:, 0]
        j = edges[:, 1]
        h_i = nodes[i]
        h_j = nodes[j]

        def mlp(x):
            return jax.nn.relu(x @ W1 + b1) @ W2 + b2
        m_ij = mlp(jnp.concatenate([h_i, h_j], axis=-1))
        m_ji = mlp(jnp.concatenate([h_j, h_i], axis=-1))
        out = nodes + jax.ops.segment_sum(m_ij, i, num_segments=N) + jax.ops.segment_sum(m_ji, j, num_segments=N)
        return out

    def _L1_gnn_ref(x, edge_index, dropout, W1_root, W1_rel, b1, W2_root, W2_rel, b2):
        import jax, jax.numpy as jnp
        import numpy as np
        N_NODES = 12500
        N_EDGES = 125000
        D = 64

        def _graph_conv(h, src, dst, n, W_root, W_rel, b):
            agg = jax.ops.segment_sum(h[src], dst, num_segments=n)
            return h @ W_root.T + agg @ W_rel.T + b
        n = x.shape[0]
        src, dst = (edge_index[0], edge_index[1])
        h = jax.nn.relu(_graph_conv(x, src, dst, n, W1_root, W1_rel, b1))
        out = jax.nn.relu(_graph_conv(h, src, dst, n, W2_root, W2_rel, b2))
        return out

    def _L2_gnn_ref(x, edge_index, W_src, b_src, W_dst, b_dst):
        import jax, jax.numpy as jnp
        import numpy as np
        N_NODES = 6250
        N_EDGES = 100000
        D_IN = 64
        D_OUT = 64
        ALPHA = 0.5

        def _dir_norm_spmm(x, row, col, n):
            ones = jnp.ones(row.shape[0], dtype=x.dtype)
            out_deg = jax.ops.segment_sum(ones, row, num_segments=n)
            in_deg = jax.ops.segment_sum(ones, col, num_segments=n)
            dinv_out = jnp.where(out_deg > 0, jax.lax.rsqrt(jnp.maximum(out_deg, 1.0)), 0.0)
            dinv_in = jnp.where(in_deg > 0, jax.lax.rsqrt(jnp.maximum(in_deg, 1.0)), 0.0)
            w = dinv_out[row] * dinv_in[col]
            msgs = w[:, None] * x[col]
            return jax.ops.segment_sum(msgs, row, num_segments=n)
        row, col = (edge_index[0], edge_index[1])
        n = x.shape[0]
        adj_norm_x = _dir_norm_spmm(x, row, col, n)
        adj_t_norm_x = _dir_norm_spmm(x, col, row, n)
        out = ALPHA * (adj_norm_x @ W_src + b_src) + (1.0 - ALPHA) * (adj_t_norm_x @ W_dst + b_dst)
        return out

    def _L3_gnn_ref(Xv, edge_index, W1, W2, W3, W4):
        import jax, jax.numpy as jnp
        import numpy as np
        N_NODES = 12500
        N_EDGES = 200000
        IN_DIM = 64
        OUT_DIM = 64
        T_STEPS = 4
        W_SCALE = 0.01
        n = Xv.shape[0]
        row = edge_index[0]
        col = edge_index[1]
        deg = jax.ops.segment_sum(jnp.ones(row.shape, Xv.dtype), row, num_segments=n)
        w4 = W4[:, 0]
        v3 = deg[:, None] * jax.nn.relu(w4)[None, :] @ W3.T
        base = Xv @ W1.T + v3
        emb = jnp.zeros((n, W1.shape[0]), Xv.dtype)
        for _ in range(T_STEPS):
            neigh = jax.ops.segment_sum(emb[col], row, num_segments=n)
            emb = jax.nn.relu(base + neigh @ W2.T)
        return emb
    edge_index = jnp.stack([src, dst])
    edge_index_t = jnp.stack([src, dst], axis=1)
    h = jnp.maximum(_layernorm(x, axis=-1), 0.0)
    x = x + _L0_gnn_ref(h, edge_index_t, L0_gnn_W1, L0_gnn_b1, L0_gnn_W2, L0_gnn_b2)
    h = jnp.maximum(_layernorm(x, axis=-1), 0.0)
    x = x + _L1_gnn_ref(h, edge_index, 0, L1_gnn_W1_root, L1_gnn_W1_rel, L1_gnn_b1, L1_gnn_W2_root, L1_gnn_W2_rel, L1_gnn_b2)
    h = jnp.maximum(_layernorm(x, axis=-1), 0.0)
    x = x + _L2_gnn_ref(h, edge_index, L2_gnn_W_src, L2_gnn_b_src, L2_gnn_W_dst, L2_gnn_b_dst)
    h = jnp.maximum(_layernorm(x, axis=-1), 0.0)
    x = x + _L3_gnn_ref(h, edge_index, L3_gnn_W1, L3_gnn_W2, L3_gnn_W3, L3_gnn_W4)
    return x

_drawn_inputs = setup_inputs


def setup_inputs(seed=0):
    import zlib

    import numpy as np

    out = dict(_drawn_inputs(seed))
    spreads = {'L0_gnn_b1': (0.0, 0.1), 'L0_gnn_b2': (0.0, 0.1)}
    factors = {'L1_gnn_b1': 4.966,
     'L1_gnn_b2': 30.759,
     'L2_gnn_W_src': 8.0,
     'L2_gnn_b_src': 64.0,
     'L2_gnn_W_dst': 8.0,
     'L2_gnn_b_dst': 64.0,
     'L3_gnn_W1': 8.0,
     'L3_gnn_W2': 8.0,
     'L3_gnn_W3': 8.0,
     'L3_gnn_W4': 8.0}
    for name, (base, spread) in spreads.items():
        noise = np.random.default_rng([zlib.crc32(name.encode()), seed]).standard_normal(out[name].shape)
        drawn = base * np.exp(spread * noise) if base else spread * noise
        out[name] = jnp.asarray(drawn.astype(out[name].dtype))
    for name, factor in factors.items():
        out[name] = (out[name] * factor).astype(out[name].dtype)
    return out
```

```python
import concourse.bass as bass
from concourse import mybir
from contextlib import ExitStack

F32 = mybir.dt.float32
BF16 = mybir.dt.bfloat16
I32 = mybir.dt.int32
ALU = mybir.AluOpType
ACT = mybir.ActivationFunctionType
AX = mybir.AxisListType

P = 128
N = 12500
D = 64
H = 128
E = 200000
GROUP = 17
BUFS = 4
EDGE_COLS = 1564
ROUNDS = EDGE_COLS // (BUFS * GROUP)
EDGES = P * EDGE_COLS
LAST_EDGES = E - (P - 1) * EDGE_COLS
NODE_COLS = (N + P - 1) // P
NODES = P * NODE_COLS
LAST_NODES = N - (NODE_COLS - 1) * P
NO_NODE = P * P - 1
CHUNK = 7
CHUNK_PAIRS = NODE_COLS // (2 * CHUNK)
DIGIT_BITS = 7
TILES = EDGES // P
BLOCKS = (TILES + P - 1) // P
LAST_TILES = TILES - (BLOCKS - 1) * P
EPS = 1e-5

assert EDGE_COLS == BUFS * GROUP * ROUNDS and EDGES >= E and 0 < LAST_EDGES <= EDGE_COLS
assert NODE_COLS == 2 * CHUNK * CHUNK_PAIRS


class Link:

    def __init__(self, eng, sem):
        self.eng, self.sem, self.before, self.n = eng, sem, 0, 0

    def __call__(self, ins):
        self.n += 1
        ins.then_inc(self.sem, 1)
        self.eng.wait_ge(self.sem, self.before + self.n)

    def start_loop(self):
        self.done, self.n = self.before + self.n, 0

    def iteration(self, i, steps):
        self.before, self.n = self.done + i * steps, 0

    def end_loop(self, rounds, steps):
        assert self.n == steps, (self.n, steps)
        self.before, self.n = self.done + rounds * steps, 0


class Scope:

    def __init__(self, nc, ctx, prefix):
        self.nc, self.ctx, self.prefix, self.sems = nc, ctx, prefix, []

    def sb(self, name, shape, dtype):
        return self.ctx.enter_context(self.nc.sbuf_tensor(self.prefix + name, shape, dtype))

    def ps(self, name, shape, dtype):
        return self.ctx.enter_context(self.nc.psum_tensor(self.prefix + name, shape, dtype))

    def sem(self, name):
        if not self.sems:
            self.ctx.callback(self.clear)
        self.sems.append(self.nc.alloc_semaphore(self.prefix + name))
        return self.sems[-1]

    def clear(self):
        self.nc.clear_and_free_semaphores(self.sems)
        self.nc.all_engine_barrier()


def part_wait(eng):
    eng.nop(nofuse=True)


def rows(ap):
    return bass.IndirectOffsetOnAxis(ap=ap, axis=0)


class Constants:
    def __init__(self, s):
        self.row = s.sb("row", [P, P], F32)
        self.row_b = s.sb("row_b", [P, P], BF16)
        self.part = s.sb("part", [P, 1], F32)
        self.part_start = s.sb("part_start", [P, 1], F32)
        self.ident = s.sb("ident", [P, P], F32)
        self.ident_b = s.sb("ident_b", [P, P], BF16)
        self.up_to = s.sb("up_to", [P, P], F32)
        self.before = s.sb("before", [P, P], F32)
        self.after = s.sb("after", [P, P], F32)
        self.ones = s.sb("ones", [P, P], F32)
        self.eps = s.sb("eps", [P, 1], F32)


class Nodes:

    def __init__(self, s, side):
        self.count = s.sb(f"count_{side}", [P, NODE_COLS], F32)
        self.start = s.sb(f"start_{side}", [P, NODE_COLS], F32)
        self.inv_root = s.sb(f"inv_root_{side}", [P, NODE_COLS], F32)
        self.start_row = s.sb(f"start_row_{side}", [P, NODE_COLS], I32)
        self.end_row = s.sb(f"end_row_{side}", [P, NODE_COLS], I32)


class EdgeColumns:

    def __init__(self, s):
        self.src_col = s.sb("src_col", [P, TILES], F32)
        self.payload = s.sb("payload", [P, TILES, 2], I32)
        self.low = [s.sb(f"low{k}", [P, TILES], BF16) for k in range(2)]
        self.high = [s.sb(f"high{k}", [P, TILES], BF16) for k in range(2)]


class Order:

    def __init__(self, s, side):
        self.name = side
        self.gather_rows = s.sb(f"gather_rows_{side}", [P, EDGE_COLS], I32)
        self.same = s.sb(f"same_{side}", [P, EDGE_COLS], F32)
        self.first_row = s.sb(f"first_row_{side}", [P, 1], I32)
        self.first_end = s.sb(f"first_end_{side}", [P, 1], I32)
        self.carry = s.sb(f"carry_{side}", [P, P], F32)


class Weights:
    def __init__(self, s):
        self.edge_in = s.sb("edge_in", [D, 2 * H], F32)
        self.edge_out = s.sb("edge_out", [H, D], F32)
        self.directed = s.sb("directed", [2 * D, D], F32)
        self.edge_bias = s.sb("edge_bias", [P, H], F32)
        self.edge_out_bias = s.sb("edge_out_bias", [P, D], F32)
        self.conv_bias = [s.sb(f"conv_bias{k}", [P, D], F32) for k in range(2)]
        self.directed_bias = s.sb("directed_bias", [P, D], F32)
        self.conv = [s.sb(f"conv{k}", [2 * D, D], F32) for k in range(2)]
        self.steps = s.sb("steps", [2 * D, D], F32)
        self.degree_row = s.sb("degree_row", [P, D], F32)


def constants(nc, cst):
    with ExitStack() as ctx:
        s = Scope(nc, ctx, "cst_")
        row_i = s.sb("row_i", [P, P], I32)
        part_i = s.sb("part_i", [P, 1], I32)
        pos_i = s.sb("pos_i", [P, 1], I32)
        iota_done, link_sem = s.sem("iota_done"), s.sem("link")
        block = ctx.enter_context(nc.Block())

        @block.gpsimd
        def _(pool):
            pool.iota(row_i[:, :], pattern=[[1, P]], base=0, channel_multiplier=0).then_inc(iota_done, 1)
            pool.iota(part_i[:, :], pattern=[[0, 1]], base=0, channel_multiplier=1).then_inc(iota_done, 1)
            pool.iota(pos_i[:, :], pattern=[[0, 1]], base=0, channel_multiplier=EDGE_COLS).then_inc(iota_done, 1)

        @block.vector
        def _(dve):
            link = Link(dve, link_sem)
            dve.wait_ge(iota_done, 3)
            nc.vector.tensor_copy(cst.row[:, :], row_i[:, :])
            nc.vector.tensor_copy(cst.row_b[:, :], row_i[:, :])
            nc.vector.tensor_copy(cst.part_start[:, :], pos_i[:, :])
            link(nc.vector.tensor_copy(cst.part[:, :], part_i[:, :]))
            nc.vector.tensor_scalar(cst.ident[:, :], cst.row[:, :], cst.part[:, 0:1], None, ALU.is_equal)
            nc.vector.tensor_scalar(cst.ident_b[:, :], cst.row[:, :], cst.part[:, 0:1], None, ALU.is_equal)
            nc.vector.tensor_scalar(cst.up_to[:, :], cst.row[:, :], cst.part[:, 0:1], None, ALU.is_ge)
            nc.vector.tensor_scalar(cst.before[:, :], cst.row[:, :], cst.part[:, 0:1], None, ALU.is_gt)
            nc.vector.tensor_scalar(cst.after[:, :], cst.row[:, :], cst.part[:, 0:1], None, ALU.is_lt)
            nc.vector.memset(cst.eps[:, :], EPS)
            link(nc.vector.memset(cst.ones[:, :], 1.0))


def load_edges(nc, cst, raw, src, dst, key_rows):
    with ExitStack() as ctx:
        s = Scope(nc, ctx, "ld_")
        tiles_i = [s.sb(f"tiles_i{k}", [P, BLOCKS, P], I32) for k in range(2)]
        tiles_f = [s.sb(f"tiles_f{k}", [P, BLOCKS, P], F32) for k in range(2)]
        col_i = s.sb("col_i", [P, TILES], I32)
        digit_i = s.sb("digit_i", [P, TILES], I32)
        table_row = s.sb("table_row", [P, TILES], F32)
        turned = s.ps("turned", [P, BLOCKS, P], F32)
        padded, loaded, converted = s.sem("padded"), s.sem("loaded"), s.sem("converted")
        turned_done, read_done, rows_stored, link_sem = s.sem("turned"), s.sem("read"), s.sem("stored"), s.sem("link")
        full = (E // P) // P * P * P
        whole_tiles = (E - full) // P
        rest = E - full - whole_tiles * P
        block = ctx.enter_context(nc.Block())

        @block.gpsimd
        def _(pool):
            for k in range(2):
                pool.memset(tiles_i[k][:, BLOCKS - 1, :], NO_NODE).then_inc(padded, 1)

        @block.sync
        def _(sp):
            sp.wait_ge(padded, 2)
            for k, edges in enumerate((src, dst)):
                sp.dma_start(tiles_i[k][:, 0:BLOCKS - 1, :],
                             edges[0:full].rearrange("(b g p) -> g b p", b=BLOCKS - 1, p=P)).then_inc(loaded, 16)
                sp.dma_start(tiles_i[k][0:whole_tiles, BLOCKS - 1, :],
                             edges[full:full + whole_tiles * P].rearrange("(g p) -> g p", p=P)).then_inc(loaded, 16)
                sp.dma_start(tiles_i[k][whole_tiles:whole_tiles + 1, BLOCKS - 1, 0:rest],
                             edges[full + whole_tiles * P:E].rearrange("(a p) -> a p", a=1)).then_inc(loaded, 16)
            sp.wait_ge(converted, 2)
            sp.dma_start(key_rows[0:(BLOCKS - 1) * P * P].rearrange("(b g p) -> g b p", b=BLOCKS - 1, p=P),
                         tiles_f[0][:, 0:BLOCKS - 1, :]).then_inc(rows_stored, 16)
            sp.dma_start(key_rows[(BLOCKS - 1) * P * P:EDGES].rearrange("(g p) -> g p", p=P),
                         tiles_f[0][0:LAST_TILES, BLOCKS - 1, :]).then_inc(rows_stored, 16)
            sp.wait_ge(rows_stored, 32)

        @block.tensor
        def _(pe):
            for k in range(2):
                pe.wait_ge(converted, 2)
                if k == 1:
                    pe.wait_ge(read_done, 1)
                for b in range(BLOCKS):
                    g = P if b < BLOCKS - 1 else LAST_TILES
                    last = nc.tensor.transpose(turned[:, b, 0:g], tiles_f[k][0:g, b, :], cst.ident[0:g, 0:g])
                last.then_inc(turned_done, 1)

        @block.vector
        def _(dve):
            link = Link(dve, link_sem)
            dve.wait_ge(loaded, 96)
            for k in range(2):
                nc.vector.tensor_copy(tiles_f[k][:, :, :], tiles_i[k][:, :, :]).then_inc(converted, 1)
            flat = turned[:, :, :].rearrange("p b g -> p (b g)")[:, 0:TILES]
            for k in range(2):
                dve.wait_ge(turned_done, k + 1)
                if k == 0:
                    nc.vector.tensor_copy(raw.src_col[:, :], flat)
                nc.vector.tensor_copy(col_i[:, :], flat).then_inc(read_done, 1)
                dve.wait_ge(read_done, k + 1)
                if k == 0:
                    nc.vector.tensor_copy(raw.payload[:, :, 0], col_i[:, :])
                for digit, op, by in ((raw.low[k], ALU.bitwise_and, P - 1),
                                      (raw.high[k], ALU.logical_shift_right, DIGIT_BITS)):
                    link(nc.vector.tensor_scalar(digit_i[:, :], col_i[:, :], by, None, op))
                    link(nc.vector.tensor_copy(digit[:, :], digit_i[:, :]))
            link(nc.vector.scalar_tensor_tensor(out=table_row[:, :], in0=raw.low[1][:, :], scalar=float(NODE_COLS),
                                                in1=raw.high[1][:, :], op0=ALU.mult, op1=ALU.add))
            link(nc.vector.tensor_scalar(raw.payload[:, :, 1], table_row[:, :], float(NODES - 1), None, ALU.min))


def count_edges(nc, cst, raw, nodes_of, zero_fill):
    with ExitStack() as ctx:
        s = Scope(nc, ctx, "cnt_")
        one_low = s.sb("one_low", [P, 2, 2, GROUP, P], BF16)
        one_high = s.sb("one_high", [P, 2, 2, GROUP, NODE_COLS], BF16)
        zero_b = s.sb("zero_b", [P, P], BF16)
        zeros = s.sb("zeros", [P, GROUP * H], F32)
        total = s.sb("total", [P, NODE_COLS], F32)
        col_end = s.sb("col_end", [P, NODE_COLS], F32)
        has = s.sb("has", [P, NODE_COLS], F32)
        work = s.sb("work", [P, NODE_COLS], F32)
        root = s.sb("root", [P, NODE_COLS], F32)
        counted = [s.ps(f"counted{k}", [P, NODE_COLS], F32) for k in range(2)]
        within = [s.ps(f"within{k}", [P, NODE_COLS], F32) for k in range(2)]
        totals = [s.ps(f"totals{k}", [P, NODE_COLS], F32) for k in range(2)]
        degree_ready, root_done = s.sem("degree"), s.sem("root")
        hot_ready, hot_free, zeroed, sums_done = s.sem("hot_ready"), s.sem("hot_free"), s.sem("zeroed"), s.sem("sums")
        counts_ready, prefix_done, filled, link_sem = s.sem("counts"), s.sem("prefix"), s.sem("filled"), s.sem("link")
        block = ctx.enter_context(nc.Block())

        @block.sync
        def _(sp):
            sp.wait_ge(zeroed, 2)
            fills, states = zero_fill
            with sp.Fori(0, EDGE_COLS // GROUP) as i:
                for fill in fills:
                    view = fill[0:EDGES, :].rearrange("(p t) f -> p (t f)", p=P)
                    sp.dma_start(view[:, bass.ds(i * (GROUP * H), GROUP * H)], zeros[:, :]).then_inc(filled, 16)
            for state, width in states:
                sp.dma_start(state[EDGES:EDGES + P, :], zeros[:, 0:width]).then_inc(filled, 16)
            sp.wait_ge(filled, 16 * (len(fills) * EDGE_COLS // GROUP + len(states)))

        @block.vector
        def _(dve):
            link = Link(dve, link_sem)
            nc.vector.memset(zero_b[:, :], 0.0).then_inc(zeroed, 1)
            nc.vector.memset(zeros[:, :], 0.0).then_inc(zeroed, 1)
            dve.sem_inc(hot_free, 2)
            row = cst.row_b[:, :].unsqueeze(1)
            with dve.Fori(0, EDGE_COLS // (2 * GROUP)) as i:
                for b in range(2):
                    dve.wait_ge(hot_free, i * 2 + b + 1)
                    at = bass.ds((i * 2 + b) * GROUP, GROUP)
                    for k in range(2):
                        nc.vector.tensor_tensor(one_low[:, b, k, :, :], row.to_broadcast([P, GROUP, P]),
                                                raw.low[k][:, at].unsqueeze(2).to_broadcast([P, GROUP, P]),
                                                ALU.is_equal)
                        last = nc.vector.tensor_tensor(
                            one_high[:, b, k, :, :], row[:, :, 0:NODE_COLS].to_broadcast([P, GROUP, NODE_COLS]),
                            raw.high[k][:, at].unsqueeze(2).to_broadcast([P, GROUP, NODE_COLS]), ALU.is_equal)
                    last.then_inc(hot_ready, 1)
            dve.wait_ge(sums_done, 1)
            for k in range(2):
                last = nc.vector.tensor_copy(nodes_of[k].count[:, :], counted[k][:, :])
            last.then_inc(counts_ready, 1)
            dve.wait_ge(counts_ready, 1)
            dve.wait_ge(prefix_done, 1)
            for k in range(2):
                o = nodes_of[k]
                link(nc.vector.tensor_copy(total[:, :], totals[k][:, :]))
                link(nc.vector.tensor_tensor_scan(out=col_end[:, :], data0=cst.ones[:, 0:NODE_COLS], data1=total[:, :],
                                                  initial=0.0, op0=ALU.mult, op1=ALU.add))
                link(nc.vector.tensor_tensor(col_end[:, :], col_end[:, :], total[:, :], ALU.subtract))
                link(nc.vector.tensor_tensor(work[:, :], col_end[:, :], within[k][:, :], ALU.add))
                link(nc.vector.tensor_tensor(o.start[:, :], work[:, :], o.count[:, :], ALU.subtract))
                link(nc.vector.tensor_scalar(has[:, :], o.count[:, :], 0.0, None, ALU.is_gt))
                link(nc.vector.tensor_scalar(work[:, :], work[:, :], -1.0 - EDGES, None, ALU.add))
                link(nc.vector.tensor_tensor(work[:, :], work[:, :], has[:, :], ALU.mult))
                link(nc.vector.tensor_scalar(o.end_row[:, :], work[:, :], float(EDGES), None, ALU.add))
                link(nc.vector.tensor_scalar(work[:, :], o.start[:, :], -float(EDGES), None, ALU.add))
                link(nc.vector.tensor_tensor(work[:, :], work[:, :], has[:, :], ALU.mult))
                link(nc.vector.tensor_scalar(o.start_row[:, :], work[:, :], float(EDGES), None, ALU.add))
                nc.vector.tensor_scalar(o.inv_root[:, :], o.count[:, :], 1.0, None, ALU.max).then_inc(degree_ready, 1)
                dve.wait_ge(root_done, k + 1)
                link(nc.vector.reciprocal(o.inv_root[:, :], root[:, :]))
                link(nc.vector.tensor_tensor(o.inv_root[:, :], o.inv_root[:, :], has[:, :], ALU.mult))

        @block.scalar
        def _(act):
            for k in range(2):
                act.wait_ge(degree_ready, k + 1)
                nc.scalar.activation(root[:, :], nodes_of[k].inv_root[:, :], ACT.Sqrt).then_inc(root_done, 1)

        @block.tensor
        def _(pe):
            pe.wait_ge(zeroed, 1)
            for k in range(2):
                nc.tensor.matmul(counted[k][:, :], zero_b[:, :], zero_b[:, 0:NODE_COLS], start=True, stop=False)
            with pe.Fori(0, EDGE_COLS // (2 * GROUP)) as i:
                for b in range(2):
                    pe.wait_ge(hot_ready, i * 2 + b + 1)
                    for k in range(2):
                        for u in range(GROUP):
                            last = nc.tensor.matmul(counted[k][:, :], one_low[:, b, k, u, :], one_high[:, b, k, u, :],
                                                    start=False, stop=False)
                    last.then_inc(hot_free, 1)
            for k in range(2):
                last = nc.tensor.matmul(counted[k][:, :], zero_b[:, :], zero_b[:, 0:NODE_COLS], start=False, stop=True)
            last.then_inc(sums_done, 1)
            pe.wait_ge(counts_ready, 1)
            for k in range(2):
                nc.tensor.matmul(within[k][:, :], cst.up_to[:, :], nodes_of[k].count[:, :], start=True, stop=True)
                last = nc.tensor.matmul(totals[k][:, :], cst.ones[:, :], nodes_of[k].count[:, :], start=True, stop=True)
            last.then_inc(prefix_done, 1)


def sort_by_src(nc, cst, raw, by_src, key_rows, by_src_edges):
    with ExitStack() as ctx:
        s = Scope(nc, ctx, "sort_")
        keys = s.sb("keys", [P, 2, GROUP, P], F32)
        one_low = s.sb("one_low", [P, 2, GROUP, P], BF16)
        one_high = s.sb("one_high", [P, 2, GROUP, NODE_COLS], BF16)
        low_t = s.sb("low_t", [P, GROUP, P], F32)
        place = s.sb("place", [P, 2, NODE_COLS], F32)
        same = s.sb("same", [P, 2, P], F32)
        picked = s.sb("picked", [P, 2, NODE_COLS], F32)
        base = s.sb("base", [P, 2, GROUP], F32)
        rank = s.sb("rank", [P, 2, GROUP], F32)
        target = s.sb("target", [P, 2, GROUP], I32)
        payload = s.sb("payload", [P, 2, GROUP, 2], I32)
        pad_place = s.sb("pad_place", [P, TILES], F32)
        place_i = s.sb("place_i", [P, TILES], I32)
        table = s.ps("table", [P, 512], F32)[:, 0:NODE_COLS]
        read = s.ps("read", [P, 2, 512], F32)
        turned = s.ps("turned", [P, 24, P], BF16)
        iota_done, keys_in = s.sem("iota_done"), [s.sem("keys_in0"), s.sem("keys_in1")]
        keys_free, hot_ready, hot_free = s.sem("keys_free"), s.sem("hot_ready"), s.sem("hot_free")
        turned_done, low_t_ready, table_ready = s.sem("turned"), s.sem("low_t_ready"), s.sem("table")
        read_done, read_free, counted = s.sem("read"), s.sem("read_free"), s.sem("counted")
        target_ready, link_sem = s.sem("target"), s.sem("link")
        scattered = [s.sem("scattered0"), s.sem("scattered1")]
        rounds = TILES // (2 * GROUP)
        block = ctx.enter_context(nc.Block())

        @block.sync
        def _(sp):
            flat = key_rows.rearrange("(a e) -> a e", a=1)
            with sp.Fori(0, rounds) as i:
                for b in range(2):
                    sp.wait_ge(keys_free, i * 2 + b + 1)
                    piece = flat[:, bass.ds((i * 2 + b) * (GROUP * P), GROUP * P)]
                    sp.dma_start(keys[:, b, :, :].rearrange("p g e -> p (g e)"),
                                 piece.to_broadcast([P, GROUP * P])).then_inc(keys_in[b], 16)

        @block.gpsimd
        def _(pool):
            pool.iota(place_i[:, :], pattern=[[P, TILES]], base=0, channel_multiplier=0).then_inc(iota_done, 1)
            with pool.Fori(0, rounds) as i:
                for b in range(2):
                    pool.wait_ge(target_ready, i * 2 + b + 1)
                    part_wait(pool)
                    for u in range(GROUP):
                        pool.indirect_dma_start(out=by_src_edges[:, :], out_offset=rows(target[:, b, u:u + 1]),
                                                in_=payload[:, b, u, :], in_offset=None).then_inc(scattered[b], 16)
            for b in range(2):
                pool.wait_ge(scattered[b], 16 * GROUP * rounds)

        @block.vector
        def _(dve):
            link = Link(dve, link_sem)
            dve.wait_ge(iota_done, 1)
            link(nc.vector.tensor_scalar(pad_place[:, :], raw.src_col[:, :], float(NO_NODE), None, ALU.is_equal))
            link(nc.vector.scalar_tensor_tensor(out=pad_place[:, :], in0=place_i[:, :], scalar=float(E),
                                                in1=pad_place[:, :], op0=ALU.max, op1=ALU.mult))
            dve.sem_inc(keys_free, 2)
            dve.sem_inc(hot_free, 2)
            dve.sem_inc(read_free, 2)
            row = cst.row_b[:, :].unsqueeze(1)
            link.start_loop()
            steps = 2
            with dve.Fori(0, rounds) as i:
                link.iteration(i, steps)
                for b in range(2):
                    at = bass.ds((i * 2 + b) * GROUP, GROUP)
                    dve.wait_ge(hot_free, i * 2 + b + 1)
                    nc.vector.tensor_tensor(one_low[:, b, :, :], row.to_broadcast([P, GROUP, P]),
                                            raw.low[0][:, at].unsqueeze(2).to_broadcast([P, GROUP, P]), ALU.is_equal)
                    nc.vector.tensor_tensor(one_high[:, b, :, :], row[:, :, 0:NODE_COLS].to_broadcast([P, GROUP, NODE_COLS]),
                                            raw.high[0][:, at].unsqueeze(2).to_broadcast([P, GROUP, NODE_COLS]),
                                            ALU.is_equal).then_inc(hot_ready, 1)
                    dve.wait_ge(hot_ready, i * 2 + b + 1)
                    dve.wait_ge(keys_in[b], 16 * (i + 1))
                    for u in range(GROUP):
                        t = (i * 2 + b) * GROUP + u
                        v = (b * GROUP + u) % 2
                        dve.wait_ge(read_free, t + 1)
                        compared = nc.vector.scalar_tensor_tensor(
                            out=same[:, v, :], in0=keys[:, b, u, :], scalar=raw.src_col[:, bass.ds(t, 1)],
                            in1=cst.after[:, :], op0=ALU.is_equal, op1=ALU.mult, accum_out=rank[:, b, u:u + 1])
                        if u == GROUP - 1:
                            compared.then_inc(keys_free, 1)
                        dve.wait_ge(read_done, t + 1)
                        nc.vector.scalar_tensor_tensor(
                            out=picked[:, v, :], in0=one_high[:, b, u, :], scalar=1.0,
                            in1=read[:, v, 0:NODE_COLS], op0=ALU.mult, op1=ALU.mult,
                            accum_out=base[:, b, u:u + 1]).then_inc(read_free, 1)
                    dve.wait_ge(read_free, 2 + (i * 2 + b + 1) * GROUP)
                    link(nc.vector.tensor_tensor(rank[:, b, :], rank[:, b, :], pad_place[:, at], ALU.add))
                    dve.wait_ge(scattered[b], i * (16 * GROUP))
                    part_wait(dve)
                    nc.vector.tensor_copy(payload[:, b, :, :], raw.payload[:, at, :])
                    nc.vector.tensor_tensor(target[:, b, :], rank[:, b, :], base[:, b, :], ALU.add).then_inc(target_ready, 1)
                    dve.wait_ge(target_ready, i * 2 + b + 1)
            link.end_loop(rounds, steps)

        @block.scalar
        def _(act):
            nc.scalar.copy(place[:, 0, :], by_src.start[:, :]).then_inc(table_ready, 1)
            with act.Fori(0, rounds) as i:
                for b in range(2):
                    act.wait_ge(turned_done, i * 2 + b + 1)
                    nc.scalar.copy(low_t[:, :, :], turned[:, 0:GROUP, :]).then_inc(low_t_ready, 1)
                    for u in range(GROUP):
                        v = b * GROUP + u
                        act.wait_ge(counted, i * (2 * GROUP) + v + 1)
                        nc.scalar.copy(place[:, (v + 1) % 2, :], table).then_inc(table_ready, 1)

        @block.tensor
        def _(pe):
            nc.tensor.matmul(table, cst.ident[:, :], by_src.start[:, :], start=True, stop=True)
            with pe.Fori(0, rounds) as i:
                for b in range(2):
                    pe.wait_ge(hot_ready, i * 2 + b + 1)
                    for u in range(GROUP):
                        last = nc.tensor.transpose(turned[:, u, :], one_low[:, b, u, :], cst.ident_b[:, :])
                    last.then_inc(turned_done, 1)
                    pe.wait_ge(low_t_ready, i * 2 + b + 1)
                    for u in range(GROUP):
                        v = b * GROUP + u
                        t = i * (2 * GROUP) + v
                        pe.wait_ge(table_ready, t + 1)
                        pe.wait_ge(read_free, t + 1)
                        nc.tensor.matmul(read[:, v % 2, 0:NODE_COLS], low_t[:, u, :], place[:, v % 2, :],
                                         start=True, stop=True).then_inc(read_done, 1)
                        last = nc.tensor.matmul(table, one_low[:, b, u, :], one_high[:, b, u, :], start=False, stop=True,
                                                skip_group_check=True)
                        last.then_inc(counted, 1)
                    pe.wait_ge(counted, (i * 2 + b + 1) * GROUP)
                    pe.sem_inc(hot_free, 1)


def edge_order(nc, cst, order, src, dst, by_src_edges):
    from_sort = order.name == "src"
    with ExitStack() as ctx:
        s = Scope(nc, ctx, order.name + "_ord_")
        pairs = s.sb("pairs", [P, EDGE_COLS, 2], I32) if from_sort else None
        key_i = s.sb("key_i", [P, EDGE_COLS], I32)
        other_i = s.sb("other_i", [P, EDGE_COLS], I32)
        key = s.sb("key", [P, EDGE_COLS], F32)
        work = s.sb("work", [P, EDGE_COLS], F32)
        digit_i = s.sb("digit_i", [P, EDGE_COLS], I32)
        high = s.sb("high", [P, EDGE_COLS], F32)
        first_of = s.sb("first_of", [P, P], F32)
        run = s.sb("run", [P, 1], F32)
        first_rows = s.ps("first_rows", [P, P], F32)
        padded, loaded, firsts_ready, firsts_turned, link_sem = (
            s.sem("padded"), s.sem("loaded"), s.sem("firsts"), s.sem("turned"), s.sem("link"))
        block = ctx.enter_context(nc.Block())

        @block.gpsimd
        def _(pool):
            if not from_sort:
                pool.memset(key_i[:, :], NO_NODE).then_inc(padded, 1)
                pool.memset(other_i[:, :], NO_NODE).then_inc(padded, 1)

        @block.sync
        def _(sp):
            if from_sort:
                sp.dma_start(pairs[:, :, :].rearrange("p t a -> p (t a)"),
                             by_src_edges.rearrange("(p t) a -> p (t a)", p=P)).then_inc(loaded, 16)
                return
            sp.wait_ge(padded, 2)
            cut = (P - 1) * EDGE_COLS
            for ends, at in ((dst, key_i), (src, other_i)):
                sp.dma_start(at[0:P - 1, :], ends[0:cut].rearrange("(p t) -> p t", p=P - 1)).then_inc(loaded, 16)
                sp.dma_start(at[P - 1:P, 0:LAST_EDGES],
                             ends[cut:E].rearrange("(a t) -> a t", a=1)).then_inc(loaded, 16)

        @block.vector
        def _(dve):
            link = Link(dve, link_sem)

            def table_rows(out, node_i, n):
                link(nc.vector.tensor_scalar(digit_i[:, 0:n], node_i, P - 1, None, ALU.bitwise_and))
                link(nc.vector.tensor_copy(work[:, 0:n], digit_i[:, 0:n]))
                link(nc.vector.tensor_scalar(digit_i[:, 0:n], node_i, DIGIT_BITS, None, ALU.logical_shift_right))
                link(nc.vector.tensor_copy(high[:, 0:n], digit_i[:, 0:n]))
                link(nc.vector.scalar_tensor_tensor(out=work[:, 0:n], in0=work[:, 0:n], scalar=float(NODE_COLS),
                                                    in1=high[:, 0:n], op0=ALU.mult, op1=ALU.add))
                link(nc.vector.tensor_scalar(out, work[:, 0:n], float(NODES - 1), None, ALU.min))

            dve.wait_ge(loaded, 16 if from_sort else 64)
            if from_sort:
                link(nc.vector.tensor_copy(key_i[:, :], pairs[:, :, 0]))
                link(nc.vector.tensor_copy(order.gather_rows[:, :], pairs[:, :, 1]))
            else:
                table_rows(order.gather_rows[:, :], other_i[:, :], EDGE_COLS)
            link(nc.vector.tensor_copy(key[:, :], key_i[:, :]))
            table_rows(order.first_row[:, :], key_i[:, 0:1], 1)
            link(nc.vector.memset(order.same[:, 0:1], 0.0))
            link(nc.vector.tensor_tensor(order.same[:, 1:EDGE_COLS], key[:, 1:EDGE_COLS], key[:, 0:EDGE_COLS - 1],
                                         ALU.is_equal))
            link(nc.vector.tensor_scalar(work[:, :], key[:, :], key[:, 0:1], None, ALU.is_equal))
            link(nc.vector.reduce_sum(run[:, :], work[:, :], AX.X))
            link(nc.vector.tensor_scalar(run[:, :], run[:, :], -1.0, None, ALU.add))
            link(nc.vector.tensor_tensor(order.first_end[:, :], run[:, :], cst.part_start[:, :], ALU.add))
            nc.vector.tensor_copy(first_of[:, :], key[:, 0:1].to_broadcast([P, P])).then_inc(firsts_ready, 1)
            dve.wait_ge(firsts_turned, 1)
            link(nc.vector.scalar_tensor_tensor(out=order.carry[:, :], in0=first_rows[:, :],
                                                scalar=key[:, EDGE_COLS - 1:EDGE_COLS], in1=cst.before[:, :],
                                                op0=ALU.is_equal, op1=ALU.mult))

        @block.tensor
        def _(pe):
            pe.wait_ge(firsts_ready, 1)
            nc.tensor.matmul(first_rows[:, :], first_of[:, :], cst.ident[:, :], start=True, stop=True).then_inc(firsts_turned, 1)


def prepare_weights(nc, cst, w, args):
    (W1, b1, W2, b2, W1_root, W1_rel, g_b1, W2_root, W2_rel, g_b2, W_src, b_src, W_dst, b_dst,
     s_W1, s_W2, s_W3, s_W4) = args
    with ExitStack() as ctx:
        s = Scope(nc, ctx, "w_")
        sides = [s.sb(f"side{n}", [D, 2 * D], F32) for n in range(4)]
        bias2 = s.sb("bias2", [P, 2, D], F32)
        w4 = s.sb("w4", [D, 1], F32)
        w4_wide = s.sb("w4_wide", [D, P], F32)
        w3_t = s.sb("w3_t", [P, D], F32)
        turned = s.ps("turned", [P, 4, P], F32)
        v_ps = s.ps("v_ps", [P, D], F32)
        loaded, turned_done, w3_ready, v_done, link_sem = (
            s.sem("loaded"), s.sem("turned"), s.sem("w3"), s.sem("v"), s.sem("link"))
        block = ctx.enter_context(nc.Block())
        pairs = ((W1_root, W1_rel), (W2_root, W2_rel), (s_W1, s_W2), (s_W3, s_W3))
        loads = []
        for side, two in zip(sides, pairs):
            loads += [(side[:, 0:D], two[0]), (side[:, D:2 * D], two[1])]
        loads += [(w.edge_in[:, 0:H], W1[0:D, :]), (w.edge_in[:, H:2 * H], W1[D:2 * D, :]), (w.edge_out[:, :], W2),
                  (w.directed[0:D, :], W_src), (w.directed[D:2 * D, :], W_dst), (w4[:, :], s_W4)]

        def wide(v, n):
            return v.rearrange("(a n) -> a n", a=1).to_broadcast([P, n])

        loads += [(w.edge_bias[:, :], wide(b1, H)), (w.edge_out_bias[:, :], wide(b2, D)),
                  (w.conv_bias[0][:, :], wide(g_b1, D)), (w.conv_bias[1][:, :], wide(g_b2, D)),
                  (bias2[:, 0, :], wide(b_src, D)), (bias2[:, 1, :], wide(b_dst, D))]

        @block.sync
        def _(sp):
            for to, of in loads:
                sp.dma_start(to, of).then_inc(loaded, 16)

        @block.tensor
        def _(pe):
            pe.wait_ge(loaded, 16 * len(loads))
            for n in range(4):
                last = nc.tensor.transpose(turned[:, n, 0:D], sides[n][:, :], cst.ident[0:D, 0:D])
            last.then_inc(turned_done, 1)
            pe.wait_ge(w3_ready, 1)
            nc.tensor.matmul(v_ps[:, :], w4_wide[:, :], w3_t[0:D, :], start=True, stop=True).then_inc(v_done, 1)

        @block.vector
        def _(dve):
            link = Link(dve, link_sem)
            dve.wait_ge(loaded, 16 * len(loads))
            link(nc.vector.tensor_scalar(w.directed[:, :], w.directed[:, :], 0.5, None, ALU.mult))
            link(nc.vector.tensor_scalar(bias2[:, :, :], bias2[:, :, :], 0.5, None, ALU.mult))
            link(nc.vector.tensor_tensor(w.directed_bias[:, :], bias2[:, 0, :], bias2[:, 1, :], ALU.add))
            link(nc.vector.tensor_scalar(w4[:, :], w4[:, :], 0.0, None, ALU.max))
            link(nc.vector.tensor_copy(w4_wide[:, :], w4[:, 0:1].to_broadcast([D, P])))
            dve.wait_ge(turned_done, 1)
            for n, to in enumerate((w.conv[0], w.conv[1], w.steps)):
                nc.vector.tensor_copy(to[:, :], turned[:, n, 0:D])
            nc.vector.tensor_copy(w3_t[:, :], turned[:, 3, 0:D]).then_inc(w3_ready, 1)
            dve.wait_ge(v_done, 1)
            link(nc.vector.tensor_copy(w.degree_row[:, :], v_ps[:, :]))


def normalise(nc, link, act_part, out, x, t):
    wide = [P, CHUNK, D]
    part_wait(link.eng)
    link(nc.vector.reduce_sum(t.mean[:, :], x, AX.X))
    link(nc.vector.tensor_scalar(t.mean[:, :], t.mean[:, :], 1.0 / D, None, ALU.mult))
    link(nc.vector.tensor_tensor(t.centred[:, :, :], x, t.mean[:, :].unsqueeze(2).to_broadcast(wide), ALU.subtract))
    link(nc.vector.tensor_tensor(t.squares[:, :, :], t.centred[:, :, :], t.centred[:, :, :], ALU.mult))
    part_wait(link.eng)
    act_part(nc.vector.reduce_sum(t.var[:, :], t.squares[:, :, :], AX.X))
    link(nc.vector.reciprocal(t.std[:, :], t.std[:, :]))
    link(nc.vector.scalar_tensor_tensor(out=out, in0=t.centred[:, :, :], scalar=0.0,
                                        in1=t.std[:, :].unsqueeze(2).to_broadcast(wide), op0=ALU.max, op1=ALU.mult))


class Temps:
    def __init__(self, s):
        self.mean, self.var, self.std = s.sb("mean", [P, CHUNK], F32), s.sb("var", [P, CHUNK], F32), s.sb("std", [P, CHUNK], F32)
        self.centred, self.squares = s.sb("centred", [P, CHUNK, D], F32), s.sb("squares", [P, CHUNK, D], F32)


def first_layer_tables(nc, cst, w, orders, nodes_of, x, x_sb, source_table, target_table, fills):
    with ExitStack() as ctx:
        s = Scope(nc, ctx, "tab_")
        t = Temps(s)
        h = s.sb("h", [P, 2, CHUNK, D], F32)
        h_t = s.sb("h_t", [D, CHUNK, P], F32)
        ends = s.sb("ends", [P, 2, CHUNK, 2 * H], F32)
        starts = s.sb("starts", [P, 2, 2, CHUNK], I32)
        firsts = s.sb("firsts", [P, 2, H], F32)
        first_rows = s.sb("first_rows", [P, 2], I32)
        turned = s.ps("turned", [D, 8, P], F32)
        products = s.ps("products", [P, 8, 2 * H], F32)
        padded, loaded, link_sem = s.sem("padded"), s.sem("loaded"), s.sem("link")
        var_ready, std_ready, h_ready, turned_done = s.sem("var"), s.sem("std"), s.sem("h"), s.sem("turned")
        h_t_ready, products_done, ends_ready = s.sem("h_t"), s.sem("products"), s.sem("ends")
        stored, scattered, first_in, first_out = s.sem("stored"), s.sem("scattered"), s.sem("first_in"), s.sem("first_out")
        block = ctx.enter_context(nc.Block())
        last_col = NODE_COLS - 1

        @block.gpsimd
        def _(pool):
            pool.memset(x_sb[:, last_col, :], 0.0).then_inc(padded, 1)
            with pool.Fori(0, CHUNK_PAIRS) as j:
                for b in range(2):
                    pool.wait_ge(ends_ready, j * 2 + b + 1)
                    part_wait(pool)
                    for c in range(CHUNK):
                        for k in range(2):
                            pool.indirect_dma_start(out=fills[k][:, :], out_offset=rows(starts[:, b, k, c:c + 1]),
                                                    in_=ends[:, b, c, 0:H], in_offset=None, bounds_check=EDGES - 1,
                                                    oob_is_err=False).then_inc(scattered, 16)
            pool.wait_ge(scattered, 16 * NODE_COLS * 2)
            pool.wait_ge(stored, 16 * NODE_COLS // CHUNK * 2)
            for k in range(2):
                pool.indirect_dma_start(out=firsts[:, k, :], out_offset=None, in_=target_table[:, :],
                                        in_offset=rows(orders[k].first_row[:, 0:1])).then_inc(first_in, 16)
            pool.wait_ge(first_in, 32)
            for k in range(2):
                pool.dma_start(fills[k][0:EDGES, :].rearrange("(p t) f -> p t f", p=P)[:, 0, :],
                               firsts[:, k, :]).then_inc(first_out, 16)
            pool.wait_ge(first_out, 32)

        @block.sync
        def _(sp):
            sp.wait_ge(padded, 1)
            sp.dma_start(x_sb[:, 0:last_col, :], x[0:last_col * P, :].rearrange("(c p) f -> p c f", p=P)).then_inc(loaded, 16)
            sp.dma_start(x_sb[0:LAST_NODES, last_col, :], x[last_col * P:N, :]).then_inc(loaded, 16)
            with sp.Fori(0, CHUNK_PAIRS) as j:
                for b in range(2):
                    sp.wait_ge(ends_ready, j * 2 + b + 1)
                    for table, half in ((target_table, 0), (source_table, 1)):
                        sp.dma_start(table.rearrange("(p c) f -> p c f", p=P)[:, bass.ds((j * 2 + b) * CHUNK, CHUNK), :],
                                     ends[:, b, :, half * H:half * H + H]).then_inc(stored, 16)
            sp.wait_ge(stored, 16 * NODE_COLS // CHUNK * 2)

        @block.scalar
        def _(act):
            with act.Fori(0, CHUNK_PAIRS) as j:
                for b in range(2):
                    act.wait_ge(var_ready, j * 2 + b + 1)
                    nc.scalar.activation(t.std[:, :], t.var[:, :], ACT.Sqrt, bias=cst.eps[:, 0:1], scale=1.0 / D).then_inc(std_ready, 1)
                    act.wait_ge(turned_done, j * 2 + b + 1)
                    nc.scalar.copy(h_t[:, :, :], turned[:, 0:CHUNK, :]).then_inc(h_t_ready, 1)

        @block.tensor
        def _(pe):
            with pe.Fori(0, CHUNK_PAIRS) as j:
                for b in range(2):
                    pe.wait_ge(h_ready, j * 2 + b + 1)
                    part_wait(pe)
                    for c in range(CHUNK):
                        last = nc.tensor.transpose(turned[:, c, :], h[:, b, c, :], cst.ident[:, :])
                    last.then_inc(turned_done, 1)
                    pe.wait_ge(h_t_ready, j * 2 + b + 1)
                    pe.wait_ge(ends_ready, j * 2 + b)
                    for c in range(CHUNK):
                        last = nc.tensor.matmul(products[:, c, :], h_t[:, c, :], w.edge_in[:, :], start=True, stop=True)
                    last.then_inc(products_done, 1)

        @block.vector
        def _(dve):
            link = Link(dve, link_sem)
            dve.wait_ge(loaded, 32)
            link.start_loop()
            steps = 2 * 6
            with dve.Fori(0, CHUNK_PAIRS) as j:
                link.iteration(j, steps)
                for b in range(2):
                    chunk = j * 2 + b
                    at = bass.ds(chunk * CHUNK, CHUNK)

                    def act_part(ins):
                        ins.then_inc(var_ready, 1)
                        dve.wait_ge(std_ready, chunk + 1)

                    normalise(nc, link, act_part, h[:, b, :, :], x_sb[:, at, :], t)
                    nc.vector.tensor_tensor(x_sb[:, at, :], x_sb[:, at, :], h[:, b, :, :], ALU.add).then_inc(h_ready, 1)
                    dve.wait_ge(products_done, chunk + 1)
                    dve.wait_ge(stored, j * (16 * 2 * 2))
                    dve.wait_ge(scattered, j * (16 * 2 * 2 * CHUNK))
                    part_wait(dve)
                    nc.vector.tensor_copy(ends[:, b, :, 0:H], products[:, 0:CHUNK, 0:H])
                    nc.vector.tensor_copy(starts[:, b, 0, :], nodes_of[0].start_row[:, at])
                    nc.vector.tensor_copy(starts[:, b, 1, :], nodes_of[1].start_row[:, at])
                    nc.vector.tensor_tensor(ends[:, b, :, H:2 * H], products[:, 0:CHUNK, H:2 * H],
                                            w.edge_bias[:, :].unsqueeze(1).to_broadcast([P, CHUNK, H]),
                                            ALU.add).then_inc(ends_ready, 1)
            link.end_loop(CHUNK_PAIRS, steps)


def sum_over_edges(nc, cst, name, order, table, state, width, fill):
    with ExitStack() as ctx:
        s = Scope(nc, ctx, name)
        got = s.sb("got", [P, BUFS, GROUP, width], F32)
        idx = s.sb("idx", [P, BUFS, GROUP], I32)
        ends = s.sb("ends", [P, 2, GROUP, width], F32) if fill is not None else None
        carry_sb = s.sb("carry_sb", [P, width], F32)
        carry_ps = s.ps("carry_ps", [P, width], F32)
        idx_ready, idx_free = s.sem("idx_ready"), s.sem("idx_free")
        gathered = [s.sem(f"gathered{b}") for b in range(BUFS)]
        stored = [s.sem(f"stored{b}") for b in range(BUFS)]
        scanned, ends_in, ends_step, rows_ready = s.sem("scanned"), [s.sem("ends_in0"), s.sem("ends_in1")], s.sem("ends_step"), s.sem("rows_ready")
        added, carried, carry_ready, carry_added, cleared = s.sem("added"), s.sem("carried"), s.sem("carry_ready"), s.sem("carry_added"), s.sem("cleared")
        block = ctx.enter_context(nc.Block())
        per_round = BUFS * GROUP
        state_v = state[0:EDGES, :].rearrange("(p t) f -> p (t f)", p=P)

        @block.sync
        def _(sp):
            with sp.Fori(0, ROUNDS) as i:
                for b in range(BUFS):
                    group = i * BUFS + b
                    if fill is not None:
                        fill_v = fill[0:EDGES, :].rearrange("(p t) f -> p (t f)", p=P)
                        sp.wait_ge(ends_step, group * GROUP)
                        sp.dma_start(ends[:, b % 2, :, :].rearrange("p u f -> p (u f)"),
                                     fill_v[:, bass.ds(group * (GROUP * width), GROUP * width)]).then_inc(ends_in[b % 2], 16)
                    sp.wait_ge(scanned, (group + 1) * GROUP)
                    sp.dma_start(state_v[:, bass.ds(group * (GROUP * width), GROUP * width)],
                                 got[:, b, :, :].rearrange("p u f -> p (u f)")).then_inc(stored[b], 16)
            for b in range(BUFS):
                sp.wait_ge(stored[b], 16 * ROUNDS)

        @block.gpsimd
        def _(pool):
            with pool.Fori(0, ROUNDS) as i:
                for b in range(BUFS):
                    pool.wait_ge(idx_ready, i * BUFS + b + 1)
                    pool.wait_ge(stored[b], i * 16)
                    part_wait(pool)
                    for u in range(GROUP):
                        pool.indirect_dma_start(out=got[:, b, u, :], out_offset=None, in_=table[:, :],
                                                in_offset=rows(idx[:, b, u:u + 1])).then_inc(gathered[b], 16)
            pool.wait_ge(carry_ready, 1)
            for b in range(BUFS):
                pool.wait_ge(stored[b], 16 * ROUNDS)
            pool.indirect_dma_start(out=state[:, :], out_offset=rows(order.first_end[:, 0:1]), in_=carry_sb[:, :],
                                    in_offset=None, compute_op=ALU.add).then_inc(carry_added, 16)
            pool.wait_ge(carry_added, 16)

        @block.scalar
        def _(act):
            with act.Fori(0, ROUNDS) as i:
                for b in range(BUFS):
                    group = i * BUFS + b
                    act.wait_ge(idx_free, group + 1)
                    nc.scalar.copy(idx[:, b, :], order.gather_rows[:, bass.ds(group * GROUP, GROUP)]).then_inc(idx_ready, 1)
                    if fill is not None:
                        act.wait_ge(added, group + 1)
                        nc.scalar.activation(got[:, b, :, :], got[:, b, :, :], ACT.Relu).then_inc(rows_ready, 1)

        @block.vector
        def _(dve):
            dve.sem_inc(idx_free, BUFS - 1)
            nc.vector.memset(got[:, BUFS - 1, GROUP - 1, :], 0.0).then_inc(cleared, 1)
            dve.wait_ge(cleared, 1)
            if fill is not None:
                nc.vector.memset(ends[:, 1, GROUP - 1, :], 0.0).then_inc(cleared, 1)
                dve.wait_ge(cleared, 2)
            with dve.Fori(0, ROUNDS) as i:
                for b in range(BUFS):
                    group = i * BUFS + b
                    first = group * GROUP
                    if fill is not None:
                        dve.wait_ge(ends_in[b % 2], (i * 2 + b // 2 + 1) * 16)
                        for u in range(GROUP):
                            before = ends[:, b % 2, u - 1, :] if u else ends[:, 1 - b % 2, GROUP - 1, :]
                            nc.vector.scalar_tensor_tensor(
                                out=ends[:, b % 2, u, :], in0=before, scalar=order.same[:, bass.ds(first + u, 1)],
                                in1=ends[:, b % 2, u, :], op0=ALU.mult, op1=ALU.add).then_inc(ends_step, 1)
                            dve.wait_ge(ends_step, first + u + 1)
                        dve.wait_ge(gathered[b], (i + 1) * (16 * GROUP))
                        nc.vector.tensor_tensor(got[:, b, :, :], got[:, b, :, :], ends[:, b % 2, :, :], ALU.add).then_inc(added, 1)
                        dve.wait_ge(rows_ready, group + 1)
                    else:
                        dve.wait_ge(gathered[b], (i + 1) * (16 * GROUP))
                    for u in range(GROUP):
                        before = got[:, b, u - 1, :] if u else got[:, (b - 1) % BUFS, GROUP - 1, :]
                        nc.vector.scalar_tensor_tensor(
                            out=got[:, b, u, :], in0=before, scalar=order.same[:, bass.ds(first + u, 1)],
                            in1=got[:, b, u, :], op0=ALU.mult, op1=ALU.add).then_inc(scanned, 1)
                        if u == 0:
                            dve.wait_ge(scanned, first + 1)
                            dve.sem_inc(idx_free, 1)
                        dve.wait_ge(scanned, first + u + 1)
            dve.wait_ge(carried, 1)
            nc.vector.tensor_copy(carry_sb[:, :], carry_ps[:, :]).then_inc(carry_ready, 1)

        @block.tensor
        def _(pe):
            pe.wait_ge(scanned, EDGE_COLS)
            nc.tensor.matmul(carry_ps[:, :], order.carry[:, :], got[:, BUFS - 1, GROUP - 1, :],
                             start=True, stop=True).then_inc(carried, 1)


def update_nodes(nc, cst, name, kind, sums, weights, nodes_of, w, x_sb, h_sb, tables, out=None):
    width = 2 * D if kind == "edge" else D
    with ExitStack() as ctx:
        s = Scope(nc, ctx, name)
        t = Temps(s)
        idx = s.sb("idx", [P, 2, 2, CHUNK], I32)
        sum_sb = s.sb("sum_sb", [P, 2, 2, CHUNK, width], F32)
        pair = s.sb("pair", [P, CHUNK, 2 * D], F32)
        pair_t = s.sb("pair_t", [P, CHUNK, P], F32)
        y = s.sb("y", [P, CHUNK, D], F32)
        degree = s.sb("degree", [P, NODE_COLS], F32)
        to_table = s.sb("to_table", [P, 2, 2, CHUNK, D], F32)
        turned = s.ps("turned", [P, 8, P], F32)
        product = s.ps("product", [P, 8, D], F32)
        idx_ready, summed = s.sem("idx_ready"), [s.sem("summed0"), s.sem("summed1")]
        pair_ready, turned_done, pair_t_ready = s.sem("pair"), s.sem("turned"), s.sem("pair_t")
        product_done, product_taken = s.sem("product"), s.sem("taken")
        var_ready, std_ready, table_ready, stored = s.sem("var"), s.sem("std"), s.sem("table"), s.sem("stored")
        link_sem = s.sem("link")
        block = ctx.enter_context(nc.Block())
        rounds = CHUNK_PAIRS
        wide = [P, CHUNK, D]
        normal = kind in ("edge", "conv2", "directed")
        of_sums = len(sums)

        if sums:
            @block.gpsimd
            def _(pool):
                with pool.Fori(0, rounds) as j:
                    for b in range(2):
                        pool.wait_ge(idx_ready, j * 2 + b + 1)
                        part_wait(pool)
                        for c in range(CHUNK):
                            for k, (order, state) in enumerate(sums):
                                pool.indirect_dma_start(out=sum_sb[:, b, k, c, :], out_offset=None, in_=state[:, :],
                                                        in_offset=rows(idx[:, b, k, c:c + 1])).then_inc(summed[b], 16)

        @block.sync
        def _(sp):
            if tables:
                with sp.Fori(0, rounds) as j:
                    for b in range(2):
                        sp.wait_ge(table_ready, j * 2 + b + 1)
                        for k, table in enumerate(tables):
                            sp.dma_start(table.rearrange("(p c) f -> p c f", p=P)[:, bass.ds((j * 2 + b) * CHUNK, CHUNK), :],
                                         to_table[:, b, k, :, :]).then_inc(stored, 16)
                sp.wait_ge(stored, 16 * len(tables) * 2 * rounds)
            if out is not None:
                sp.wait_ge(table_ready, 2 * rounds)
                last_col = NODE_COLS - 1
                sp.dma_start(out[0:last_col * P, :].rearrange("(c p) f -> p c f", p=P), x_sb[:, 0:last_col, :]).then_inc(stored, 16)
                sp.dma_start(out[last_col * P:N, :], x_sb[0:LAST_NODES, last_col, :]).then_inc(stored, 16)
                sp.wait_ge(stored, 32)

        @block.scalar
        def _(act):
            if kind == "first":
                nc.scalar.activation(pair[:, :, D:2 * D], x_sb[:, 0:CHUNK, :], ACT.Copy, scale=0.0)
            with act.Fori(0, rounds) as j:
                for b in range(2):
                    chunk = j * 2 + b
                    at = bass.ds(chunk * CHUNK, CHUNK)
                    if sums:
                        act.wait_ge(summed[b], (j + 1) * (16 * CHUNK * of_sums))
                    act.wait_ge(turned_done, chunk)
                    if kind == "directed":
                        for c in range(CHUNK):
                            for k, (order, state) in enumerate(sums):
                                last = nc.scalar.activation(pair[:, c, k * D:k * D + D], sum_sb[:, b, k, c, :], ACT.Copy,
                                                            scale=nodes_of[k].inv_root[:, bass.ds(chunk * CHUNK + c, 1)])
                        last.then_inc(pair_ready, 1)
                    elif kind == "first":
                        nc.scalar.copy(pair[:, :, 0:D], h_sb[:, at, :]).then_inc(pair_ready, 1)
                    elif kind != "edge":
                        nc.scalar.copy(pair[:, :, 0:D], h_sb[:, at, :])
                        nc.scalar.copy(pair[:, :, D:2 * D], sum_sb[:, b, 0, :, :]).then_inc(pair_ready, 1)
                    act.wait_ge(turned_done, chunk + 1)
                    nc.scalar.copy(pair_t[:, :, :], turned[:, 0:CHUNK, :]).then_inc(pair_t_ready, 1)
                    if normal:
                        act.wait_ge(var_ready, chunk + 1)
                        nc.scalar.activation(t.std[:, :], t.var[:, :], ACT.Sqrt, bias=cst.eps[:, 0:1], scale=1.0 / D).then_inc(std_ready, 1)

        @block.tensor
        def _(pe):
            with pe.Fori(0, rounds) as j:
                for b in range(2):
                    chunk = j * 2 + b
                    pe.wait_ge(pair_ready, chunk + 1)
                    pe.wait_ge(pair_t_ready, chunk)
                    for c in range(CHUNK):
                        last = nc.tensor.transpose(turned[:, c, :], pair[:, c, :], cst.ident[:, :])
                    last.then_inc(turned_done, 1)
                    pe.wait_ge(pair_t_ready, chunk + 1)
                    pe.wait_ge(product_taken, chunk)
                    for c in range(CHUNK):
                        last = nc.tensor.matmul(product[:, c, :], pair_t[:, c, :], weights[:, :], start=True, stop=True)
                    last.then_inc(product_done, 1)

        @block.vector
        def _(dve):
            link = Link(dve, link_sem)

            def stage_rows(b, at):
                part_wait(dve)
                for k, (order, state) in enumerate(sums):
                    last = nc.vector.tensor_copy(idx[:, b, k, :], nodes_of[order].end_row[:, at])
                last.then_inc(idx_ready, 1)

            if kind == "edge":
                link(nc.vector.tensor_tensor(degree[:, :], nodes_of[0].count[:, :], nodes_of[1].count[:, :], ALU.add))
            if sums:
                for b in range(2):
                    stage_rows(b, slice(b * CHUNK, (b + 1) * CHUNK))

            def chunk_steps(j, b, more):
                chunk = j * 2 + b
                at = bass.ds(chunk * CHUNK, CHUNK)
                if kind == "edge":
                    dve.wait_ge(summed[b], (j + 1) * (16 * CHUNK * 2))
                    dve.wait_ge(turned_done, chunk)
                    nc.vector.tensor_tensor(pair[:, :, :], sum_sb[:, b, 0, :, :], sum_sb[:, b, 1, :, :], ALU.add).then_inc(pair_ready, 1)
                dve.wait_ge(pair_ready, chunk + 1)
                if sums and more:
                    stage_rows(b, bass.ds((chunk + 2) * CHUNK, CHUNK))
                by_degree = {"edge": (degree, w.edge_out_bias), "first": (nodes_of[0].count, w.degree_row),
                             "step": (nodes_of[0].count, w.degree_row), "last": (nodes_of[0].count, w.degree_row)}
                if kind in by_degree:
                    count, row = by_degree[kind]
                    link(nc.vector.tensor_tensor(y[:, :, :], row[:, :].unsqueeze(1).to_broadcast(wide),
                                                 count[:, at].unsqueeze(2).to_broadcast(wide), ALU.mult))
                    bias = y[:, :, :]
                else:
                    row = {"conv1": w.conv_bias[0], "conv2": w.conv_bias[1], "directed": w.directed_bias}[kind]
                    bias = row[:, :].unsqueeze(1).to_broadcast(wide)
                dve.wait_ge(product_done, chunk + 1)
                nc.vector.tensor_tensor(y[:, :, :], product[:, 0:CHUNK, :], bias, ALU.add).then_inc(product_taken, 1)
                dve.wait_ge(product_taken, chunk + 1)
                if tables:
                    dve.wait_ge(stored, j * (16 * 2 * len(tables)))
                if kind in ("conv1", "first", "step"):
                    ins = nc.vector.tensor_scalar(to_table[:, b, 0, :, :], y[:, :, :], 0.0, None, ALU.max)
                    ins.then_inc(table_ready, 1)
                    dve.wait_ge(table_ready, chunk + 1)
                    if kind == "conv1":
                        part_wait(dve)
                        link(nc.vector.tensor_copy(h_sb[:, at, :], to_table[:, b, 0, :, :]))
                    return
                if kind in ("conv2", "last"):
                    link(nc.vector.tensor_scalar(y[:, :, :], y[:, :, :], 0.0, None, ALU.max))
                ins = nc.vector.tensor_tensor(x_sb[:, at, :], x_sb[:, at, :], y[:, :, :], ALU.add)
                if kind == "last":
                    ins.then_inc(table_ready, 1)
                    dve.wait_ge(table_ready, chunk + 1)
                    return
                link(ins)

                def act_part(ins):
                    ins.then_inc(var_ready, 1)
                    dve.wait_ge(std_ready, chunk + 1)

                normalise(nc, link, act_part, h_sb[:, at, :], x_sb[:, at, :], t)
                if kind == "edge":
                    part_wait(dve)
                    nc.vector.tensor_copy(to_table[:, b, 0, :, :], h_sb[:, at, :]).then_inc(table_ready, 1)
                elif kind == "conv2":
                    for k in range(2):
                        last = nc.vector.tensor_tensor(to_table[:, b, k, :, :], h_sb[:, at, :],
                                                       nodes_of[k].inv_root[:, at].unsqueeze(2).to_broadcast(wide), ALU.mult)
                    last.then_inc(table_ready, 1)

            steps = {"edge": 2 * 8, "conv1": 2, "conv2": 2 * 8, "directed": 2 * 7, "first": 2, "step": 2, "last": 4}[kind]
            link.start_loop()
            with dve.Fori(0, rounds - 1) as j:
                link.iteration(j, steps)
                for b in range(2):
                    chunk_steps(j, b, True)
            link.end_loop(rounds - 1, steps)
            for b in range(2):
                chunk_steps(rounds - 1, b, False)


def graph_layers(nc, x, src, dst, *weights_and_out):
    weights, out = weights_and_out[:-1], weights_and_out[-1]

    def dram(name, shape, dtype=F32):
        return nc.dram_tensor(name, shape, dtype, kind="Internal").ap()

    key_rows = dram("key_rows", [EDGES])
    by_src_edges = dram("by_src_edges", [EDGES, 2], I32)
    source_table, target_table = dram("source_table", [NODES, H]), dram("target_table", [NODES, H])
    tables = [dram("table0", [NODES, D]), dram("table1", [NODES, D])]
    wide_states = [dram(f"wide_state{k}", [EDGES + P, H]) for k in range(2)]
    states = [dram(f"state{k}", [EDGES + P, D]) for k in range(2)]
    fills = [dram(f"fill{k}", [EDGES, H]) for k in range(2)]

    with ExitStack() as ctx:
        s = Scope(nc, ctx, "")
        cst = Constants(s)
        nodes_of = [Nodes(s, side) for side in ("src", "dst")]
        constants(nc, cst)
        with ExitStack() as raw_ctx:
            r = Scope(nc, raw_ctx, "raw_")
            raw = EdgeColumns(r)
            load_edges(nc, cst, raw, src, dst, key_rows)
            count_edges(nc, cst, raw, nodes_of,
                        (fills, [(wide_states[0], H), (wide_states[1], H), (states[0], D), (states[1], D)]))
            sort_by_src(nc, cst, raw, nodes_of[0], key_rows, by_src_edges)
        orders = [Order(s, side) for side in ("src", "dst")]
        for order in orders:
            edge_order(nc, cst, order, src, dst, by_src_edges)
        w = Weights(s)
        prepare_weights(nc, cst, w, weights)
        x_sb = s.sb("x_sb", [P, NODE_COLS, D], F32)
        h_sb = s.sb("h_sb", [P, NODE_COLS, D], F32)

        first_layer_tables(nc, cst, w, orders, nodes_of, x, x_sb, source_table, target_table, fills)
        sum_over_edges(nc, cst, "e1_", orders[1], source_table, wide_states[1], H, fills[1])
        sum_over_edges(nc, cst, "e0_", orders[0], source_table, wide_states[0], H, fills[0])
        update_nodes(nc, cst, "ne_", "edge", [(0, wide_states[0]), (1, wide_states[1])], w.edge_out, nodes_of, w,
                     x_sb, h_sb, tables[:1])
        sum_over_edges(nc, cst, "c1_", orders[1], tables[0], states[1], D, None)
        update_nodes(nc, cst, "n1_", "conv1", [(1, states[1])], w.conv[0], nodes_of, w, x_sb, h_sb, tables[:1])
        sum_over_edges(nc, cst, "c2_", orders[1], tables[0], states[1], D, None)
        update_nodes(nc, cst, "n2_", "conv2", [(1, states[1])], w.conv[1], nodes_of, w, x_sb, h_sb, tables)
        sum_over_edges(nc, cst, "d0_", orders[0], tables[1], states[0], D, None)
        sum_over_edges(nc, cst, "d1_", orders[1], tables[0], states[1], D, None)
        update_nodes(nc, cst, "nd_", "directed", [(0, states[0]), (1, states[1])], w.directed, nodes_of, w,
                     x_sb, h_sb, [])
        update_nodes(nc, cst, "s0_", "first", [], w.steps, nodes_of, w, x_sb, h_sb, tables[:1])
        for step in range(1, 4):
            sum_over_edges(nc, cst, f"p{step}_", orders[0], tables[0], states[0], D, None)
            update_nodes(nc, cst, f"s{step}_", "last" if step == 3 else "step", [(0, states[0])], w.steps, nodes_of, w,
                         x_sb, h_sb, [] if step == 3 else tables[:1], out if step == 3 else None)


_INS = ['x', 'src', 'dst', 'L0_gnn_W1', 'L0_gnn_b1', 'L0_gnn_W2', 'L0_gnn_b2', 'L1_gnn_W1_root', 'L1_gnn_W1_rel',
        'L1_gnn_b1', 'L1_gnn_W2_root', 'L1_gnn_W2_rel', 'L1_gnn_b2', 'L2_gnn_W_src', 'L2_gnn_b_src', 'L2_gnn_W_dst',
        'L2_gnn_b_dst', 'L3_gnn_W1', 'L3_gnn_W2', 'L3_gnn_W3', 'L3_gnn_W4']


def kernel(**inputs):
    import numpy as _np
    import concourse.bacc as _bacc
    from concourse import mybir as _mybir
    from concourse.bass_utils import run_bass_kernel_spmd as _run

    nc = _bacc.Bacc("TRN2", target_bir_lowering=False, num_devices=1)
    arrays, args = {}, []
    for name in _INS:
        a = _np.ascontiguousarray(inputs[name])
        arrays[f"in_{name}_dram"] = a
        args.append(nc.dram_tensor(f"in_{name}_dram", a.shape, _mybir.dt.from_np(a.dtype), kind="ExternalInput").ap())
    out = nc.dram_tensor("out_0_dram", (N, D), F32, kind="ExternalOutput").ap()
    graph_layers(nc, *args, out)
    r = _run(nc, [arrays], core_ids=[0])
    return r.results[0]["out_0_dram"]
```

```python
import concourse.bass as bass
from concourse import mybir
from contextlib import ExitStack

F32 = mybir.dt.float32
BF16 = mybir.dt.bfloat16
I32 = mybir.dt.int32
ALU = mybir.AluOpType
ACT = mybir.ActivationFunctionType
AX = mybir.AxisListType

P = 128
N = 12500
D = 64
H = 128
E = 200000
GROUP = 17
BUFS = 4
AHEAD = BUFS - 1
EDGE_COLS = 1564
ROUNDS = EDGE_COLS // (BUFS * GROUP)
EDGES = P * EDGE_COLS
LAST_EDGES = E - (P - 1) * EDGE_COLS
NODE_COLS = (N + P - 1) // P
NODES = P * NODE_COLS
LAST_NODES = N - (NODE_COLS - 1) * P
NO_NODE = P * P - 1
CHUNK = 7
CHUNK_PAIRS = NODE_COLS // (2 * CHUNK)
DIGIT_BITS = 7
TILES = EDGES // P
BLOCKS = (TILES + P - 1) // P
LAST_TILES = TILES - (BLOCKS - 1) * P
HOT_AFTER = (1, 4, 7, 10)
TURN_AT = 13
EPS = 1e-5

assert EDGE_COLS == BUFS * GROUP * ROUNDS and EDGES >= E and 0 < LAST_EDGES <= EDGE_COLS
assert NODE_COLS == 2 * CHUNK * CHUNK_PAIRS


class Link:

    def __init__(self, eng, sem):
        self.eng, self.sem, self.before, self.n = eng, sem, 0, 0

    def __call__(self, ins):
        self.n += 1
        ins.then_inc(self.sem, 1)
        self.eng.wait_ge(self.sem, self.before + self.n)

    def start_loop(self):
        self.done, self.n = self.before + self.n, 0

    def iteration(self, i, steps):
        self.before, self.n = self.done + i * steps, 0

    def end_loop(self, rounds, steps):
        assert self.n == steps, (self.n, steps)
        self.before, self.n = self.done + rounds * steps, 0


class Scope:

    def __init__(self, nc, ctx, prefix):
        self.nc, self.ctx, self.prefix, self.sems = nc, ctx, prefix, []

    def sb(self, name, shape, dtype):
        return self.ctx.enter_context(self.nc.sbuf_tensor(self.prefix + name, shape, dtype))

    def ps(self, name, shape, dtype):
        return self.ctx.enter_context(self.nc.psum_tensor(self.prefix + name, shape, dtype))

    def sem(self, name):
        if not self.sems:
            self.ctx.callback(self.clear)
        self.sems.append(self.nc.alloc_semaphore(self.prefix + name))
        return self.sems[-1]

    def clear(self):
        self.nc.clear_and_free_semaphores(self.sems)
        self.nc.all_engine_barrier()


def part_wait(eng):
    eng.nop(nofuse=True)


def wait_if(eng, sem, value):
    if not (isinstance(value, int) and value <= 0):
        eng.wait_ge(sem, value)


def run_rounds(eng, rounds, body):
    body(0)
    with eng.Fori(1, rounds - 1) as i:
        body(i)
    body(rounds - 1)


def rows(ap):
    return bass.IndirectOffsetOnAxis(ap=ap, axis=0)


class Constants:
    def __init__(self, s):
        self.row = s.sb("row", [P, P], F32)
        self.row_b = s.sb("row_b", [P, P], BF16)
        self.part = s.sb("part", [P, 1], F32)
        self.part_start = s.sb("part_start", [P, 1], F32)
        self.ident = s.sb("ident", [P, P], F32)
        self.ident_b = s.sb("ident_b", [P, P], BF16)
        self.up_to = s.sb("up_to", [P, P], F32)
        self.before = s.sb("before", [P, P], F32)
        self.after = s.sb("after", [P, P], F32)
        self.ones = s.sb("ones", [P, P], F32)
        self.eps = s.sb("eps", [P, 1], F32)


class Nodes:

    def __init__(self, s, side):
        self.count = s.sb(f"count_{side}", [P, NODE_COLS], F32)
        self.start = s.sb(f"start_{side}", [P, NODE_COLS], F32)
        self.inv_root = s.sb(f"inv_root_{side}", [P, NODE_COLS], F32)
        self.start_row = s.sb(f"start_row_{side}", [P, NODE_COLS], I32)
        self.end_row = s.sb(f"end_row_{side}", [P, NODE_COLS], I32)


class EdgeColumns:

    def __init__(self, s):
        self.src_col = s.sb("src_col", [P, TILES], F32)
        self.payload = s.sb("payload", [P, TILES, 2], I32)
        self.low = [s.sb(f"low{k}", [P, TILES], BF16) for k in range(2)]
        self.high = [s.sb(f"high{k}", [P, TILES], BF16) for k in range(2)]


class Order:

    def __init__(self, s, side):
        self.name = side
        self.gather_rows = s.sb(f"gather_rows_{side}", [P, EDGE_COLS], I32)
        self.same = s.sb(f"same_{side}", [P, EDGE_COLS], F32)
        self.first_row = s.sb(f"first_row_{side}", [P, 1], I32)
        self.first_end = s.sb(f"first_end_{side}", [P, 1], I32)
        self.carry = s.sb(f"carry_{side}", [P, P], F32)


class Weights:
    def __init__(self, s):
        self.edge_in = s.sb("edge_in", [D, 2 * H], F32)
        self.edge_out = s.sb("edge_out", [H, D], F32)
        self.directed = s.sb("directed", [2 * D, D], F32)
        self.edge_bias = s.sb("edge_bias", [P, H], F32)
        self.edge_out_bias = s.sb("edge_out_bias", [P, D], F32)
        self.conv_bias = [s.sb(f"conv_bias{k}", [P, D], F32) for k in range(2)]
        self.directed_bias = s.sb("directed_bias", [P, D], F32)
        self.conv = [s.sb(f"conv{k}", [2 * D, D], F32) for k in range(2)]
        self.steps = s.sb("steps", [2 * D, D], F32)
        self.degree_row = s.sb("degree_row", [P, D], F32)


def constants(nc, cst):
    with ExitStack() as ctx:
        s = Scope(nc, ctx, "cst_")
        row_i = s.sb("row_i", [P, P], I32)
        part_i = s.sb("part_i", [P, 1], I32)
        pos_i = s.sb("pos_i", [P, 1], I32)
        iota_done, link_sem = s.sem("iota_done"), s.sem("link")
        block = ctx.enter_context(nc.Block())

        @block.gpsimd
        def _(pool):
            pool.iota(row_i[:, :], pattern=[[1, P]], base=0, channel_multiplier=0).then_inc(iota_done, 1)
            pool.iota(part_i[:, :], pattern=[[0, 1]], base=0, channel_multiplier=1).then_inc(iota_done, 1)
            pool.iota(pos_i[:, :], pattern=[[0, 1]], base=0, channel_multiplier=EDGE_COLS).then_inc(iota_done, 1)

        @block.vector
        def _(dve):
            link = Link(dve, link_sem)
            dve.wait_ge(iota_done, 3)
            nc.vector.tensor_copy(cst.row[:, :], row_i[:, :])
            nc.vector.tensor_copy(cst.row_b[:, :], row_i[:, :])
            nc.vector.tensor_copy(cst.part_start[:, :], pos_i[:, :])
            link(nc.vector.tensor_copy(cst.part[:, :], part_i[:, :]))
            nc.vector.tensor_scalar(cst.ident[:, :], cst.row[:, :], cst.part[:, 0:1], None, ALU.is_equal)
            nc.vector.tensor_scalar(cst.ident_b[:, :], cst.row[:, :], cst.part[:, 0:1], None, ALU.is_equal)
            nc.vector.tensor_scalar(cst.up_to[:, :], cst.row[:, :], cst.part[:, 0:1], None, ALU.is_ge)
            nc.vector.tensor_scalar(cst.before[:, :], cst.row[:, :], cst.part[:, 0:1], None, ALU.is_gt)
            nc.vector.tensor_scalar(cst.after[:, :], cst.row[:, :], cst.part[:, 0:1], None, ALU.is_lt)
            nc.vector.memset(cst.eps[:, :], EPS)
            link(nc.vector.memset(cst.ones[:, :], 1.0))


def load_edges(nc, cst, raw, src, dst, key_rows):
    with ExitStack() as ctx:
        s = Scope(nc, ctx, "ld_")
        tiles_i = [s.sb(f"tiles_i{k}", [P, BLOCKS, P], I32) for k in range(2)]
        tiles_f = [s.sb(f"tiles_f{k}", [P, BLOCKS, P], F32) for k in range(2)]
        col_i = s.sb("col_i", [P, TILES], I32)
        digit_i = s.sb("digit_i", [P, TILES], I32)
        table_row = s.sb("table_row", [P, TILES], F32)
        turned = s.ps("turned", [P, BLOCKS, P], F32)
        padded, loaded, converted = s.sem("padded"), s.sem("loaded"), s.sem("converted")
        turned_done, read_done, rows_stored, link_sem = s.sem("turned"), s.sem("read"), s.sem("stored"), s.sem("link")
        full = (E // P) // P * P * P
        whole_tiles = (E - full) // P
        rest = E - full - whole_tiles * P
        block = ctx.enter_context(nc.Block())

        @block.gpsimd
        def _(pool):
            for k in range(2):
                pool.memset(tiles_i[k][:, BLOCKS - 1, :], NO_NODE).then_inc(padded, 1)

        @block.sync
        def _(sp):
            sp.wait_ge(padded, 2)
            for k, edges in enumerate((src, dst)):
                sp.dma_start(tiles_i[k][:, 0:BLOCKS - 1, :],
                             edges[0:full].rearrange("(b g p) -> g b p", b=BLOCKS - 1, p=P)).then_inc(loaded, 16)
                sp.dma_start(tiles_i[k][0:whole_tiles, BLOCKS - 1, :],
                             edges[full:full + whole_tiles * P].rearrange("(g p) -> g p", p=P)).then_inc(loaded, 16)
                sp.dma_start(tiles_i[k][whole_tiles:whole_tiles + 1, BLOCKS - 1, 0:rest],
                             edges[full + whole_tiles * P:E].rearrange("(a p) -> a p", a=1)).then_inc(loaded, 16)
            sp.wait_ge(converted, 2)
            sp.dma_start(key_rows[0:(BLOCKS - 1) * P * P].rearrange("(b g p) -> g b p", b=BLOCKS - 1, p=P),
                         tiles_f[0][:, 0:BLOCKS - 1, :]).then_inc(rows_stored, 16)
            sp.dma_start(key_rows[(BLOCKS - 1) * P * P:EDGES].rearrange("(g p) -> g p", p=P),
                         tiles_f[0][0:LAST_TILES, BLOCKS - 1, :]).then_inc(rows_stored, 16)
            sp.wait_ge(rows_stored, 32)

        @block.tensor
        def _(pe):
            for k in range(2):
                pe.wait_ge(converted, 2)
                if k == 1:
                    pe.wait_ge(read_done, 1)
                for b in range(BLOCKS):
                    g = P if b < BLOCKS - 1 else LAST_TILES
                    last = nc.tensor.transpose(turned[:, b, 0:g], tiles_f[k][0:g, b, :], cst.ident[0:g, 0:g])
                last.then_inc(turned_done, 1)

        @block.vector
        def _(dve):
            link = Link(dve, link_sem)
            dve.wait_ge(loaded, 96)
            for k in range(2):
                nc.vector.tensor_copy(tiles_f[k][:, :, :], tiles_i[k][:, :, :]).then_inc(converted, 1)
            flat = turned[:, :, :].rearrange("p b g -> p (b g)")[:, 0:TILES]
            for k in range(2):
                dve.wait_ge(turned_done, k + 1)
                if k == 0:
                    nc.vector.tensor_copy(raw.src_col[:, :], flat)
                nc.vector.tensor_copy(col_i[:, :], flat).then_inc(read_done, 1)
                dve.wait_ge(read_done, k + 1)
                if k == 0:
                    nc.vector.tensor_copy(raw.payload[:, :, 0], col_i[:, :])
                for digit, op, by in ((raw.low[k], ALU.bitwise_and, P - 1),
                                      (raw.high[k], ALU.logical_shift_right, DIGIT_BITS)):
                    link(nc.vector.tensor_scalar(digit_i[:, :], col_i[:, :], by, None, op))
                    link(nc.vector.tensor_copy(digit[:, :], digit_i[:, :]))
            link(nc.vector.scalar_tensor_tensor(out=table_row[:, :], in0=raw.low[1][:, :], scalar=float(NODE_COLS),
                                                in1=raw.high[1][:, :], op0=ALU.mult, op1=ALU.add))
            link(nc.vector.tensor_scalar(raw.payload[:, :, 1], table_row[:, :], float(NODES - 1), None, ALU.min))


def one_hot(nc, cst, out, digit, width):
    shape = [P, GROUP, width]
    return nc.vector.tensor_tensor(out, cst.row_b[:, 0:width].unsqueeze(1).to_broadcast(shape),
                             digit.unsqueeze(2).to_broadcast(shape), ALU.is_equal)


def count_edges(nc, cst, raw, side, o):
    with ExitStack() as ctx:
        s = Scope(nc, ctx, "cnt_")
        one_low = s.sb("one_low", [P, 2, GROUP, P], BF16)
        one_high = s.sb("one_high", [P, 2, GROUP, NODE_COLS], BF16)
        zero_b = s.sb("zero_b", [P, P], BF16)
        counted = s.ps("counted", [P, NODE_COLS], F32)
        hot_ready, hot_free, zeroed, sums_done = s.sem("hot_ready"), s.sem("hot_free"), s.sem("zeroed"), s.sem("sums")
        block = ctx.enter_context(nc.Block())
        rounds = TILES // (2 * GROUP)

        @block.vector
        def _(dve):
            nc.vector.memset(zero_b[:, :], 0.0).then_inc(zeroed, 1)

            def round_(i):
                for b in range(2):
                    wait_if(dve, hot_free, i * 2 + b - 1)
                    at = bass.ds((i * 2 + b) * GROUP, GROUP)
                    one_hot(nc, cst, one_low[:, b, :, :], raw.low[side][:, at], P)
                    one_hot(nc, cst, one_high[:, b, :, :], raw.high[side][:, at], NODE_COLS).then_inc(hot_ready, 1)

            run_rounds(dve, rounds, round_)
            dve.wait_ge(sums_done, 1)
            nc.vector.tensor_copy(o.count[:, :], counted[:, :])

        @block.tensor
        def _(pe):
            pe.wait_ge(zeroed, 1)
            nc.tensor.matmul(counted[:, :], zero_b[:, :], zero_b[:, 0:NODE_COLS], start=True, stop=False)

            def round_(i):
                for b in range(2):
                    pe.wait_ge(hot_ready, i * 2 + b + 1)
                    for u in range(GROUP):
                        last = nc.tensor.matmul(counted[:, :], one_low[:, b, u, :], one_high[:, b, u, :],
                                                start=False, stop=False)
                    last.then_inc(hot_free, 1)

            run_rounds(pe, rounds, round_)
            nc.tensor.matmul(counted[:, :], zero_b[:, :], zero_b[:, 0:NODE_COLS], start=False, stop=True).then_inc(sums_done, 1)


def place_nodes(nc, cst, name, o):
    with ExitStack() as ctx:
        s = Scope(nc, ctx, name)
        total = s.sb("total", [P, NODE_COLS], F32)
        col_end = s.sb("col_end", [P, NODE_COLS], F32)
        has = s.sb("has", [P, NODE_COLS], F32)
        work = s.sb("work", [P, NODE_COLS], F32)
        root = s.sb("root", [P, NODE_COLS], F32)
        within = s.ps("within", [P, NODE_COLS], F32)
        totals = s.ps("totals", [P, NODE_COLS], F32)
        degree_ready, root_done, prefix_done, link_sem = s.sem("degree"), s.sem("root"), s.sem("prefix"), s.sem("link")
        block = ctx.enter_context(nc.Block())

        @block.tensor
        def _(pe):
            nc.tensor.matmul(within[:, :], cst.up_to[:, :], o.count[:, :], start=True, stop=True)
            nc.tensor.matmul(totals[:, :], cst.ones[:, :], o.count[:, :], start=True, stop=True).then_inc(prefix_done, 1)

        @block.scalar
        def _(act):
            act.wait_ge(degree_ready, 1)
            nc.scalar.activation(root[:, :], o.inv_root[:, :], ACT.Sqrt).then_inc(root_done, 1)

        @block.vector
        def _(dve):
            link = Link(dve, link_sem)
            nc.vector.tensor_scalar(o.inv_root[:, :], o.count[:, :], 1.0, None, ALU.max).then_inc(degree_ready, 1)
            link(nc.vector.tensor_scalar(has[:, :], o.count[:, :], 0.0, None, ALU.is_gt))
            dve.wait_ge(prefix_done, 1)
            link(nc.vector.tensor_copy(total[:, :], totals[:, :]))
            link(nc.vector.tensor_tensor_scan(out=col_end[:, :], data0=cst.ones[:, 0:NODE_COLS], data1=total[:, :],
                                              initial=0.0, op0=ALU.mult, op1=ALU.add))
            link(nc.vector.tensor_tensor(col_end[:, :], col_end[:, :], total[:, :], ALU.subtract))
            link(nc.vector.tensor_tensor(work[:, :], col_end[:, :], within[:, :], ALU.add))
            link(nc.vector.tensor_tensor(o.start[:, :], work[:, :], o.count[:, :], ALU.subtract))
            link(nc.vector.tensor_scalar(work[:, :], work[:, :], -1.0 - EDGES, None, ALU.add))
            link(nc.vector.tensor_tensor(work[:, :], work[:, :], has[:, :], ALU.mult))
            link(nc.vector.tensor_scalar(o.end_row[:, :], work[:, :], float(EDGES), None, ALU.add))
            link(nc.vector.tensor_scalar(work[:, :], o.start[:, :], -float(EDGES), None, ALU.add))
            link(nc.vector.tensor_tensor(work[:, :], work[:, :], has[:, :], ALU.mult))
            link(nc.vector.tensor_scalar(o.start_row[:, :], work[:, :], float(EDGES), None, ALU.add))
            dve.wait_ge(root_done, 1)
            link(nc.vector.reciprocal(o.inv_root[:, :], root[:, :]))
            link(nc.vector.tensor_tensor(o.inv_root[:, :], o.inv_root[:, :], has[:, :], ALU.mult))


def sort_by_src(nc, cst, raw, by_src, by_dst, key_rows, by_src_edges, fills, states):
    with ExitStack() as ctx:
        s = Scope(nc, ctx, "sort_")
        keys = s.sb("keys", [P, 2, GROUP, P], F32)
        one_low = [s.sb(f"one_low{k}", [P, 2, GROUP, P], BF16) for k in range(2)]
        one_high = [s.sb(f"one_high{k}", [P, 2, GROUP, NODE_COLS], BF16) for k in range(2)]
        low_t = s.sb("low_t", [P, 2, GROUP, P], F32)
        place = s.sb("place", [P, 2, NODE_COLS], F32)
        same = s.sb("same", [P, 2, P], F32)
        picked = s.sb("picked", [P, 2, NODE_COLS], F32)
        base = s.sb("base", [P, 2, GROUP], F32)
        rank = s.sb("rank", [P, 2, GROUP], F32)
        target = s.sb("target", [P, 2, GROUP], I32)
        payload = s.sb("payload", [P, 2, GROUP, 2], I32)
        pad_place = s.sb("pad_place", [P, TILES], F32)
        place_i = s.sb("place_i", [P, TILES], I32)
        zeros = s.sb("zeros", [P, GROUP * H], F32)
        zero_b = s.sb("zero_b", [P, P], BF16)
        table = s.ps("table", [P, 512], F32)[:, 0:NODE_COLS]
        counts = s.ps("counts", [P, 512], F32)[:, 0:NODE_COLS]
        read = s.ps("read", [P, 2, 512], F32)
        turned = s.ps("turned", [P, 24, P], BF16)
        iota_done, keys_in = s.sem("iota_done"), [s.sem("keys_in0"), s.sem("keys_in1")]
        keys_free, hot_ready, hot_free = s.sem("keys_free"), s.sem("hot_ready"), s.sem("hot_free")
        turned_done, low_t_ready, table_ready = s.sem("turned"), s.sem("low_t_ready"), s.sem("table")
        read_done, read_free, table_counted = s.sem("read"), s.sem("read_free"), s.sem("table_counted")
        target_ready, link_sem, counts_done = s.sem("target"), s.sem("link"), s.sem("counts_done")
        scattered = [s.sem("scattered0"), s.sem("scattered1")]
        zeroed, filled = s.sem("zeroed"), s.sem("filled")
        rounds = TILES // (2 * GROUP)
        block = ctx.enter_context(nc.Block())

        @block.sync
        def _(sp):
            flat = key_rows.rearrange("(a e) -> a e", a=1)
            sp.wait_ge(zeroed, 1)

            def round_(i):
                for b in range(2):
                    wait_if(sp, keys_free, i * 2 + b - 1)
                    piece = flat[:, bass.ds((i * 2 + b) * (GROUP * P), GROUP * P)]
                    sp.dma_start(keys[:, b, :, :].rearrange("p g e -> p (g e)"),
                                 piece.to_broadcast([P, GROUP * P])).then_inc(keys_in[b], 16)
                    for fill in fills:
                        view = fill[0:EDGES, :].rearrange("(p t) f -> p (t f)", p=P)
                        sp.dma_start(view[:, bass.ds((i * 2 + b) * (GROUP * H), GROUP * H)],
                                     zeros[:, :]).then_inc(filled, 16)

            run_rounds(sp, rounds, round_)
            for state, width in states:
                sp.dma_start(state[EDGES:EDGES + P, :], zeros[:, 0:width]).then_inc(filled, 16)
            sp.wait_ge(filled, 16 * (len(fills) * rounds * 2 + len(states)))

        @block.gpsimd
        def _(pool):
            pool.memset(zeros[:, :], 0.0).then_inc(zeroed, 1)
            pool.iota(place_i[:, :], pattern=[[P, TILES]], base=0, channel_multiplier=0).then_inc(iota_done, 1)

            def round_(i):
                for b in range(2):
                    pool.wait_ge(target_ready, i * 2 + b + 1)
                    part_wait(pool)
                    for u in range(GROUP):
                        pool.indirect_dma_start(out=by_src_edges[:, :], out_offset=rows(target[:, b, u:u + 1]),
                                                in_=payload[:, b, u, :], in_offset=None).then_inc(scattered[b], 16)

            run_rounds(pool, rounds, round_)
            for b in range(2):
                pool.wait_ge(scattered[b], 16 * GROUP * rounds)

        @block.vector
        def _(dve):
            link = Link(dve, link_sem)
            nc.vector.memset(zero_b[:, :], 0.0)
            dve.wait_ge(iota_done, 1)
            link(nc.vector.tensor_scalar(pad_place[:, :], raw.src_col[:, :], float(NO_NODE), None, ALU.is_equal))
            link(nc.vector.scalar_tensor_tensor(out=pad_place[:, :], in0=place_i[:, :], scalar=float(E),
                                                in1=pad_place[:, :], op0=ALU.max, op1=ALU.mult))

            def hot_parts(group, b):
                at = bass.ds(group * GROUP, GROUP)

                def piece(part):
                    k, high = divmod(part, 2)
                    if high:
                        ins = one_hot(nc, cst, one_high[k][:, b, :, :], raw.high[k][:, at], NODE_COLS)
                    else:
                        ins = one_hot(nc, cst, one_low[k][:, b, :, :], raw.low[k][:, at], P)
                    if part == 3:
                        ins.then_inc(hot_ready, 1)

                return piece

            for part in range(4):
                hot_parts(0, 0)(part)
            dve.wait_ge(hot_ready, 1)
            link.start_loop()
            steps = 2

            def round_(i):
                link.iteration(i, steps)
                for b in range(2):
                    group = i * 2 + b
                    at = bass.ds(group * GROUP, GROUP)
                    next_group = not (isinstance(i, int) and i == rounds - 1 and b == 1)
                    dve.wait_ge(keys_in[b], 16 * (i + 1))
                    for u in range(GROUP):
                        t = group * GROUP + u
                        v = (b * GROUP + u) % 2
                        wait_if(dve, read_free, t - 1)
                        compared = nc.vector.scalar_tensor_tensor(
                            out=same[:, v, :], in0=keys[:, b, u, :], scalar=raw.src_col[:, bass.ds(t, 1)],
                            in1=cst.after[:, :], op0=ALU.is_equal, op1=ALU.mult, accum_out=rank[:, b, u:u + 1])
                        if u == GROUP - 1:
                            compared.then_inc(keys_free, 1)
                        dve.wait_ge(read_done, t + 1)
                        nc.vector.scalar_tensor_tensor(
                            out=picked[:, v, :], in0=one_high[0][:, b, u, :], scalar=1.0,
                            in1=read[:, v, 0:NODE_COLS], op0=ALU.mult, op1=ALU.mult,
                            accum_out=base[:, b, u:u + 1]).then_inc(read_free, 1)
                        if next_group and u in HOT_AFTER:
                            if u == HOT_AFTER[0]:
                                wait_if(dve, hot_free, group)
                            hot_parts(group + 1, 1 - b)(HOT_AFTER.index(u))
                    dve.wait_ge(read_free, (group + 1) * GROUP)
                    link(nc.vector.tensor_tensor(rank[:, b, :], rank[:, b, :], pad_place[:, at], ALU.add))
                    wait_if(dve, scattered[b], i * (16 * GROUP))
                    part_wait(dve)
                    nc.vector.tensor_copy(payload[:, b, :, :], raw.payload[:, at, :])
                    nc.vector.tensor_tensor(target[:, b, :], rank[:, b, :], base[:, b, :], ALU.add).then_inc(target_ready, 1)
                    dve.wait_ge(target_ready, group + 1)

            run_rounds(dve, rounds, round_)
            dve.wait_ge(counts_done, 1)
            nc.vector.tensor_copy(by_dst.count[:, :], counts)

        @block.scalar
        def _(act):
            nc.scalar.copy(place[:, 0, :], by_src.start[:, :]).then_inc(table_ready, 1)
            act.wait_ge(turned_done, 1)
            nc.scalar.copy(low_t[:, 0, :, :], turned[:, 0:GROUP, :]).then_inc(low_t_ready, 1)

            def round_(i):
                for b in range(2):
                    group = i * 2 + b
                    for u in range(GROUP):
                        v = b * GROUP + u
                        act.wait_ge(table_counted, group * GROUP + u + 1)
                        nc.scalar.copy(place[:, (v + 1) % 2, :], table).then_inc(table_ready, 1)
                        if u == TURN_AT and not (isinstance(i, int) and i == rounds - 1 and b == 1):
                            act.wait_ge(turned_done, group + 2)
                            nc.scalar.copy(low_t[:, 1 - b, :, :], turned[:, 0:GROUP, :]).then_inc(low_t_ready, 1)

            run_rounds(act, rounds, round_)

        @block.tensor
        def _(pe):
            def turn(b):
                for u in range(GROUP):
                    last = nc.tensor.transpose(turned[:, u, :], one_low[0][:, b, u, :], cst.ident_b[:, :])
                last.then_inc(turned_done, 1)

            nc.tensor.matmul(table, cst.ident[:, :], by_src.start[:, :], start=True, stop=True)
            pe.wait_ge(hot_ready, 1)
            nc.tensor.matmul(counts, zero_b[:, :], zero_b[:, 0:NODE_COLS], start=True, stop=False)
            turn(0)

            def round_(i):
                for b in range(2):
                    group = i * 2 + b
                    pe.wait_ge(low_t_ready, group + 1)
                    for u in range(GROUP):
                        v = b * GROUP + u
                        t = group * GROUP + u
                        pe.wait_ge(table_ready, t + 1)
                        nc.tensor.matmul(table, one_low[0][:, b, u, :], one_high[0][:, b, u, :], start=False, stop=True,
                                         skip_group_check=True).then_inc(table_counted, 1)
                        wait_if(pe, read_free, t - 1)
                        nc.tensor.matmul(read[:, v % 2, 0:NODE_COLS], low_t[:, b, u, :], place[:, v % 2, :],
                                         start=True, stop=True).then_inc(read_done, 1)
                        counted = nc.tensor.matmul(counts, one_low[1][:, b, u, :], one_high[1][:, b, u, :],
                                                   start=False, stop=False)
                        if u == GROUP - 1:
                            counted.then_inc(hot_free, 1)
                        if u == TURN_AT and not (isinstance(i, int) and i == rounds - 1 and b == 1):
                            pe.wait_ge(hot_ready, group + 2)
                            turn(1 - b)

            run_rounds(pe, rounds, round_)
            nc.tensor.matmul(counts, zero_b[:, :], zero_b[:, 0:NODE_COLS], start=False, stop=True).then_inc(counts_done, 1)


def edge_order(nc, cst, order, src, dst, by_src_edges):
    from_sort = order.name == "src"
    with ExitStack() as ctx:
        s = Scope(nc, ctx, order.name + "_ord_")
        pairs = s.sb("pairs", [P, EDGE_COLS, 2], I32) if from_sort else None
        key_i = s.sb("key_i", [P, EDGE_COLS], I32)
        other_i = s.sb("other_i", [P, EDGE_COLS], I32)
        key = s.sb("key", [P, EDGE_COLS], F32)
        work = s.sb("work", [P, EDGE_COLS], F32)
        digit_i = s.sb("digit_i", [P, EDGE_COLS], I32)
        high = s.sb("high", [P, EDGE_COLS], F32)
        first_of = s.sb("first_of", [P, P], F32)
        run = s.sb("run", [P, 1], F32)
        first_rows = s.ps("first_rows", [P, P], F32)
        padded, loaded, firsts_ready, firsts_turned, link_sem = (
            s.sem("padded"), s.sem("loaded"), s.sem("firsts"), s.sem("turned"), s.sem("link"))
        block = ctx.enter_context(nc.Block())

        @block.gpsimd
        def _(pool):
            if not from_sort:
                pool.memset(key_i[:, :], NO_NODE).then_inc(padded, 1)
                pool.memset(other_i[:, :], NO_NODE).then_inc(padded, 1)

        @block.sync
        def _(sp):
            if from_sort:
                sp.dma_start(pairs[:, :, :].rearrange("p t a -> p (t a)"),
                             by_src_edges.rearrange("(p t) a -> p (t a)", p=P)).then_inc(loaded, 16)
                return
            sp.wait_ge(padded, 2)
            cut = (P - 1) * EDGE_COLS
            for ends, at in ((dst, key_i), (src, other_i)):
                sp.dma_start(at[0:P - 1, :], ends[0:cut].rearrange("(p t) -> p t", p=P - 1)).then_inc(loaded, 16)
                sp.dma_start(at[P - 1:P, 0:LAST_EDGES],
                             ends[cut:E].rearrange("(a t) -> a t", a=1)).then_inc(loaded, 16)

        @block.vector
        def _(dve):
            link = Link(dve, link_sem)

            def table_rows(out, node_i, n):
                link(nc.vector.tensor_scalar(digit_i[:, 0:n], node_i, P - 1, None, ALU.bitwise_and))
                link(nc.vector.tensor_copy(work[:, 0:n], digit_i[:, 0:n]))
                link(nc.vector.tensor_scalar(digit_i[:, 0:n], node_i, DIGIT_BITS, None, ALU.logical_shift_right))
                link(nc.vector.tensor_copy(high[:, 0:n], digit_i[:, 0:n]))
                link(nc.vector.scalar_tensor_tensor(out=work[:, 0:n], in0=work[:, 0:n], scalar=float(NODE_COLS),
                                                    in1=high[:, 0:n], op0=ALU.mult, op1=ALU.add))
                link(nc.vector.tensor_scalar(out, work[:, 0:n], float(NODES - 1), None, ALU.min))

            dve.wait_ge(loaded, 16 if from_sort else 64)
            if from_sort:
                link(nc.vector.tensor_copy(key_i[:, :], pairs[:, :, 0]))
                link(nc.vector.tensor_copy(order.gather_rows[:, :], pairs[:, :, 1]))
            else:
                table_rows(order.gather_rows[:, :], other_i[:, :], EDGE_COLS)
            link(nc.vector.tensor_copy(key[:, :], key_i[:, :]))
            table_rows(order.first_row[:, :], key_i[:, 0:1], 1)
            link(nc.vector.memset(order.same[:, 0:1], 0.0))
            link(nc.vector.tensor_tensor(order.same[:, 1:EDGE_COLS], key[:, 1:EDGE_COLS], key[:, 0:EDGE_COLS - 1],
                                         ALU.is_equal))
            link(nc.vector.tensor_scalar(work[:, :], key[:, :], key[:, 0:1], None, ALU.is_equal))
            link(nc.vector.reduce_sum(run[:, :], work[:, :], AX.X))
            link(nc.vector.tensor_scalar(run[:, :], run[:, :], -1.0, None, ALU.add))
            link(nc.vector.tensor_tensor(order.first_end[:, :], run[:, :], cst.part_start[:, :], ALU.add))
            nc.vector.tensor_copy(first_of[:, :], key[:, 0:1].to_broadcast([P, P])).then_inc(firsts_ready, 1)
            dve.wait_ge(firsts_turned, 1)
            link(nc.vector.scalar_tensor_tensor(out=order.carry[:, :], in0=first_rows[:, :],
                                                scalar=key[:, EDGE_COLS - 1:EDGE_COLS], in1=cst.before[:, :],
                                                op0=ALU.is_equal, op1=ALU.mult))

        @block.tensor
        def _(pe):
            pe.wait_ge(firsts_ready, 1)
            nc.tensor.matmul(first_rows[:, :], first_of[:, :], cst.ident[:, :], start=True, stop=True).then_inc(firsts_turned, 1)


def prepare_weights(nc, cst, w, args):
    (W1, b1, W2, b2, W1_root, W1_rel, g_b1, W2_root, W2_rel, g_b2, W_src, b_src, W_dst, b_dst,
     s_W1, s_W2, s_W3, s_W4) = args
    with ExitStack() as ctx:
        s = Scope(nc, ctx, "w_")
        sides = [s.sb(f"side{n}", [D, 2 * D], F32) for n in range(4)]
        bias2 = s.sb("bias2", [P, 2, D], F32)
        w4 = s.sb("w4", [D, 1], F32)
        w4_wide = s.sb("w4_wide", [D, P], F32)
        w3_t = s.sb("w3_t", [P, D], F32)
        turned = s.ps("turned", [P, 4, P], F32)
        v_ps = s.ps("v_ps", [P, D], F32)
        loaded, turned_done, w3_ready, v_done, link_sem = (
            s.sem("loaded"), s.sem("turned"), s.sem("w3"), s.sem("v"), s.sem("link"))
        block = ctx.enter_context(nc.Block())
        pairs = ((W1_root, W1_rel), (W2_root, W2_rel), (s_W1, s_W2), (s_W3, s_W3))
        loads = []
        for side, two in zip(sides, pairs):
            loads += [(side[:, 0:D], two[0]), (side[:, D:2 * D], two[1])]
        loads += [(w.edge_in[:, 0:H], W1[0:D, :]), (w.edge_in[:, H:2 * H], W1[D:2 * D, :]), (w.edge_out[:, :], W2),
                  (w.directed[0:D, :], W_src), (w.directed[D:2 * D, :], W_dst), (w4[:, :], s_W4)]

        def wide(v, n):
            return v.rearrange("(a n) -> a n", a=1).to_broadcast([P, n])

        loads += [(w.edge_bias[:, :], wide(b1, H)), (w.edge_out_bias[:, :], wide(b2, D)),
                  (w.conv_bias[0][:, :], wide(g_b1, D)), (w.conv_bias[1][:, :], wide(g_b2, D)),
                  (bias2[:, 0, :], wide(b_src, D)), (bias2[:, 1, :], wide(b_dst, D))]

        @block.sync
        def _(sp):
            for to, of in loads:
                sp.dma_start(to, of).then_inc(loaded, 16)

        @block.tensor
        def _(pe):
            pe.wait_ge(loaded, 16 * len(loads))
            for n in range(4):
                last = nc.tensor.transpose(turned[:, n, 0:D], sides[n][:, :], cst.ident[0:D, 0:D])
            last.then_inc(turned_done, 1)
            pe.wait_ge(w3_ready, 1)
            nc.tensor.matmul(v_ps[:, :], w4_wide[:, :], w3_t[0:D, :], start=True, stop=True).then_inc(v_done, 1)

        @block.vector
        def _(dve):
            link = Link(dve, link_sem)
            dve.wait_ge(loaded, 16 * len(loads))
            link(nc.vector.tensor_scalar(w.directed[:, :], w.directed[:, :], 0.5, None, ALU.mult))
            link(nc.vector.tensor_scalar(bias2[:, :, :], bias2[:, :, :], 0.5, None, ALU.mult))
            link(nc.vector.tensor_tensor(w.directed_bias[:, :], bias2[:, 0, :], bias2[:, 1, :], ALU.add))
            link(nc.vector.tensor_scalar(w4[:, :], w4[:, :], 0.0, None, ALU.max))
            link(nc.vector.tensor_copy(w4_wide[:, :], w4[:, 0:1].to_broadcast([D, P])))
            dve.wait_ge(turned_done, 1)
            for n, to in enumerate((w.conv[0], w.conv[1], w.steps)):
                nc.vector.tensor_copy(to[:, :], turned[:, n, 0:D])
            nc.vector.tensor_copy(w3_t[:, :], turned[:, 3, 0:D]).then_inc(w3_ready, 1)
            dve.wait_ge(v_done, 1)
            link(nc.vector.tensor_copy(w.degree_row[:, :], v_ps[:, :]))


def normalise(nc, link, act_part, out, x, t):
    wide = [P, CHUNK, D]
    part_wait(link.eng)
    link(nc.vector.reduce_sum(t.mean[:, :], x, AX.X))
    link(nc.vector.tensor_scalar(t.mean[:, :], t.mean[:, :], 1.0 / D, None, ALU.mult))
    link(nc.vector.tensor_tensor(t.centred[:, :, :], x, t.mean[:, :].unsqueeze(2).to_broadcast(wide), ALU.subtract))
    link(nc.vector.tensor_tensor(t.squares[:, :, :], t.centred[:, :, :], t.centred[:, :, :], ALU.mult))
    part_wait(link.eng)
    act_part(nc.vector.reduce_sum(t.var[:, :], t.squares[:, :, :], AX.X))
    link(nc.vector.reciprocal(t.std[:, :], t.std[:, :]))
    link(nc.vector.scalar_tensor_tensor(out=out, in0=t.centred[:, :, :], scalar=0.0,
                                        in1=t.std[:, :].unsqueeze(2).to_broadcast(wide), op0=ALU.max, op1=ALU.mult))


class Temps:
    def __init__(self, s):
        self.mean, self.var, self.std = s.sb("mean", [P, CHUNK], F32), s.sb("var", [P, CHUNK], F32), s.sb("std", [P, CHUNK], F32)
        self.centred, self.squares = s.sb("centred", [P, CHUNK, D], F32), s.sb("squares", [P, CHUNK, D], F32)


def first_layer_tables(nc, cst, w, orders, nodes_of, x, x_sb, source_table, target_table, fills):
    with ExitStack() as ctx:
        s = Scope(nc, ctx, "tab_")
        t = Temps(s)
        h = s.sb("h", [P, 2, CHUNK, D], F32)
        h_t = s.sb("h_t", [D, CHUNK, P], F32)
        ends = s.sb("ends", [P, 2, CHUNK, 2 * H], F32)
        starts = s.sb("starts", [P, 2, 2, CHUNK], I32)
        firsts = s.sb("firsts", [P, 2, H], F32)
        first_rows = s.sb("first_rows", [P, 2], I32)
        turned = s.ps("turned", [D, 8, P], F32)
        products = s.ps("products", [P, 8, 2 * H], F32)
        padded, loaded, link_sem = s.sem("padded"), s.sem("loaded"), s.sem("link")
        var_ready, std_ready, h_ready, turned_done = s.sem("var"), s.sem("std"), s.sem("h"), s.sem("turned")
        h_t_ready, products_done, ends_ready = s.sem("h_t"), s.sem("products"), s.sem("ends")
        stored, scattered, first_in, first_out = s.sem("stored"), s.sem("scattered"), s.sem("first_in"), s.sem("first_out")
        block = ctx.enter_context(nc.Block())
        last_col = NODE_COLS - 1

        @block.gpsimd
        def _(pool):
            pool.memset(x_sb[:, last_col, :], 0.0).then_inc(padded, 1)

            def round_(j):
                for b in range(2):
                    pool.wait_ge(ends_ready, j * 2 + b + 1)
                    part_wait(pool)
                    for c in range(CHUNK):
                        for k in range(2):
                            pool.indirect_dma_start(out=fills[k][:, :], out_offset=rows(starts[:, b, k, c:c + 1]),
                                                    in_=ends[:, b, c, 0:H], in_offset=None, bounds_check=EDGES - 1,
                                                    oob_is_err=False).then_inc(scattered, 16)

            run_rounds(pool, CHUNK_PAIRS, round_)
            pool.wait_ge(scattered, 16 * NODE_COLS * 2)
            pool.wait_ge(stored, 16 * NODE_COLS // CHUNK * 2)
            for k in range(2):
                pool.indirect_dma_start(out=firsts[:, k, :], out_offset=None, in_=target_table[:, :],
                                        in_offset=rows(orders[k].first_row[:, 0:1])).then_inc(first_in, 16)
            pool.wait_ge(first_in, 32)
            for k in range(2):
                pool.dma_start(fills[k][0:EDGES, :].rearrange("(p t) f -> p t f", p=P)[:, 0, :],
                               firsts[:, k, :]).then_inc(first_out, 16)
            pool.wait_ge(first_out, 32)

        @block.sync
        def _(sp):
            sp.wait_ge(padded, 1)
            sp.dma_start(x_sb[:, 0:last_col, :], x[0:last_col * P, :].rearrange("(c p) f -> p c f", p=P)).then_inc(loaded, 16)
            sp.dma_start(x_sb[0:LAST_NODES, last_col, :], x[last_col * P:N, :]).then_inc(loaded, 16)

            def round_(j):
                for b in range(2):
                    sp.wait_ge(ends_ready, j * 2 + b + 1)
                    for table, half in ((target_table, 0), (source_table, 1)):
                        sp.dma_start(table.rearrange("(p c) f -> p c f", p=P)[:, bass.ds((j * 2 + b) * CHUNK, CHUNK), :],
                                     ends[:, b, :, half * H:half * H + H]).then_inc(stored, 16)

            run_rounds(sp, CHUNK_PAIRS, round_)
            sp.wait_ge(stored, 16 * NODE_COLS // CHUNK * 2)

        @block.scalar
        def _(act):
            def round_(j):
                for b in range(2):
                    act.wait_ge(var_ready, j * 2 + b + 1)
                    nc.scalar.activation(t.std[:, :], t.var[:, :], ACT.Sqrt, bias=cst.eps[:, 0:1], scale=1.0 / D).then_inc(std_ready, 1)
                    act.wait_ge(turned_done, j * 2 + b + 1)
                    nc.scalar.copy(h_t[:, :, :], turned[:, 0:CHUNK, :]).then_inc(h_t_ready, 1)

            run_rounds(act, CHUNK_PAIRS, round_)

        @block.tensor
        def _(pe):
            def round_(j):
                for b in range(2):
                    pe.wait_ge(h_ready, j * 2 + b + 1)
                    part_wait(pe)
                    for c in range(CHUNK):
                        last = nc.tensor.transpose(turned[:, c, :], h[:, b, c, :], cst.ident[:, :])
                    last.then_inc(turned_done, 1)
                    pe.wait_ge(h_t_ready, j * 2 + b + 1)
                    wait_if(pe, ends_ready, j * 2 + b)
                    for c in range(CHUNK):
                        last = nc.tensor.matmul(products[:, c, :], h_t[:, c, :], w.edge_in[:, :], start=True, stop=True)
                    last.then_inc(products_done, 1)

            run_rounds(pe, CHUNK_PAIRS, round_)

        @block.vector
        def _(dve):
            link = Link(dve, link_sem)
            dve.wait_ge(loaded, 32)
            link.start_loop()
            steps = 2 * 6

            def round_(j):
                link.iteration(j, steps)
                for b in range(2):
                    chunk = j * 2 + b
                    at = bass.ds(chunk * CHUNK, CHUNK)

                    def act_part(ins):
                        ins.then_inc(var_ready, 1)
                        dve.wait_ge(std_ready, chunk + 1)

                    normalise(nc, link, act_part, h[:, b, :, :], x_sb[:, at, :], t)
                    nc.vector.tensor_tensor(x_sb[:, at, :], x_sb[:, at, :], h[:, b, :, :], ALU.add).then_inc(h_ready, 1)
                    dve.wait_ge(products_done, chunk + 1)
                    wait_if(dve, stored, j * (16 * 2 * 2))
                    wait_if(dve, scattered, j * (16 * 2 * 2 * CHUNK))
                    part_wait(dve)
                    nc.vector.tensor_copy(ends[:, b, :, 0:H], products[:, 0:CHUNK, 0:H])
                    nc.vector.tensor_copy(starts[:, b, 0, :], nodes_of[0].start_row[:, at])
                    nc.vector.tensor_copy(starts[:, b, 1, :], nodes_of[1].start_row[:, at])
                    nc.vector.tensor_tensor(ends[:, b, :, H:2 * H], products[:, 0:CHUNK, H:2 * H],
                                            w.edge_bias[:, :].unsqueeze(1).to_broadcast([P, CHUNK, H]),
                                            ALU.add).then_inc(ends_ready, 1)

            run_rounds(dve, CHUNK_PAIRS, round_)
            link.end_loop(CHUNK_PAIRS, steps)


def sum_over_edges(nc, cst, name, order, table, state, width, fill):
    with ExitStack() as ctx:
        s = Scope(nc, ctx, name)
        got = s.sb("got", [P, BUFS, GROUP, width], F32)
        idx = s.sb("idx", [P, BUFS, GROUP], I32)
        ends = s.sb("ends", [P, 2, GROUP, width], F32) if fill is not None else None
        carry_sb = s.sb("carry_sb", [P, width], F32)
        carry_ps = s.ps("carry_ps", [P, width], F32)
        idx_ready = s.sem("idx_ready")
        gathered = [s.sem(f"gathered{b}") for b in range(BUFS)]
        stored = [s.sem(f"stored{b}") for b in range(BUFS)]
        scanned, ends_in, ends_step, rows_ready = s.sem("scanned"), [s.sem("ends_in0"), s.sem("ends_in1")], s.sem("ends_step"), s.sem("rows_ready")
        added, carried, carry_ready, carry_added, cleared = s.sem("added"), s.sem("carried"), s.sem("carry_ready"), s.sem("carry_added"), s.sem("cleared")
        block = ctx.enter_context(nc.Block())

        def last_group(i, b):
            return isinstance(i, int) and i == ROUNDS - 1 and b == BUFS - 1

        state_v = state[0:EDGES, :].rearrange("(p t) f -> p (t f)", p=P)

        @block.sync
        def _(sp):
            def load_ends(group, b):
                fill_v = fill[0:EDGES, :].rearrange("(p t) f -> p (t f)", p=P)
                sp.dma_start(ends[:, b % 2, :, :].rearrange("p u f -> p (u f)"),
                             fill_v[:, bass.ds(group * (GROUP * width), GROUP * width)]).then_inc(ends_in[b % 2], 16)

            if fill is not None:
                load_ends(0, 0)

            def round_(i):
                for b in range(BUFS):
                    group = i * BUFS + b
                    if fill is not None and not last_group(i, b):
                        sp.wait_ge(ends_step, (group + 1) * GROUP)
                        load_ends(group + 1, b + 1)
                    sp.wait_ge(scanned, (group + 1) * GROUP)
                    sp.dma_start(state_v[:, bass.ds(group * (GROUP * width), GROUP * width)],
                                 got[:, b, :, :].rearrange("p u f -> p (u f)")).then_inc(stored[b], 16)

            run_rounds(sp, ROUNDS, round_)
            for b in range(BUFS):
                sp.wait_ge(stored[b], 16 * ROUNDS)

        @block.gpsimd
        def _(pool):
            def round_(i):
                for b in range(BUFS):
                    pool.wait_ge(idx_ready, i * BUFS + b + 1)
                    wait_if(pool, stored[b], i * 16)
                    part_wait(pool)
                    for u in range(GROUP):
                        pool.indirect_dma_start(out=got[:, b, u, :], out_offset=None, in_=table[:, :],
                                                in_offset=rows(idx[:, b, u:u + 1])).then_inc(gathered[b], 16)

            run_rounds(pool, ROUNDS, round_)
            pool.wait_ge(carry_ready, 1)
            for b in range(BUFS):
                pool.wait_ge(stored[b], 16 * ROUNDS)
            pool.indirect_dma_start(out=state[:, :], out_offset=rows(order.first_end[:, 0:1]), in_=carry_sb[:, :],
                                    in_offset=None, compute_op=ALU.add).then_inc(carry_added, 16)
            pool.wait_ge(carry_added, 16)

        @block.scalar
        def _(act):
            def stage(group, b):
                nc.scalar.copy(idx[:, b % BUFS, :], order.gather_rows[:, bass.ds(group * GROUP, GROUP)]).then_inc(idx_ready, 1)

            for group in range(AHEAD):
                stage(group, group)

            def round_(i):
                for b in range(BUFS):
                    group = i * BUFS + b
                    if fill is not None:
                        act.wait_ge(added, group + 1)
                        nc.scalar.activation(got[:, b, :, :], got[:, b, :, :], ACT.Relu).then_inc(rows_ready, 1)
                    if not (isinstance(i, int) and i == ROUNDS - 1 and b + AHEAD >= BUFS):
                        act.wait_ge(scanned, group * GROUP + 1)
                        stage(group + AHEAD, b + AHEAD)

            run_rounds(act, ROUNDS, round_)

        @block.vector
        def _(dve):
            nc.vector.memset(got[:, BUFS - 1, GROUP - 1, :], 0.0).then_inc(cleared, 1)
            if fill is not None:
                nc.vector.memset(ends[:, 1, GROUP - 1, :], 0.0).then_inc(cleared, 1)
            dve.wait_ge(cleared, 1 if fill is None else 2)

            def round_(i):
                for b in range(BUFS):
                    group = i * BUFS + b
                    first = group * GROUP
                    if fill is not None:
                        dve.wait_ge(ends_in[b % 2], (i * 2 + b // 2 + 1) * 16)
                        for u in range(GROUP):
                            before = ends[:, b % 2, u - 1, :] if u else ends[:, 1 - b % 2, GROUP - 1, :]
                            nc.vector.scalar_tensor_tensor(
                                out=ends[:, b % 2, u, :], in0=before, scalar=order.same[:, bass.ds(first + u, 1)],
                                in1=ends[:, b % 2, u, :], op0=ALU.mult, op1=ALU.add).then_inc(ends_step, 1)
                            dve.wait_ge(ends_step, first + u + 1)
                        dve.wait_ge(gathered[b], (i + 1) * (16 * GROUP))
                        nc.vector.tensor_tensor(got[:, b, :, :], got[:, b, :, :], ends[:, b % 2, :, :], ALU.add).then_inc(added, 1)
                        dve.wait_ge(rows_ready, group + 1)
                    else:
                        dve.wait_ge(gathered[b], (i + 1) * (16 * GROUP))
                    for u in range(GROUP):
                        before = got[:, b, u - 1, :] if u else got[:, (b - 1) % BUFS, GROUP - 1, :]
                        nc.vector.scalar_tensor_tensor(
                            out=got[:, b, u, :], in0=before, scalar=order.same[:, bass.ds(first + u, 1)],
                            in1=got[:, b, u, :], op0=ALU.mult, op1=ALU.add).then_inc(scanned, 1)
                        dve.wait_ge(scanned, first + u + 1)

            run_rounds(dve, ROUNDS, round_)
            dve.wait_ge(carried, 1)
            nc.vector.tensor_copy(carry_sb[:, :], carry_ps[:, :]).then_inc(carry_ready, 1)

        @block.tensor
        def _(pe):
            pe.wait_ge(scanned, EDGE_COLS)
            nc.tensor.matmul(carry_ps[:, :], order.carry[:, :], got[:, BUFS - 1, GROUP - 1, :],
                             start=True, stop=True).then_inc(carried, 1)


def update_nodes(nc, cst, name, kind, sums, weights, nodes_of, w, x_sb, h_sb, tables, out=None):
    width = 2 * D if kind == "edge" else D
    with ExitStack() as ctx:
        s = Scope(nc, ctx, name)
        t = Temps(s)
        idx = s.sb("idx", [P, 2, 2, CHUNK], I32)
        sum_sb = s.sb("sum_sb", [P, 2, 2, CHUNK, width], F32)
        pair = s.sb("pair", [P, CHUNK, 2 * D], F32)
        pair_t = s.sb("pair_t", [P, CHUNK, P], F32)
        y = s.sb("y", [P, CHUNK, D], F32)
        degree = s.sb("degree", [P, NODE_COLS], F32)
        to_table = s.sb("to_table", [P, 2, 2, CHUNK, D], F32)
        turned = s.ps("turned", [P, 8, P], F32)
        product = s.ps("product", [P, 8, D], F32)
        idx_ready, summed = s.sem("idx_ready"), [s.sem("summed0"), s.sem("summed1")]
        pair_ready, turned_done, pair_t_ready = s.sem("pair"), s.sem("turned"), s.sem("pair_t")
        product_done, product_taken = s.sem("product"), s.sem("taken")
        var_ready, std_ready, table_ready, stored = s.sem("var"), s.sem("std"), s.sem("table"), s.sem("stored")
        link_sem = s.sem("link")
        block = ctx.enter_context(nc.Block())
        rounds = CHUNK_PAIRS
        wide = [P, CHUNK, D]
        normal = kind in ("edge", "conv2", "directed")
        of_sums = len(sums)

        if sums:
            @block.gpsimd
            def _(pool):
                def round_(j):
                    for b in range(2):
                        pool.wait_ge(idx_ready, j * 2 + b + 1)
                        part_wait(pool)
                        for c in range(CHUNK):
                            for k, (order, state) in enumerate(sums):
                                pool.indirect_dma_start(out=sum_sb[:, b, k, c, :], out_offset=None, in_=state[:, :],
                                                        in_offset=rows(idx[:, b, k, c:c + 1])).then_inc(summed[b], 16)

                run_rounds(pool, rounds, round_)

        @block.sync
        def _(sp):
            if tables:
                def round_(j):
                    for b in range(2):
                        sp.wait_ge(table_ready, j * 2 + b + 1)
                        for k, table in enumerate(tables):
                            sp.dma_start(table.rearrange("(p c) f -> p c f", p=P)[:, bass.ds((j * 2 + b) * CHUNK, CHUNK), :],
                                         to_table[:, b, k, :, :]).then_inc(stored, 16)

                run_rounds(sp, rounds, round_)
                sp.wait_ge(stored, 16 * len(tables) * 2 * rounds)
            if out is not None:
                sp.wait_ge(table_ready, 2 * rounds)
                last_col = NODE_COLS - 1
                sp.dma_start(out[0:last_col * P, :].rearrange("(c p) f -> p c f", p=P), x_sb[:, 0:last_col, :]).then_inc(stored, 16)
                sp.dma_start(out[last_col * P:N, :], x_sb[0:LAST_NODES, last_col, :]).then_inc(stored, 16)
                sp.wait_ge(stored, 32)

        @block.scalar
        def _(act):
            if kind == "first":
                nc.scalar.activation(pair[:, :, D:2 * D], x_sb[:, 0:CHUNK, :], ACT.Copy, scale=0.0)

            def make_pair(j, b):
                chunk = j * 2 + b
                at = bass.ds(chunk * CHUNK, CHUNK)
                if kind == "edge":
                    return
                if sums:
                    act.wait_ge(summed[b], (j + 1) * (16 * CHUNK * of_sums))
                wait_if(act, turned_done, chunk)
                if kind == "directed":
                    for c in range(CHUNK):
                        for k in range(2):
                            last = nc.scalar.activation(pair[:, c, k * D:k * D + D], sum_sb[:, b, k, c, :], ACT.Copy,
                                                        scale=nodes_of[k].inv_root[:, bass.ds(chunk * CHUNK + c, 1)])
                    last.then_inc(pair_ready, 1)
                elif kind == "first":
                    nc.scalar.copy(pair[:, :, 0:D], h_sb[:, at, :]).then_inc(pair_ready, 1)
                else:
                    nc.scalar.copy(pair[:, :, 0:D], h_sb[:, at, :])
                    nc.scalar.copy(pair[:, :, D:2 * D], sum_sb[:, b, 0, :, :]).then_inc(pair_ready, 1)

            make_pair(0, 0)

            def round_(j):
                for b in range(2):
                    chunk = j * 2 + b
                    act.wait_ge(turned_done, chunk + 1)
                    nc.scalar.copy(pair_t[:, :, :], turned[:, 0:CHUNK, :]).then_inc(pair_t_ready, 1)
                    if not (isinstance(j, int) and j == rounds - 1 and b == 1):
                        make_pair(j + b, 1 - b)
                    if normal:
                        act.wait_ge(var_ready, chunk + 1)
                        nc.scalar.activation(t.std[:, :], t.var[:, :], ACT.Sqrt, bias=cst.eps[:, 0:1], scale=1.0 / D).then_inc(std_ready, 1)

            run_rounds(act, rounds, round_)

        @block.tensor
        def _(pe):
            def round_(j):
                for b in range(2):
                    chunk = j * 2 + b
                    pe.wait_ge(pair_ready, chunk + 1)
                    wait_if(pe, pair_t_ready, chunk)
                    for c in range(CHUNK):
                        last = nc.tensor.transpose(turned[:, c, :], pair[:, c, :], cst.ident[:, :])
                    last.then_inc(turned_done, 1)
                    pe.wait_ge(pair_t_ready, chunk + 1)
                    wait_if(pe, product_taken, chunk)
                    for c in range(CHUNK):
                        last = nc.tensor.matmul(product[:, c, :], pair_t[:, c, :], weights[:, :], start=True, stop=True)
                    last.then_inc(product_done, 1)

            run_rounds(pe, rounds, round_)

        @block.vector
        def _(dve):
            link = Link(dve, link_sem)

            def stage_rows(b, at):
                part_wait(dve)
                for k, (order, state) in enumerate(sums):
                    last = nc.vector.tensor_copy(idx[:, b, k, :], nodes_of[order].end_row[:, at])
                last.then_inc(idx_ready, 1)

            if kind == "edge":
                link(nc.vector.tensor_tensor(degree[:, :], nodes_of[0].count[:, :], nodes_of[1].count[:, :], ALU.add))
            if sums:
                for b in range(2):
                    stage_rows(b, slice(b * CHUNK, (b + 1) * CHUNK))

            def chunk_steps(j, b, more):
                chunk = j * 2 + b
                at = bass.ds(chunk * CHUNK, CHUNK)
                if kind == "edge":
                    dve.wait_ge(summed[b], (j + 1) * (16 * CHUNK * 2))
                    wait_if(dve, turned_done, chunk)
                    nc.vector.tensor_tensor(pair[:, :, :], sum_sb[:, b, 0, :, :], sum_sb[:, b, 1, :, :], ALU.add).then_inc(pair_ready, 1)
                dve.wait_ge(pair_ready, chunk + 1)
                if sums and more:
                    stage_rows(b, bass.ds((chunk + 2) * CHUNK, CHUNK))
                by_degree = {"edge": (degree, w.edge_out_bias), "first": (nodes_of[0].count, w.degree_row),
                             "step": (nodes_of[0].count, w.degree_row), "last": (nodes_of[0].count, w.degree_row)}
                if kind in by_degree:
                    count, row = by_degree[kind]
                    link(nc.vector.tensor_tensor(y[:, :, :], row[:, :].unsqueeze(1).to_broadcast(wide),
                                                 count[:, at].unsqueeze(2).to_broadcast(wide), ALU.mult))
                    bias = y[:, :, :]
                else:
                    row = {"conv1": w.conv_bias[0], "conv2": w.conv_bias[1], "directed": w.directed_bias}[kind]
                    bias = row[:, :].unsqueeze(1).to_broadcast(wide)
                dve.wait_ge(product_done, chunk + 1)
                nc.vector.tensor_tensor(y[:, :, :], product[:, 0:CHUNK, :], bias, ALU.add).then_inc(product_taken, 1)
                dve.wait_ge(product_taken, chunk + 1)
                if tables:
                    wait_if(dve, stored, j * (16 * 2 * len(tables)))
                if kind in ("conv1", "first", "step"):
                    ins = nc.vector.tensor_scalar(to_table[:, b, 0, :, :], y[:, :, :], 0.0, None, ALU.max)
                    ins.then_inc(table_ready, 1)
                    dve.wait_ge(table_ready, chunk + 1)
                    if kind == "conv1":
                        part_wait(dve)
                        link(nc.vector.tensor_copy(h_sb[:, at, :], to_table[:, b, 0, :, :]))
                    return
                if kind in ("conv2", "last"):
                    link(nc.vector.tensor_scalar(y[:, :, :], y[:, :, :], 0.0, None, ALU.max))
                ins = nc.vector.tensor_tensor(x_sb[:, at, :], x_sb[:, at, :], y[:, :, :], ALU.add)
                if kind == "last":
                    ins.then_inc(table_ready, 1)
                    dve.wait_ge(table_ready, chunk + 1)
                    return
                link(ins)

                def act_part(ins):
                    ins.then_inc(var_ready, 1)
                    dve.wait_ge(std_ready, chunk + 1)

                normalise(nc, link, act_part, h_sb[:, at, :], x_sb[:, at, :], t)
                if kind == "edge":
                    part_wait(dve)
                    nc.vector.tensor_copy(to_table[:, b, 0, :, :], h_sb[:, at, :]).then_inc(table_ready, 1)
                elif kind == "conv2":
                    for k in range(2):
                        last = nc.vector.tensor_tensor(to_table[:, b, k, :, :], h_sb[:, at, :],
                                                       nodes_of[k].inv_root[:, at].unsqueeze(2).to_broadcast(wide), ALU.mult)
                    last.then_inc(table_ready, 1)

            steps = {"edge": 2 * 8, "conv1": 2, "conv2": 2 * 8, "directed": 2 * 7, "first": 2, "step": 2, "last": 4}[kind]
            link.start_loop()

            def round_(j):
                link.iteration(j, steps)
                for b in range(2):
                    chunk_steps(j, b, not (isinstance(j, int) and j == rounds - 1))

            run_rounds(dve, rounds, round_)
            link.end_loop(rounds, steps)


def graph_layers(nc, x, src, dst, *weights_and_out):
    weights, out = weights_and_out[:-1], weights_and_out[-1]

    def dram(name, shape, dtype=F32):
        return nc.dram_tensor(name, shape, dtype, kind="Internal").ap()

    key_rows = dram("key_rows", [EDGES])
    by_src_edges = dram("by_src_edges", [EDGES, 2], I32)
    source_table, target_table = dram("source_table", [NODES, H]), dram("target_table", [NODES, H])
    tables = [dram("table0", [NODES, D]), dram("table1", [NODES, D])]
    wide_states = [dram(f"wide_state{k}", [EDGES + P, H]) for k in range(2)]
    states = [dram(f"state{k}", [EDGES + P, D]) for k in range(2)]
    fills = [dram(f"fill{k}", [EDGES, H]) for k in range(2)]

    with ExitStack() as ctx:
        s = Scope(nc, ctx, "")
        cst = Constants(s)
        nodes_of = [Nodes(s, side) for side in ("src", "dst")]
        constants(nc, cst)
        with ExitStack() as raw_ctx:
            r = Scope(nc, raw_ctx, "raw_")
            raw = EdgeColumns(r)
            load_edges(nc, cst, raw, src, dst, key_rows)
            count_edges(nc, cst, raw, 0, nodes_of[0])
            place_nodes(nc, cst, "by_src_", nodes_of[0])
            sort_by_src(nc, cst, raw, nodes_of[0], nodes_of[1], key_rows, by_src_edges, fills,
                        [(wide_states[0], H), (wide_states[1], H), (states[0], D), (states[1], D)])
            place_nodes(nc, cst, "by_dst_", nodes_of[1])
        orders = [Order(s, side) for side in ("src", "dst")]
        for order in orders:
            edge_order(nc, cst, order, src, dst, by_src_edges)
        w = Weights(s)
        prepare_weights(nc, cst, w, weights)
        x_sb = s.sb("x_sb", [P, NODE_COLS, D], F32)
        h_sb = s.sb("h_sb", [P, NODE_COLS, D], F32)

        first_layer_tables(nc, cst, w, orders, nodes_of, x, x_sb, source_table, target_table, fills)
        sum_over_edges(nc, cst, "e1_", orders[1], source_table, wide_states[1], H, fills[1])
        sum_over_edges(nc, cst, "e0_", orders[0], source_table, wide_states[0], H, fills[0])
        update_nodes(nc, cst, "ne_", "edge", [(0, wide_states[0]), (1, wide_states[1])], w.edge_out, nodes_of, w,
                     x_sb, h_sb, tables[:1])
        sum_over_edges(nc, cst, "c1_", orders[1], tables[0], states[1], D, None)
        update_nodes(nc, cst, "n1_", "conv1", [(1, states[1])], w.conv[0], nodes_of, w, x_sb, h_sb, tables[:1])
        sum_over_edges(nc, cst, "c2_", orders[1], tables[0], states[1], D, None)
        update_nodes(nc, cst, "n2_", "conv2", [(1, states[1])], w.conv[1], nodes_of, w, x_sb, h_sb, tables)
        sum_over_edges(nc, cst, "d0_", orders[0], tables[1], states[0], D, None)
        sum_over_edges(nc, cst, "d1_", orders[1], tables[0], states[1], D, None)
        update_nodes(nc, cst, "nd_", "directed", [(0, states[0]), (1, states[1])], w.directed, nodes_of, w,
                     x_sb, h_sb, [])
        update_nodes(nc, cst, "s0_", "first", [], w.steps, nodes_of, w, x_sb, h_sb, tables[:1])
        for step in range(1, 4):
            sum_over_edges(nc, cst, f"p{step}_", orders[0], tables[0], states[0], D, None)
            update_nodes(nc, cst, f"s{step}_", "last" if step == 3 else "step", [(0, states[0])], w.steps, nodes_of, w,
                         x_sb, h_sb, [] if step == 3 else tables[:1], out if step == 3 else None)


_INS = ['x', 'src', 'dst', 'L0_gnn_W1', 'L0_gnn_b1', 'L0_gnn_W2', 'L0_gnn_b2', 'L1_gnn_W1_root', 'L1_gnn_W1_rel',
        'L1_gnn_b1', 'L1_gnn_W2_root', 'L1_gnn_W2_rel', 'L1_gnn_b2', 'L2_gnn_W_src', 'L2_gnn_b_src', 'L2_gnn_W_dst',
        'L2_gnn_b_dst', 'L3_gnn_W1', 'L3_gnn_W2', 'L3_gnn_W3', 'L3_gnn_W4']


def kernel(**inputs):
    import numpy as _np
    import concourse.bacc as _bacc
    from concourse import mybir as _mybir
    from concourse.bass_utils import run_bass_kernel_spmd as _run

    nc = _bacc.Bacc("TRN2", target_bir_lowering=False, num_devices=1)
    arrays, args = {}, []
    for name in _INS:
        a = _np.ascontiguousarray(inputs[name])
        arrays[f"in_{name}_dram"] = a
        args.append(nc.dram_tensor(f"in_{name}_dram", a.shape, _mybir.dt.from_np(a.dtype), kind="ExternalInput").ap())
    out = nc.dram_tensor("out_0_dram", (N, D), F32, kind="ExternalOutput").ap()
    graph_layers(nc, *args, out)
    r = _run(nc, [arrays], core_ids=[0])
    return r.results[0]["out_0_dram"]
```

```python
import concourse.bass as bass
from concourse import mybir
from contextlib import ExitStack

F32 = mybir.dt.float32
BF16 = mybir.dt.bfloat16
I32 = mybir.dt.int32
ALU = mybir.AluOpType
ACT = mybir.ActivationFunctionType
AX = mybir.AxisListType

P = 128
N = 12500
D = 64
H = 128
E = 200000
GROUP = 17
BUFS = 4
AHEAD = BUFS - 1
EDGE_COLS = 1564
ROUNDS = EDGE_COLS // (BUFS * GROUP)
EDGES = P * EDGE_COLS
LAST_EDGES = E - (P - 1) * EDGE_COLS
NODE_COLS = (N + P - 1) // P
NODES = P * NODE_COLS
LAST_NODES = N - (NODE_COLS - 1) * P
NO_NODE = P * P - 1
CHUNK = 7
CHUNK_PAIRS = NODE_COLS // (2 * CHUNK)
DIGIT_BITS = 7
TILES = EDGES // P
BLOCKS = (TILES + P - 1) // P
LAST_TILES = TILES - (BLOCKS - 1) * P
LOW_AT, HIGH_AT, TURN_AT = 3, 8, 12
EPS = 1e-5

assert EDGE_COLS == BUFS * GROUP * ROUNDS and EDGES >= E and 0 < LAST_EDGES <= EDGE_COLS
assert NODE_COLS == 2 * CHUNK * CHUNK_PAIRS


class Link:

    def __init__(self, eng, sem):
        self.eng, self.sem, self.before, self.n = eng, sem, 0, 0

    def __call__(self, ins):
        self.n += 1
        ins.then_inc(self.sem, 1)
        self.eng.wait_ge(self.sem, self.before + self.n)

    def start_loop(self):
        self.done, self.n = self.before + self.n, 0

    def iteration(self, i, steps):
        self.before, self.n = self.done + i * steps, 0

    def end_loop(self, rounds, steps):
        assert self.n == steps, (self.n, steps)
        self.before, self.n = self.done + rounds * steps, 0


class Scope:

    def __init__(self, nc, ctx, prefix):
        self.nc, self.ctx, self.prefix, self.sems = nc, ctx, prefix, []

    def sb(self, name, shape, dtype):
        return self.ctx.enter_context(self.nc.sbuf_tensor(self.prefix + name, shape, dtype))

    def ps(self, name, shape, dtype):
        return self.ctx.enter_context(self.nc.psum_tensor(self.prefix + name, shape, dtype))

    def sem(self, name):
        if not self.sems:
            self.ctx.callback(self.clear)
        self.sems.append(self.nc.alloc_semaphore(self.prefix + name))
        return self.sems[-1]

    def clear(self):
        self.nc.clear_and_free_semaphores(self.sems)
        self.nc.all_engine_barrier()


def part_wait(eng):
    eng.nop(nofuse=True)


def wait_if(eng, sem, value):
    if not (isinstance(value, int) and value <= 0):
        eng.wait_ge(sem, value)


def run_rounds(eng, rounds, body):
    body(0)
    with eng.Fori(1, rounds - 1) as i:
        body(i)
    body(rounds - 1)


def rows(ap):
    return bass.IndirectOffsetOnAxis(ap=ap, axis=0)


class Constants:
    def __init__(self, s):
        self.row = s.sb("row", [P, P], F32)
        self.row_b = s.sb("row_b", [P, P], BF16)
        self.part = s.sb("part", [P, 1], F32)
        self.part_start = s.sb("part_start", [P, 1], F32)
        self.ident = s.sb("ident", [P, P], F32)
        self.ident_b = s.sb("ident_b", [P, P], BF16)
        self.up_to = s.sb("up_to", [P, P], F32)
        self.before = s.sb("before", [P, P], F32)
        self.after = s.sb("after", [P, P], F32)
        self.ones = s.sb("ones", [P, P], F32)
        self.eps = s.sb("eps", [P, 1], F32)


class Nodes:

    def __init__(self, s, side):
        self.count = s.sb(f"count_{side}", [P, NODE_COLS], F32)
        self.start = s.sb(f"start_{side}", [P, NODE_COLS], F32)
        self.inv_root = s.sb(f"inv_root_{side}", [P, NODE_COLS], F32)
        self.start_row = s.sb(f"start_row_{side}", [P, NODE_COLS], I32)
        self.end_row = s.sb(f"end_row_{side}", [P, NODE_COLS], I32)


class EdgeColumns:

    def __init__(self, s, other_low, other_high):
        self.key_col = s.sb("key_col", [P, TILES], F32)
        self.payload = s.sb("payload", [P, TILES, 2], I32)
        self.low = [s.sb("low", [P, TILES], BF16), other_low]
        self.high = [s.sb("high", [P, TILES], BF16), other_high]


class Order:

    def __init__(self, s, side):
        self.name = side
        self.gather_rows = s.sb(f"gather_rows_{side}", [P, EDGE_COLS], I32)
        self.same = s.sb(f"same_{side}", [P, EDGE_COLS], F32)
        self.first_row = s.sb(f"first_row_{side}", [P, 1], I32)
        self.first_end = s.sb(f"first_end_{side}", [P, 1], I32)
        self.carry = s.sb(f"carry_{side}", [P, P], F32)


class Weights:
    def __init__(self, s):
        self.edge_in = s.sb("edge_in", [D, 2 * H], F32)
        self.edge_out = s.sb("edge_out", [H, D], F32)
        self.directed = s.sb("directed", [2 * D, D], F32)
        self.edge_bias = s.sb("edge_bias", [P, H], F32)
        self.edge_out_bias = s.sb("edge_out_bias", [P, D], F32)
        self.conv_bias = [s.sb(f"conv_bias{k}", [P, D], F32) for k in range(2)]
        self.directed_bias = s.sb("directed_bias", [P, D], F32)
        self.conv = [s.sb(f"conv{k}", [2 * D, D], F32) for k in range(2)]
        self.steps = s.sb("steps", [2 * D, D], F32)
        self.degree_row = s.sb("degree_row", [P, D], F32)


def constants(nc, cst):
    with ExitStack() as ctx:
        s = Scope(nc, ctx, "cst_")
        row_i = s.sb("row_i", [P, P], I32)
        part_i = s.sb("part_i", [P, 1], I32)
        pos_i = s.sb("pos_i", [P, 1], I32)
        iota_done, link_sem = s.sem("iota_done"), s.sem("link")
        block = ctx.enter_context(nc.Block())

        @block.gpsimd
        def _(pool):
            pool.iota(row_i[:, :], pattern=[[1, P]], base=0, channel_multiplier=0).then_inc(iota_done, 1)
            pool.iota(part_i[:, :], pattern=[[0, 1]], base=0, channel_multiplier=1).then_inc(iota_done, 1)
            pool.iota(pos_i[:, :], pattern=[[0, 1]], base=0, channel_multiplier=EDGE_COLS).then_inc(iota_done, 1)

        @block.vector
        def _(dve):
            link = Link(dve, link_sem)
            dve.wait_ge(iota_done, 3)
            nc.vector.tensor_copy(cst.row[:, :], row_i[:, :])
            nc.vector.tensor_copy(cst.row_b[:, :], row_i[:, :])
            nc.vector.tensor_copy(cst.part_start[:, :], pos_i[:, :])
            link(nc.vector.tensor_copy(cst.part[:, :], part_i[:, :]))
            nc.vector.tensor_scalar(cst.ident[:, :], cst.row[:, :], cst.part[:, 0:1], None, ALU.is_equal)
            nc.vector.tensor_scalar(cst.ident_b[:, :], cst.row[:, :], cst.part[:, 0:1], None, ALU.is_equal)
            nc.vector.tensor_scalar(cst.up_to[:, :], cst.row[:, :], cst.part[:, 0:1], None, ALU.is_ge)
            nc.vector.tensor_scalar(cst.before[:, :], cst.row[:, :], cst.part[:, 0:1], None, ALU.is_gt)
            nc.vector.tensor_scalar(cst.after[:, :], cst.row[:, :], cst.part[:, 0:1], None, ALU.is_lt)
            nc.vector.memset(cst.eps[:, :], EPS)
            link(nc.vector.memset(cst.ones[:, :], 1.0))


def load_edges(nc, cst, name, raw, keys, others, key_rows):
    with ExitStack() as ctx:
        s = Scope(nc, ctx, name)
        tiles_i = [s.sb(f"tiles_i{k}", [P, BLOCKS, P], I32) for k in range(2)]
        tiles_f = [s.sb(f"tiles_f{k}", [P, BLOCKS, P], F32) for k in range(2)]
        col_i = s.sb("col_i", [P, TILES], I32)
        digit_i = s.sb("digit_i", [P, TILES], I32)
        table_row = s.sb("table_row", [P, TILES], F32)
        turned = s.ps("turned", [P, BLOCKS, P], F32)
        padded, loaded, converted = s.sem("padded"), s.sem("loaded"), s.sem("converted")
        turned_done, read_done, rows_stored, link_sem = s.sem("turned"), s.sem("read"), s.sem("stored"), s.sem("link")
        full = (E // P) // P * P * P
        whole_tiles = (E - full) // P
        rest = E - full - whole_tiles * P
        block = ctx.enter_context(nc.Block())

        def load(eng, k, edges):
            eng.wait_ge(padded, 2)
            eng.dma_start(tiles_i[k][:, 0:BLOCKS - 1, :],
                          edges[0:full].rearrange("(b g p) -> g b p", b=BLOCKS - 1, p=P)).then_inc(loaded, 16)
            eng.dma_start(tiles_i[k][0:whole_tiles, BLOCKS - 1, :],
                          edges[full:full + whole_tiles * P].rearrange("(g p) -> g p", p=P)).then_inc(loaded, 16)
            eng.dma_start(tiles_i[k][whole_tiles:whole_tiles + 1, BLOCKS - 1, 0:rest],
                          edges[full + whole_tiles * P:E].rearrange("(a p) -> a p", a=1)).then_inc(loaded, 16)

        @block.scalar
        def _(act):
            load(act, 1, others)

        @block.gpsimd
        def _(pool):
            for k in range(2):
                pool.memset(tiles_i[k][:, BLOCKS - 1, :], NO_NODE).then_inc(padded, 1)

        @block.sync
        def _(sp):
            load(sp, 0, keys)
            sp.wait_ge(converted, 2)
            sp.dma_start(key_rows[0:(BLOCKS - 1) * P * P].rearrange("(b g p) -> g b p", b=BLOCKS - 1, p=P),
                         tiles_f[0][:, 0:BLOCKS - 1, :]).then_inc(rows_stored, 16)
            sp.dma_start(key_rows[(BLOCKS - 1) * P * P:EDGES].rearrange("(g p) -> g p", p=P),
                         tiles_f[0][0:LAST_TILES, BLOCKS - 1, :]).then_inc(rows_stored, 16)
            sp.wait_ge(rows_stored, 32)

        @block.tensor
        def _(pe):
            for k in range(2):
                pe.wait_ge(converted, 2)
                if k == 1:
                    pe.wait_ge(read_done, 1)
                for b in range(BLOCKS):
                    g = P if b < BLOCKS - 1 else LAST_TILES
                    last = nc.tensor.transpose(turned[:, b, 0:g], tiles_f[k][0:g, b, :], cst.ident[0:g, 0:g])
                last.then_inc(turned_done, 1)

        @block.vector
        def _(dve):
            link = Link(dve, link_sem)
            dve.wait_ge(loaded, 96)
            for k in range(2):
                nc.vector.tensor_copy(tiles_f[k][:, :, :], tiles_i[k][:, :, :]).then_inc(converted, 1)
            flat = turned[:, :, :].rearrange("p b g -> p (b g)")[:, 0:TILES]
            for k in range(2):
                dve.wait_ge(turned_done, k + 1)
                if k == 0:
                    nc.vector.tensor_copy(raw.key_col[:, :], flat)
                nc.vector.tensor_copy(col_i[:, :], flat).then_inc(read_done, 1)
                dve.wait_ge(read_done, k + 1)
                if k == 0:
                    nc.vector.tensor_copy(raw.payload[:, :, 0], col_i[:, :])
                for digit, op, by in ((raw.low[k], ALU.bitwise_and, P - 1),
                                      (raw.high[k], ALU.logical_shift_right, DIGIT_BITS)):
                    link(nc.vector.tensor_scalar(digit_i[:, :], col_i[:, :], by, None, op))
                    link(nc.vector.tensor_copy(digit[:, :], digit_i[:, :]))
            link(nc.vector.scalar_tensor_tensor(out=table_row[:, :], in0=raw.low[1][:, :], scalar=float(NODE_COLS),
                                                in1=raw.high[1][:, :], op0=ALU.mult, op1=ALU.add))
            link(nc.vector.tensor_scalar(raw.payload[:, :, 1], table_row[:, :], float(NODES - 1), None, ALU.min))


def one_hot(nc, cst, out, digit, width):
    shape = [P, GROUP, width]
    return nc.vector.tensor_tensor(out, cst.row_b[:, 0:width].unsqueeze(1).to_broadcast(shape),
                             digit.unsqueeze(2).to_broadcast(shape), ALU.is_equal)


def count_edges(nc, cst, low, high, o):
    with ExitStack() as ctx:
        s = Scope(nc, ctx, "cnt_")
        one_low = s.sb("one_low", [P, 2, GROUP, P], BF16)
        one_high = s.sb("one_high", [P, 2, GROUP, NODE_COLS], BF16)
        zero_b = s.sb("zero_b", [P, P], BF16)
        counted = s.ps("counted", [P, NODE_COLS], F32)
        hot_ready, hot_free, zeroed, sums_done = s.sem("hot_ready"), s.sem("hot_free"), s.sem("zeroed"), s.sem("sums")
        block = ctx.enter_context(nc.Block())
        rounds = TILES // (2 * GROUP)

        @block.vector
        def _(dve):
            nc.vector.memset(zero_b[:, :], 0.0).then_inc(zeroed, 1)

            def round_(i):
                for b in range(2):
                    wait_if(dve, hot_free, i * 2 + b - 1)
                    at = bass.ds((i * 2 + b) * GROUP, GROUP)
                    one_hot(nc, cst, one_low[:, b, :, :], low[:, at], P)
                    one_hot(nc, cst, one_high[:, b, :, :], high[:, at], NODE_COLS).then_inc(hot_ready, 1)

            run_rounds(dve, rounds, round_)
            dve.wait_ge(sums_done, 1)
            nc.vector.tensor_copy(o.count[:, :], counted[:, :])

        @block.tensor
        def _(pe):
            pe.wait_ge(zeroed, 1)
            nc.tensor.matmul(counted[:, :], zero_b[:, :], zero_b[:, 0:NODE_COLS], start=True, stop=False)

            def round_(i):
                for b in range(2):
                    pe.wait_ge(hot_ready, i * 2 + b + 1)
                    for u in range(GROUP):
                        last = nc.tensor.matmul(counted[:, :], one_low[:, b, u, :], one_high[:, b, u, :],
                                                start=False, stop=False)
                    last.then_inc(hot_free, 1)

            run_rounds(pe, rounds, round_)
            nc.tensor.matmul(counted[:, :], zero_b[:, :], zero_b[:, 0:NODE_COLS], start=False, stop=True).then_inc(sums_done, 1)


def place_nodes(nc, cst, name, o):
    with ExitStack() as ctx:
        s = Scope(nc, ctx, name)
        total = s.sb("total", [P, NODE_COLS], F32)
        col_end = s.sb("col_end", [P, NODE_COLS], F32)
        has = s.sb("has", [P, NODE_COLS], F32)
        work = s.sb("work", [P, NODE_COLS], F32)
        root = s.sb("root", [P, NODE_COLS], F32)
        within = s.ps("within", [P, NODE_COLS], F32)
        totals = s.ps("totals", [P, NODE_COLS], F32)
        degree_ready, root_done, prefix_done, link_sem = s.sem("degree"), s.sem("root"), s.sem("prefix"), s.sem("link")
        block = ctx.enter_context(nc.Block())

        @block.tensor
        def _(pe):
            nc.tensor.matmul(within[:, :], cst.up_to[:, :], o.count[:, :], start=True, stop=True)
            nc.tensor.matmul(totals[:, :], cst.ones[:, :], o.count[:, :], start=True, stop=True).then_inc(prefix_done, 1)

        @block.scalar
        def _(act):
            act.wait_ge(degree_ready, 1)
            nc.scalar.activation(root[:, :], o.inv_root[:, :], ACT.Sqrt).then_inc(root_done, 1)

        @block.vector
        def _(dve):
            link = Link(dve, link_sem)
            nc.vector.tensor_scalar(o.inv_root[:, :], o.count[:, :], 1.0, None, ALU.max).then_inc(degree_ready, 1)
            link(nc.vector.tensor_scalar(has[:, :], o.count[:, :], 0.0, None, ALU.is_gt))
            dve.wait_ge(prefix_done, 1)
            link(nc.vector.tensor_copy(total[:, :], totals[:, :]))
            link(nc.vector.tensor_tensor_scan(out=col_end[:, :], data0=cst.ones[:, 0:NODE_COLS], data1=total[:, :],
                                              initial=0.0, op0=ALU.mult, op1=ALU.add))
            link(nc.vector.tensor_tensor(col_end[:, :], col_end[:, :], total[:, :], ALU.subtract))
            link(nc.vector.tensor_tensor(work[:, :], col_end[:, :], within[:, :], ALU.add))
            link(nc.vector.tensor_tensor(o.start[:, :], work[:, :], o.count[:, :], ALU.subtract))
            link(nc.vector.tensor_scalar(work[:, :], work[:, :], -1.0 - EDGES, None, ALU.add))
            link(nc.vector.tensor_tensor(work[:, :], work[:, :], has[:, :], ALU.mult))
            link(nc.vector.tensor_scalar(o.end_row[:, :], work[:, :], float(EDGES), None, ALU.add))
            link(nc.vector.tensor_scalar(work[:, :], o.start[:, :], -float(EDGES), None, ALU.add))
            link(nc.vector.tensor_tensor(work[:, :], work[:, :], has[:, :], ALU.mult))
            link(nc.vector.tensor_scalar(o.start_row[:, :], work[:, :], float(EDGES), None, ALU.add))
            dve.wait_ge(root_done, 1)
            link(nc.vector.reciprocal(o.inv_root[:, :], root[:, :]))
            link(nc.vector.tensor_tensor(o.inv_root[:, :], o.inv_root[:, :], has[:, :], ALU.mult))


def sort_edges(nc, cst, name, raw, nodes, key_rows, sorted_edges, fills=(), states=()):
    with ExitStack() as ctx:
        s = Scope(nc, ctx, name)
        keys = s.sb("keys", [P, 2, GROUP, P], F32)
        one_low = s.sb("one_low", [P, 2, GROUP, P], BF16)
        one_high = s.sb("one_high", [P, 2, GROUP, NODE_COLS], BF16)
        low_t = s.sb("low_t", [P, 2, GROUP, P], F32)
        place = s.sb("place", [P, 2, NODE_COLS], F32)
        same = s.sb("same", [P, 2, P], F32)
        picked = s.sb("picked", [P, 2, NODE_COLS], F32)
        base = s.sb("base", [P, 2, GROUP], F32)
        rank = s.sb("rank", [P, 2, GROUP], F32)
        target = s.sb("target", [P, 2, GROUP], I32)
        payload = s.sb("payload", [P, 2, GROUP, 2], I32)
        pad_place = s.sb("pad_place", [P, TILES], F32)
        place_i = s.sb("place_i", [P, TILES], I32)
        zeros = s.sb("zeros", [P, GROUP * H], F32)
        table = s.ps("table", [P, 512], F32)[:, 0:NODE_COLS]
        read = s.ps("read", [P, 2, 512], F32)
        turned = s.ps("turned", [P, 24, P], BF16)
        iota_done, keys_in = s.sem("iota_done"), [s.sem("keys_in0"), s.sem("keys_in1")]
        keys_free, hot_ready, hot_free = s.sem("keys_free"), s.sem("hot_ready"), s.sem("hot_free")
        turned_done, low_t_ready, table_ready = s.sem("turned"), s.sem("low_t_ready"), s.sem("table")
        read_done, read_free, table_counted = s.sem("read"), s.sem("read_free"), s.sem("table_counted")
        target_ready, link_sem = s.sem("target"), s.sem("link")
        scattered = [s.sem("scattered0"), s.sem("scattered1")]
        zeroed, filled = s.sem("zeroed"), s.sem("filled")
        rounds = TILES // (2 * GROUP)
        block = ctx.enter_context(nc.Block())

        @block.sync
        def _(sp):
            flat = key_rows.rearrange("(a e) -> a e", a=1)
            sp.wait_ge(zeroed, 1)

            def round_(i):
                for b in range(2):
                    wait_if(sp, keys_free, i * 2 + b - 1)
                    piece = flat[:, bass.ds((i * 2 + b) * (GROUP * P), GROUP * P)]
                    sp.dma_start(keys[:, b, :, :].rearrange("p g e -> p (g e)"),
                                 piece.to_broadcast([P, GROUP * P])).then_inc(keys_in[b], 16)
                    for fill in fills:
                        view = fill[0:EDGES, :].rearrange("(p t) f -> p (t f)", p=P)
                        sp.dma_start(view[:, bass.ds((i * 2 + b) * (GROUP * H), GROUP * H)],
                                     zeros[:, :]).then_inc(filled, 16)

            run_rounds(sp, rounds, round_)
            for state, width in states:
                sp.dma_start(state[EDGES:EDGES + P, :], zeros[:, 0:width]).then_inc(filled, 16)
            wait_if(sp, filled, 16 * (len(fills) * rounds * 2 + len(states)))

        @block.gpsimd
        def _(pool):
            pool.memset(zeros[:, :], 0.0).then_inc(zeroed, 1)
            pool.iota(place_i[:, :], pattern=[[P, TILES]], base=0, channel_multiplier=0).then_inc(iota_done, 1)

            def round_(i):
                for b in range(2):
                    pool.wait_ge(target_ready, i * 2 + b + 1)
                    part_wait(pool)
                    for u in range(GROUP):
                        pool.indirect_dma_start(out=sorted_edges[:, :], out_offset=rows(target[:, b, u:u + 1]),
                                                in_=payload[:, b, u, :], in_offset=None).then_inc(scattered[b], 16)

            run_rounds(pool, rounds, round_)
            for b in range(2):
                pool.wait_ge(scattered[b], 16 * GROUP * rounds)

        @block.vector
        def _(dve):
            link = Link(dve, link_sem)
            dve.wait_ge(iota_done, 1)
            link(nc.vector.tensor_scalar(pad_place[:, :], raw.key_col[:, :], float(NO_NODE), None, ALU.is_equal))
            link(nc.vector.scalar_tensor_tensor(out=pad_place[:, :], in0=place_i[:, :], scalar=float(E),
                                                in1=pad_place[:, :], op0=ALU.max, op1=ALU.mult))

            def hot_low(group, b):
                one_hot(nc, cst, one_low[:, b, :, :], raw.low[0][:, bass.ds(group * GROUP, GROUP)], P)

            def hot_high(group, b):
                one_hot(nc, cst, one_high[:, b, :, :], raw.high[0][:, bass.ds(group * GROUP, GROUP)],
                        NODE_COLS).then_inc(hot_ready, 1)

            hot_low(0, 0)
            hot_high(0, 0)
            dve.wait_ge(hot_ready, 1)
            link.start_loop()
            steps = 2

            def round_(i):
                link.iteration(i, steps)
                for b in range(2):
                    group = i * 2 + b
                    at = bass.ds(group * GROUP, GROUP)
                    next_group = not (isinstance(i, int) and i == rounds - 1 and b == 1)
                    dve.wait_ge(keys_in[b], 16 * (i + 1))
                    for u in range(GROUP):
                        t = group * GROUP + u
                        v = (b * GROUP + u) % 2
                        wait_if(dve, read_free, t - 1)
                        compared = nc.vector.scalar_tensor_tensor(
                            out=same[:, v, :], in0=keys[:, b, u, :], scalar=raw.key_col[:, bass.ds(t, 1)],
                            in1=cst.after[:, :], op0=ALU.is_equal, op1=ALU.mult, accum_out=rank[:, b, u:u + 1])
                        if u == GROUP - 1:
                            compared.then_inc(keys_free, 1)
                        dve.wait_ge(read_done, t + 1)
                        nc.vector.scalar_tensor_tensor(
                            out=picked[:, v, :], in0=one_high[:, b, u, :], scalar=1.0,
                            in1=read[:, v, 0:NODE_COLS], op0=ALU.mult, op1=ALU.mult,
                            accum_out=base[:, b, u:u + 1]).then_inc(read_free, 1)
                        if next_group and u == LOW_AT:
                            wait_if(dve, hot_free, group)
                            hot_low(group + 1, 1 - b)
                        if next_group and u == HIGH_AT:
                            hot_high(group + 1, 1 - b)
                    dve.wait_ge(read_free, (group + 1) * GROUP)
                    link(nc.vector.tensor_tensor(rank[:, b, :], rank[:, b, :], pad_place[:, at], ALU.add))
                    wait_if(dve, scattered[b], i * (16 * GROUP))
                    part_wait(dve)
                    nc.vector.tensor_copy(payload[:, b, :, :], raw.payload[:, at, :])
                    nc.vector.tensor_tensor(target[:, b, :], rank[:, b, :], base[:, b, :], ALU.add).then_inc(target_ready, 1)
                    dve.wait_ge(target_ready, group + 1)

            run_rounds(dve, rounds, round_)

        @block.scalar
        def _(act):
            nc.scalar.copy(place[:, 0, :], nodes.start[:, :]).then_inc(table_ready, 1)
            act.wait_ge(turned_done, 1)
            nc.scalar.copy(low_t[:, 0, :, :], turned[:, 0:GROUP, :]).then_inc(low_t_ready, 1)

            def round_(i):
                for b in range(2):
                    group = i * 2 + b
                    for u in range(GROUP):
                        v = b * GROUP + u
                        act.wait_ge(table_counted, group * GROUP + u + 1)
                        nc.scalar.copy(place[:, (v + 1) % 2, :], table).then_inc(table_ready, 1)
                        if u == TURN_AT and not (isinstance(i, int) and i == rounds - 1 and b == 1):
                            act.wait_ge(turned_done, group + 2)
                            nc.scalar.copy(low_t[:, 1 - b, :, :], turned[:, 0:GROUP, :]).then_inc(low_t_ready, 1)

            run_rounds(act, rounds, round_)

        @block.tensor
        def _(pe):
            def turn(b):
                for u in range(GROUP):
                    last = nc.tensor.transpose(turned[:, u, :], one_low[:, b, u, :], cst.ident_b[:, :])
                last.then_inc(turned_done, 1)

            nc.tensor.matmul(table, cst.ident[:, :], nodes.start[:, :], start=True, stop=True)
            pe.wait_ge(hot_ready, 1)
            turn(0)

            def round_(i):
                for b in range(2):
                    group = i * 2 + b
                    pe.wait_ge(low_t_ready, group + 1)
                    for u in range(GROUP):
                        v = b * GROUP + u
                        t = group * GROUP + u
                        pe.wait_ge(table_ready, t + 1)
                        nc.tensor.matmul(table, one_low[:, b, u, :], one_high[:, b, u, :], start=False, stop=True,
                                         skip_group_check=True).then_inc(table_counted, 1)
                        wait_if(pe, read_free, t - 1)
                        nc.tensor.matmul(read[:, v % 2, 0:NODE_COLS], low_t[:, b, u, :], place[:, v % 2, :],
                                         start=True, stop=True).then_inc(read_done, 1)
                        if u == GROUP - 1:
                            pe.wait_ge(table_counted, t + 1)
                            pe.sem_inc(hot_free, 1)
                        if u == TURN_AT and not (isinstance(i, int) and i == rounds - 1 and b == 1):
                            pe.wait_ge(hot_ready, group + 2)
                            turn(1 - b)

            run_rounds(pe, rounds, round_)


def edge_order(nc, cst, name, order, keys=None, others=None, sorted_edges=None, unsorted=None):
    from_sort = sorted_edges is not None
    with ExitStack() as ctx:
        s = Scope(nc, ctx, name)
        pairs = s.sb("pairs", [P, EDGE_COLS, 2], I32) if from_sort else None
        key_i = s.sb("key_i", [P, EDGE_COLS], I32)
        other_i = s.sb("other_i", [P, EDGE_COLS], I32)
        key = s.sb("key", [P, EDGE_COLS], F32)
        work = s.sb("work", [P, EDGE_COLS], F32)
        digit_i = s.sb("digit_i", [P, EDGE_COLS], I32)
        high = s.sb("high", [P, EDGE_COLS], F32)
        first_of = s.sb("first_of", [P, P], F32)
        run = s.sb("run", [P, 1], F32)
        drops = s.sb("drops", [P, 2], F32)
        first_rows = s.ps("first_rows", [P, 512], F32)[:, 0:P]
        all_drops = s.ps("all_drops", [P, 512], F32)[:, 0:1]
        drops_ready, drops_summed = s.sem("drops"), s.sem("drops_summed")
        padded, loaded, firsts_ready, firsts_turned, link_sem = (
            s.sem("padded"), s.sem("loaded"), s.sem("firsts"), s.sem("turned"), s.sem("link"))
        block = ctx.enter_context(nc.Block())

        @block.gpsimd
        def _(pool):
            if not from_sort:
                pool.memset(key_i[:, :], NO_NODE).then_inc(padded, 1)
                pool.memset(other_i[:, :], NO_NODE).then_inc(padded, 1)

        @block.sync
        def _(sp):
            if from_sort:
                sp.dma_start(pairs[:, :, :].rearrange("p t a -> p (t a)"),
                             sorted_edges.rearrange("(p t) a -> p (t a)", p=P)).then_inc(loaded, 16)
                return
            sp.wait_ge(padded, 2)
            cut = (P - 1) * EDGE_COLS
            for ends, at in ((keys, key_i), (others, other_i)):
                sp.dma_start(at[0:P - 1, :], ends[0:cut].rearrange("(p t) -> p t", p=P - 1)).then_inc(loaded, 16)
                sp.dma_start(at[P - 1:P, 0:LAST_EDGES],
                             ends[cut:E].rearrange("(a t) -> a t", a=1)).then_inc(loaded, 16)

        @block.vector
        def _(dve):
            link = Link(dve, link_sem)

            def table_rows(out, node_i, n):
                link(nc.vector.tensor_scalar(digit_i[:, 0:n], node_i, P - 1, None, ALU.bitwise_and))
                link(nc.vector.tensor_copy(work[:, 0:n], digit_i[:, 0:n]))
                link(nc.vector.tensor_scalar(digit_i[:, 0:n], node_i, DIGIT_BITS, None, ALU.logical_shift_right))
                link(nc.vector.tensor_copy(high[:, 0:n], digit_i[:, 0:n]))
                link(nc.vector.scalar_tensor_tensor(out=work[:, 0:n], in0=work[:, 0:n], scalar=float(NODE_COLS),
                                                    in1=high[:, 0:n], op0=ALU.mult, op1=ALU.add))
                link(nc.vector.tensor_scalar(out, work[:, 0:n], float(NODES - 1), None, ALU.min))

            dve.wait_ge(loaded, 16 if from_sort else 64)
            if from_sort:
                link(nc.vector.tensor_copy(key_i[:, :], pairs[:, :, 0]))
                link(nc.vector.tensor_copy(order.gather_rows[:, :], pairs[:, :, 1]))
            else:
                table_rows(order.gather_rows[:, :], other_i[:, :], EDGE_COLS)
            link(nc.vector.tensor_copy(key[:, :], key_i[:, :]))
            table_rows(order.first_row[:, :], key_i[:, 0:1], 1)
            link(nc.vector.memset(order.same[:, 0:1], 0.0))
            link(nc.vector.tensor_tensor(order.same[:, 1:EDGE_COLS], key[:, 1:EDGE_COLS], key[:, 0:EDGE_COLS - 1],
                                         ALU.is_equal))
            link(nc.vector.tensor_scalar(work[:, :], key[:, :], key[:, 0:1], None, ALU.is_equal))
            link(nc.vector.reduce_sum(run[:, :], work[:, :], AX.X))
            link(nc.vector.tensor_scalar(run[:, :], run[:, :], -1.0, None, ALU.add))
            link(nc.vector.tensor_tensor(order.first_end[:, :], run[:, :], cst.part_start[:, :], ALU.add))
            last_key = key[:, EDGE_COLS - 1:EDGE_COLS]
            nc.vector.tensor_copy(first_of[:, :], key[:, 0:1].to_broadcast([P, P])).then_inc(firsts_ready, 1)
            dve.wait_ge(firsts_turned, 1)
            link(nc.vector.scalar_tensor_tensor(out=order.carry[:, :], in0=first_rows, scalar=last_key,
                                                in1=cst.before[:, :], op0=ALU.is_equal, op1=ALU.mult))
            if unsorted is None:
                return
            link(nc.vector.tensor_tensor(work[:, 1:EDGE_COLS], key[:, 1:EDGE_COLS], key[:, 0:EDGE_COLS - 1], ALU.is_lt))
            link(nc.vector.reduce_sum(drops[:, 0:1], work[:, 1:EDGE_COLS], AX.X))
            link(nc.vector.scalar_tensor_tensor(out=first_of[:, :], in0=first_rows, scalar=last_key,
                                                in1=cst.before[:, :], op0=ALU.is_lt, op1=ALU.mult))
            link(nc.vector.reduce_sum(drops[:, 1:2], first_of[:, :], AX.X))
            nc.vector.tensor_tensor(drops[:, 0:1], drops[:, 0:1], drops[:, 1:2], ALU.add).then_inc(drops_ready, 1)
            dve.wait_ge(drops_summed, 1)
            link(nc.vector.tensor_copy(unsorted[:, :], all_drops))

        @block.tensor
        def _(pe):
            pe.wait_ge(firsts_ready, 1)
            nc.tensor.matmul(first_rows, first_of[:, :], cst.ident[:, :], start=True, stop=True).then_inc(firsts_turned, 1)
            if unsorted is not None:
                pe.wait_ge(drops_ready, 1)
                nc.tensor.matmul(all_drops, cst.ones[:, :], drops[:, 0:1], start=True, stop=True).then_inc(drops_summed, 1)


def prepare_weights(nc, cst, w, args):
    (W1, b1, W2, b2, W1_root, W1_rel, g_b1, W2_root, W2_rel, g_b2, W_src, b_src, W_dst, b_dst,
     s_W1, s_W2, s_W3, s_W4) = args
    with ExitStack() as ctx:
        s = Scope(nc, ctx, "w_")
        sides = [s.sb(f"side{n}", [D, 2 * D], F32) for n in range(4)]
        bias2 = s.sb("bias2", [P, 2, D], F32)
        w4 = s.sb("w4", [D, 1], F32)
        w4_wide = s.sb("w4_wide", [D, P], F32)
        w3_t = s.sb("w3_t", [P, D], F32)
        turned = s.ps("turned", [P, 4, P], F32)
        v_ps = s.ps("v_ps", [P, D], F32)
        loaded, turned_done, w3_ready, v_done, link_sem = (
            s.sem("loaded"), s.sem("turned"), s.sem("w3"), s.sem("v"), s.sem("link"))
        block = ctx.enter_context(nc.Block())
        pairs = ((W1_root, W1_rel), (W2_root, W2_rel), (s_W1, s_W2), (s_W3, s_W3))
        loads = []
        for side, two in zip(sides, pairs):
            loads += [(side[:, 0:D], two[0]), (side[:, D:2 * D], two[1])]
        loads += [(w.edge_in[:, 0:H], W1[0:D, :]), (w.edge_in[:, H:2 * H], W1[D:2 * D, :]), (w.edge_out[:, :], W2),
                  (w.directed[0:D, :], W_src), (w.directed[D:2 * D, :], W_dst), (w4[:, :], s_W4)]

        def wide(v, n):
            return v.rearrange("(a n) -> a n", a=1).to_broadcast([P, n])

        loads += [(w.edge_bias[:, :], wide(b1, H)), (w.edge_out_bias[:, :], wide(b2, D)),
                  (w.conv_bias[0][:, :], wide(g_b1, D)), (w.conv_bias[1][:, :], wide(g_b2, D)),
                  (bias2[:, 0, :], wide(b_src, D)), (bias2[:, 1, :], wide(b_dst, D))]

        @block.sync
        def _(sp):
            for to, of in loads:
                sp.dma_start(to, of).then_inc(loaded, 16)

        @block.tensor
        def _(pe):
            pe.wait_ge(loaded, 16 * len(loads))
            for n in range(4):
                last = nc.tensor.transpose(turned[:, n, 0:D], sides[n][:, :], cst.ident[0:D, 0:D])
            last.then_inc(turned_done, 1)
            pe.wait_ge(w3_ready, 1)
            nc.tensor.matmul(v_ps[:, :], w4_wide[:, :], w3_t[0:D, :], start=True, stop=True).then_inc(v_done, 1)

        @block.vector
        def _(dve):
            link = Link(dve, link_sem)
            dve.wait_ge(loaded, 16 * len(loads))
            link(nc.vector.tensor_scalar(w.directed[:, :], w.directed[:, :], 0.5, None, ALU.mult))
            link(nc.vector.tensor_scalar(bias2[:, :, :], bias2[:, :, :], 0.5, None, ALU.mult))
            link(nc.vector.tensor_tensor(w.directed_bias[:, :], bias2[:, 0, :], bias2[:, 1, :], ALU.add))
            link(nc.vector.tensor_scalar(w4[:, :], w4[:, :], 0.0, None, ALU.max))
            link(nc.vector.tensor_copy(w4_wide[:, :], w4[:, 0:1].to_broadcast([D, P])))
            dve.wait_ge(turned_done, 1)
            for n, to in enumerate((w.conv[0], w.conv[1], w.steps)):
                nc.vector.tensor_copy(to[:, :], turned[:, n, 0:D])
            nc.vector.tensor_copy(w3_t[:, :], turned[:, 3, 0:D]).then_inc(w3_ready, 1)
            dve.wait_ge(v_done, 1)
            link(nc.vector.tensor_copy(w.degree_row[:, :], v_ps[:, :]))


def normalise(nc, link, act_part, out, x, t):
    wide = [P, CHUNK, D]
    part_wait(link.eng)
    link(nc.vector.reduce_sum(t.mean[:, :], x, AX.X))
    link(nc.vector.tensor_scalar(t.mean[:, :], t.mean[:, :], 1.0 / D, None, ALU.mult))
    link(nc.vector.tensor_tensor(t.centred[:, :, :], x, t.mean[:, :].unsqueeze(2).to_broadcast(wide), ALU.subtract))
    link(nc.vector.tensor_tensor(t.squares[:, :, :], t.centred[:, :, :], t.centred[:, :, :], ALU.mult))
    part_wait(link.eng)
    act_part(nc.vector.reduce_sum(t.var[:, :], t.squares[:, :, :], AX.X))
    link(nc.vector.reciprocal(t.std[:, :], t.std[:, :]))
    link(nc.vector.scalar_tensor_tensor(out=out, in0=t.centred[:, :, :], scalar=0.0,
                                        in1=t.std[:, :].unsqueeze(2).to_broadcast(wide), op0=ALU.max, op1=ALU.mult))


class Temps:
    def __init__(self, s):
        self.mean, self.var, self.std = s.sb("mean", [P, CHUNK], F32), s.sb("var", [P, CHUNK], F32), s.sb("std", [P, CHUNK], F32)
        self.centred, self.squares = s.sb("centred", [P, CHUNK, D], F32), s.sb("squares", [P, CHUNK, D], F32)


def start_partitions(pool, order, target_table, fill, firsts, first_in, first_out):
    pool.indirect_dma_start(out=firsts[:, :], out_offset=None, in_=target_table[:, :],
                            in_offset=rows(order.first_row[:, 0:1])).then_inc(first_in, 16)
    pool.wait_ge(first_in, 16)
    pool.dma_start(fill[0:EDGES, :].rearrange("(p t) f -> p t f", p=P)[:, 0, :], firsts[:, :]).then_inc(first_out, 16)
    pool.wait_ge(first_out, 16)


def fill_starts(nc, cst, order, nodes, target_table, fill):
    with ExitStack() as ctx:
        s = Scope(nc, ctx, "fill_")
        ends = s.sb("ends", [P, NODE_COLS, H], F32)
        starts = s.sb("starts", [P, 2, CHUNK], I32)
        firsts = s.sb("firsts", [P, H], F32)
        starts_ready, loaded, scattered = s.sem("starts"), s.sem("loaded"), [s.sem("scattered0"), s.sem("scattered1")]
        first_in, first_out = s.sem("first_in"), s.sem("first_out")
        block = ctx.enter_context(nc.Block())

        @block.sync
        def _(sp):
            sp.dma_start(ends[:, :, :], target_table.rearrange("(p c) f -> p c f", p=P)).then_inc(loaded, 16)

        @block.vector
        def _(dve):
            def round_(j):
                for b in range(2):
                    wait_if(dve, scattered[b], j * (16 * CHUNK))
                    part_wait(dve)
                    nc.vector.tensor_copy(starts[:, b, :], nodes.start_row[:, bass.ds((j * 2 + b) * CHUNK, CHUNK)]).then_inc(starts_ready, 1)

            run_rounds(dve, CHUNK_PAIRS, round_)

        @block.gpsimd
        def _(pool):
            pool.wait_ge(loaded, 16)
            for chunk in range(NODE_COLS // CHUNK):
                b = chunk % 2
                pool.wait_ge(starts_ready, chunk + 1)
                for c in range(CHUNK):
                    pool.indirect_dma_start(out=fill[:, :], out_offset=rows(starts[:, b, c:c + 1]),
                                            in_=ends[:, chunk * CHUNK + c, :], in_offset=None, bounds_check=EDGES - 1,
                                            oob_is_err=False).then_inc(scattered[b], 16)
            for b in range(2):
                pool.wait_ge(scattered[b], 16 * NODE_COLS // 2)
            start_partitions(pool, order, target_table, fill, firsts, first_in, first_out)


def first_layer_tables(nc, cst, w, order, nodes, x, x_sb, source_table, target_table, fill):
    with ExitStack() as ctx:
        s = Scope(nc, ctx, "tab_")
        t = Temps(s)
        h = s.sb("h", [P, 2, CHUNK, D], F32)
        h_t = s.sb("h_t", [D, CHUNK, P], F32)
        ends = s.sb("ends", [P, 2, CHUNK, 2 * H], F32)
        starts = s.sb("starts", [P, 2, CHUNK], I32)
        firsts = s.sb("firsts", [P, H], F32)
        turned = s.ps("turned", [D, 8, P], F32)
        products = s.ps("products", [P, 8, 2 * H], F32)
        padded, loaded, link_sem = s.sem("padded"), s.sem("loaded"), s.sem("link")
        var_ready, std_ready, h_ready, turned_done = s.sem("var"), s.sem("std"), s.sem("h"), s.sem("turned")
        h_t_ready, products_done, ends_ready = s.sem("h_t"), s.sem("products"), s.sem("ends")
        stored, scattered, first_in, first_out = s.sem("stored"), s.sem("scattered"), s.sem("first_in"), s.sem("first_out")
        block = ctx.enter_context(nc.Block())
        last_col = NODE_COLS - 1

        @block.gpsimd
        def _(pool):
            pool.memset(x_sb[:, last_col, :], 0.0).then_inc(padded, 1)

            def round_(j):
                for b in range(2):
                    pool.wait_ge(ends_ready, j * 2 + b + 1)
                    part_wait(pool)
                    for c in range(CHUNK):
                        pool.indirect_dma_start(out=fill[:, :], out_offset=rows(starts[:, b, c:c + 1]),
                                                in_=ends[:, b, c, 0:H], in_offset=None, bounds_check=EDGES - 1,
                                                oob_is_err=False).then_inc(scattered, 16)

            run_rounds(pool, CHUNK_PAIRS, round_)
            pool.wait_ge(scattered, 16 * NODE_COLS)
            pool.wait_ge(stored, 16 * NODE_COLS // CHUNK * 2)
            start_partitions(pool, order, target_table, fill, firsts, first_in, first_out)

        @block.sync
        def _(sp):
            sp.wait_ge(padded, 1)
            sp.dma_start(x_sb[:, 0:last_col, :], x[0:last_col * P, :].rearrange("(c p) f -> p c f", p=P)).then_inc(loaded, 16)
            sp.dma_start(x_sb[0:LAST_NODES, last_col, :], x[last_col * P:N, :]).then_inc(loaded, 16)

            def round_(j):
                for b in range(2):
                    sp.wait_ge(ends_ready, j * 2 + b + 1)
                    for table, half in ((target_table, 0), (source_table, 1)):
                        sp.dma_start(table.rearrange("(p c) f -> p c f", p=P)[:, bass.ds((j * 2 + b) * CHUNK, CHUNK), :],
                                     ends[:, b, :, half * H:half * H + H]).then_inc(stored, 16)

            run_rounds(sp, CHUNK_PAIRS, round_)
            sp.wait_ge(stored, 16 * NODE_COLS // CHUNK * 2)

        @block.scalar
        def _(act):
            def round_(j):
                for b in range(2):
                    act.wait_ge(var_ready, j * 2 + b + 1)
                    nc.scalar.activation(t.std[:, :], t.var[:, :], ACT.Sqrt, bias=cst.eps[:, 0:1], scale=1.0 / D).then_inc(std_ready, 1)
                    act.wait_ge(turned_done, j * 2 + b + 1)
                    nc.scalar.copy(h_t[:, :, :], turned[:, 0:CHUNK, :]).then_inc(h_t_ready, 1)

            run_rounds(act, CHUNK_PAIRS, round_)

        @block.tensor
        def _(pe):
            def round_(j):
                for b in range(2):
                    pe.wait_ge(h_ready, j * 2 + b + 1)
                    part_wait(pe)
                    for c in range(CHUNK):
                        last = nc.tensor.transpose(turned[:, c, :], h[:, b, c, :], cst.ident[:, :])
                    last.then_inc(turned_done, 1)
                    pe.wait_ge(h_t_ready, j * 2 + b + 1)
                    wait_if(pe, ends_ready, j * 2 + b)
                    for c in range(CHUNK):
                        last = nc.tensor.matmul(products[:, c, :], h_t[:, c, :], w.edge_in[:, :], start=True, stop=True)
                    last.then_inc(products_done, 1)

            run_rounds(pe, CHUNK_PAIRS, round_)

        @block.vector
        def _(dve):
            link = Link(dve, link_sem)
            dve.wait_ge(loaded, 32)
            link.start_loop()
            steps = 2 * 6

            def round_(j):
                link.iteration(j, steps)
                for b in range(2):
                    chunk = j * 2 + b
                    at = bass.ds(chunk * CHUNK, CHUNK)

                    def act_part(ins):
                        ins.then_inc(var_ready, 1)
                        dve.wait_ge(std_ready, chunk + 1)

                    normalise(nc, link, act_part, h[:, b, :, :], x_sb[:, at, :], t)
                    nc.vector.tensor_tensor(x_sb[:, at, :], x_sb[:, at, :], h[:, b, :, :], ALU.add).then_inc(h_ready, 1)
                    dve.wait_ge(products_done, chunk + 1)
                    wait_if(dve, stored, j * (16 * 2 * 2))
                    wait_if(dve, scattered, j * (16 * 2 * CHUNK))
                    part_wait(dve)
                    nc.vector.tensor_copy(ends[:, b, :, 0:H], products[:, 0:CHUNK, 0:H])
                    nc.vector.tensor_copy(starts[:, b, :], nodes.start_row[:, at])
                    nc.vector.tensor_tensor(ends[:, b, :, H:2 * H], products[:, 0:CHUNK, H:2 * H],
                                            w.edge_bias[:, :].unsqueeze(1).to_broadcast([P, CHUNK, H]),
                                            ALU.add).then_inc(ends_ready, 1)

            run_rounds(dve, CHUNK_PAIRS, round_)
            link.end_loop(CHUNK_PAIRS, steps)


def sum_mlp_over_edges(nc, cst, name, order, table, state, fill, count=None):
    with ExitStack() as ctx:
        s = Scope(nc, ctx, name)
        got = s.sb("got", [P, BUFS, GROUP, H], F32)
        idx = s.sb("idx", [P, BUFS, GROUP], I32)
        ends = s.sb("ends", [P, 2, GROUP, H], F32)
        carry_sb = s.sb("carry_sb", [P, H], F32)
        carry_ps = s.ps("carry_ps", [P, 512], F32)[:, 0:H]
        idx_ready = s.sem("idx_ready")
        gathered = [s.sem(f"gathered{b}") for b in range(BUFS)]
        stored = [s.sem(f"stored{b}") for b in range(BUFS)]
        scanned, ends_in, ends_step, rows_ready = s.sem("scanned"), [s.sem("ends_in0"), s.sem("ends_in1")], s.sem("ends_step"), s.sem("rows_ready")
        added, carried, carry_ready, carry_added, cleared = s.sem("added"), s.sem("carried"), s.sem("carry_ready"), s.sem("carry_added"), s.sem("cleared")
        hot_ready, hot_free, sums_done = s.sem("hot_ready"), s.sem("hot_free"), s.sem("sums")
        if count is not None:
            low, high, counted_nodes = count
            one_low = s.sb("one_low", [P, 2, GROUP, P], BF16)
            one_high = s.sb("one_high", [P, 2, GROUP, NODE_COLS], BF16)
            zero_b = s.sb("zero_b", [P, P], BF16)
            counted = s.ps("counted", [P, 512], F32)[:, 0:NODE_COLS]
        block = ctx.enter_context(nc.Block())
        state_v = state[0:EDGES, :].rearrange("(p t) f -> p (t f)", p=P)
        fill_v = fill[0:EDGES, :].rearrange("(p t) f -> p (t f)", p=P)

        def past_end(i, b, ahead):
            return isinstance(i, int) and i == ROUNDS - 1 and b + ahead >= BUFS

        @block.sync
        def _(sp):
            def load_ends(group, b):
                sp.dma_start(ends[:, b % 2, :, :].rearrange("p u f -> p (u f)"),
                             fill_v[:, bass.ds(group * (GROUP * H), GROUP * H)]).then_inc(ends_in[b % 2], 16)

            load_ends(0, 0)
            sp.wait_ge(cleared, 2)
            sp.wait_ge(ends_step, 1)
            load_ends(1, 1)

            def round_(i):
                for b in range(BUFS):
                    group = i * BUFS + b
                    if not past_end(i, b, 2):
                        sp.wait_ge(ends_step, (group + 1) * GROUP + 1)
                        load_ends(group + 2, b)
                    sp.wait_ge(scanned, (group + 1) * GROUP)
                    sp.dma_start(state_v[:, bass.ds(group * (GROUP * H), GROUP * H)],
                                 got[:, b, :, :].rearrange("p u f -> p (u f)")).then_inc(stored[b], 16)

            run_rounds(sp, ROUNDS, round_)
            for b in range(BUFS):
                sp.wait_ge(stored[b], 16 * ROUNDS)

        @block.gpsimd
        def _(pool):
            gather_groups(pool, table, got, idx, idx_ready, stored, gathered)
            add_carry(pool, order, state, carry_sb, carry_ready, stored, carry_added)

        @block.scalar
        def _(act):
            def stage(group, b):
                nc.scalar.copy(idx[:, b % BUFS, :], order.gather_rows[:, bass.ds(group * GROUP, GROUP)]).then_inc(idx_ready, 1)

            def relu(group, b):
                act.wait_ge(added, group + 1)
                nc.scalar.activation(got[:, b % BUFS, :, :], got[:, b % BUFS, :, :], ACT.Relu).then_inc(rows_ready, 1)

            for group in range(AHEAD):
                stage(group, group)
            relu(0, 0)

            def round_(i):
                for b in range(BUFS):
                    group = i * BUFS + b
                    if not past_end(i, b, AHEAD):
                        act.wait_ge(scanned, group * GROUP + 1)
                        stage(group + AHEAD, b + AHEAD)
                    if not past_end(i, b, 1):
                        relu(group + 1, b + 1)

            run_rounds(act, ROUNDS, round_)

        @block.vector
        def _(dve):
            def fill_step(first, b, u):
                before = ends[:, b % 2, u - 1, :] if u else ends[:, 1 - b % 2, GROUP - 1, :]
                wait_if(dve, ends_step, first + u)
                nc.vector.scalar_tensor_tensor(
                    out=ends[:, b % 2, u, :], in0=before, scalar=order.same[:, bass.ds(first + u, 1)],
                    in1=ends[:, b % 2, u, :], op0=ALU.mult, op1=ALU.add).then_inc(ends_step, 1)

            def sum_step(first, b, u):
                before = got[:, b, u - 1, :] if u else got[:, (b - 1) % BUFS, GROUP - 1, :]
                wait_if(dve, scanned, first + u)
                nc.vector.scalar_tensor_tensor(
                    out=got[:, b, u, :], in0=before, scalar=order.same[:, bass.ds(first + u, 1)],
                    in1=got[:, b, u, :], op0=ALU.mult, op1=ALU.add).then_inc(scanned, 1)

            def add_ends(i, group, b):
                dve.wait_ge(gathered[b % BUFS], (i + b // BUFS + 1) * (16 * GROUP))
                dve.wait_ge(ends_step, (group + 1) * GROUP)
                nc.vector.tensor_tensor(got[:, b % BUFS, :, :], got[:, b % BUFS, :, :], ends[:, b % 2, :, :],
                                        ALU.add).then_inc(added, 1)

            nc.vector.memset(got[:, BUFS - 1, GROUP - 1, :], 0.0).then_inc(cleared, 1)
            nc.vector.memset(ends[:, 1, GROUP - 1, :], 0.0).then_inc(cleared, 1)
            if count is not None:
                nc.vector.memset(zero_b[:, :], 0.0)
            dve.wait_ge(cleared, 2)
            dve.wait_ge(ends_in[0], 16)
            for u in range(GROUP):
                fill_step(0, 0, u)
            add_ends(0, 0, 0)

            def round_(i):
                for b in range(BUFS):
                    group = i * BUFS + b
                    more = not past_end(i, b, 1)
                    if count is not None:
                        wait_if(dve, hot_free, group - 1)
                        at = bass.ds(group * GROUP, GROUP)
                        one_hot(nc, cst, one_low[:, b % 2, :, :], low[:, at], P)
                        one_hot(nc, cst, one_high[:, b % 2, :, :], high[:, at], NODE_COLS).then_inc(hot_ready, 1)
                    if more:
                        dve.wait_ge(ends_in[(b + 1) % 2], (i * 2 + (b + 1) // 2 + 1) * 16)
                    dve.wait_ge(rows_ready, group + 1)
                    for u in range(GROUP):
                        if more:
                            fill_step((group + 1) * GROUP, b + 1, u)
                        sum_step(group * GROUP, b, u)
                    if more:
                        add_ends(i, group + 1, b + 1)

            run_rounds(dve, ROUNDS, round_)
            if count is not None:
                dve.wait_ge(sums_done, 1)
                nc.vector.tensor_copy(counted_nodes.count[:, :], counted)
            dve.wait_ge(carried, 1)
            nc.vector.tensor_copy(carry_sb[:, :], carry_ps).then_inc(carry_ready, 1)

        @block.tensor
        def _(pe):
            if count is not None:
                pe.wait_ge(hot_ready, 1)
                nc.tensor.matmul(counted, zero_b[:, :], zero_b[:, 0:NODE_COLS], start=True, stop=False)

                def round_(i):
                    for b in range(BUFS):
                        pe.wait_ge(hot_ready, i * BUFS + b + 1)
                        for u in range(GROUP):
                            last = nc.tensor.matmul(counted, one_low[:, b % 2, u, :], one_high[:, b % 2, u, :],
                                                    start=False, stop=False)
                        last.then_inc(hot_free, 1)

                run_rounds(pe, ROUNDS, round_)
                nc.tensor.matmul(counted, zero_b[:, :], zero_b[:, 0:NODE_COLS], start=False, stop=True).then_inc(sums_done, 1)
            pe.wait_ge(scanned, EDGE_COLS)
            nc.tensor.matmul(carry_ps, order.carry[:, :], got[:, BUFS - 1, GROUP - 1, :],
                             start=True, stop=True).then_inc(carried, 1)


def gather_groups(pool, table, got, idx, idx_ready, stored, gathered):
    def round_(i):
        for b in range(BUFS):
            pool.wait_ge(idx_ready, i * BUFS + b + 1)
            wait_if(pool, stored[b], i * 16)
            part_wait(pool)
            for u in range(GROUP):
                pool.indirect_dma_start(out=got[:, b, u, :], out_offset=None, in_=table[:, :],
                                        in_offset=rows(idx[:, b, u:u + 1])).then_inc(gathered[b], 16)

    run_rounds(pool, ROUNDS, round_)


def add_carry(pool, order, state, carry_sb, carry_ready, stored, carry_added):
    pool.wait_ge(carry_ready, 1)
    for b in range(BUFS):
        pool.wait_ge(stored[b], 16 * ROUNDS)
    pool.indirect_dma_start(out=state[:, :], out_offset=rows(order.first_end[:, 0:1]), in_=carry_sb[:, :],
                            in_offset=None, compute_op=ALU.add).then_inc(carry_added, 16)
    pool.wait_ge(carry_added, 16)


def sum_over_edges(nc, cst, name, order, table, state):
    with ExitStack() as ctx:
        s = Scope(nc, ctx, name)
        got = s.sb("got", [P, BUFS, GROUP, D], F32)
        idx = s.sb("idx", [P, BUFS, GROUP], I32)
        carry_sb = s.sb("carry_sb", [P, D], F32)
        carry_ps = s.ps("carry_ps", [P, D], F32)
        idx_ready, scanned, cleared = s.sem("idx_ready"), s.sem("scanned"), s.sem("cleared")
        gathered = [s.sem(f"gathered{b}") for b in range(BUFS)]
        stored = [s.sem(f"stored{b}") for b in range(BUFS)]
        carried, carry_ready, carry_added = s.sem("carried"), s.sem("carry_ready"), s.sem("carry_added")
        block = ctx.enter_context(nc.Block())
        state_v = state[0:EDGES, :].rearrange("(p t) f -> p (t f)", p=P)

        @block.sync
        def _(sp):
            def round_(i):
                for b in range(BUFS):
                    group = i * BUFS + b
                    sp.wait_ge(scanned, (group + 1) * GROUP)
                    sp.dma_start(state_v[:, bass.ds(group * (GROUP * D), GROUP * D)],
                                 got[:, b, :, :].rearrange("p u f -> p (u f)")).then_inc(stored[b], 16)

            run_rounds(sp, ROUNDS, round_)
            for b in range(BUFS):
                sp.wait_ge(stored[b], 16 * ROUNDS)

        @block.gpsimd
        def _(pool):
            gather_groups(pool, table, got, idx, idx_ready, stored, gathered)
            add_carry(pool, order, state, carry_sb, carry_ready, stored, carry_added)

        @block.scalar
        def _(act):
            def stage(group, b):
                nc.scalar.copy(idx[:, b % BUFS, :], order.gather_rows[:, bass.ds(group * GROUP, GROUP)]).then_inc(idx_ready, 1)

            for group in range(AHEAD):
                stage(group, group)

            def round_(i):
                for b in range(BUFS):
                    group = i * BUFS + b
                    if not (isinstance(i, int) and i == ROUNDS - 1 and b + AHEAD >= BUFS):
                        act.wait_ge(scanned, group * GROUP + 1)
                        stage(group + AHEAD, b + AHEAD)

            run_rounds(act, ROUNDS, round_)

        @block.vector
        def _(dve):
            nc.vector.memset(got[:, BUFS - 1, GROUP - 1, :], 0.0).then_inc(cleared, 1)
            dve.wait_ge(cleared, 1)

            def round_(i):
                for b in range(BUFS):
                    first = (i * BUFS + b) * GROUP
                    dve.wait_ge(gathered[b], (i + 1) * (16 * GROUP))
                    for u in range(GROUP):
                        before = got[:, b, u - 1, :] if u else got[:, (b - 1) % BUFS, GROUP - 1, :]
                        nc.vector.scalar_tensor_tensor(
                            out=got[:, b, u, :], in0=before, scalar=order.same[:, bass.ds(first + u, 1)],
                            in1=got[:, b, u, :], op0=ALU.mult, op1=ALU.add).then_inc(scanned, 1)
                        dve.wait_ge(scanned, first + u + 1)

            run_rounds(dve, ROUNDS, round_)
            dve.wait_ge(carried, 1)
            nc.vector.tensor_copy(carry_sb[:, :], carry_ps[:, :]).then_inc(carry_ready, 1)

        @block.tensor
        def _(pe):
            pe.wait_ge(scanned, EDGE_COLS)
            nc.tensor.matmul(carry_ps[:, :], order.carry[:, :], got[:, BUFS - 1, GROUP - 1, :],
                             start=True, stop=True).then_inc(carried, 1)


def update_nodes(nc, cst, name, kind, sums, weights, nodes_of, w, x_sb, h_sb, tables, out=None):
    width = 2 * D if kind == "edge" else D
    with ExitStack() as ctx:
        s = Scope(nc, ctx, name)
        t = Temps(s)
        idx = s.sb("idx", [P, 2, 2, CHUNK], I32)
        sum_sb = s.sb("sum_sb", [P, 2, 2, CHUNK, width], F32)
        pair = s.sb("pair", [P, CHUNK, 2 * D], F32)
        pair_t = s.sb("pair_t", [P, CHUNK, P], F32)
        y = s.sb("y", [P, CHUNK, D], F32)
        degree = s.sb("degree", [P, NODE_COLS], F32)
        to_table = s.sb("to_table", [P, 2, 2, CHUNK, D], F32)
        turned = s.ps("turned", [P, 8, P], F32)
        product = s.ps("product", [P, 8, D], F32)
        idx_ready, summed = s.sem("idx_ready"), [s.sem("summed0"), s.sem("summed1")]
        pair_ready, turned_done, pair_t_ready = s.sem("pair"), s.sem("turned"), s.sem("pair_t")
        product_done, product_taken = s.sem("product"), s.sem("taken")
        var_ready, std_ready, table_ready, stored = s.sem("var"), s.sem("std"), s.sem("table"), s.sem("stored")
        link_sem = s.sem("link")
        block = ctx.enter_context(nc.Block())
        rounds = CHUNK_PAIRS
        wide = [P, CHUNK, D]
        normal = kind in ("edge", "conv2", "directed")
        of_sums = len(sums)

        if sums:
            @block.gpsimd
            def _(pool):
                def round_(j):
                    for b in range(2):
                        pool.wait_ge(idx_ready, j * 2 + b + 1)
                        part_wait(pool)
                        for c in range(CHUNK):
                            for k, (order, state) in enumerate(sums):
                                pool.indirect_dma_start(out=sum_sb[:, b, k, c, :], out_offset=None, in_=state[:, :],
                                                        in_offset=rows(idx[:, b, k, c:c + 1])).then_inc(summed[b], 16)

                run_rounds(pool, rounds, round_)

        @block.sync
        def _(sp):
            if tables:
                def round_(j):
                    for b in range(2):
                        sp.wait_ge(table_ready, j * 2 + b + 1)
                        for k, table in enumerate(tables):
                            sp.dma_start(table.rearrange("(p c) f -> p c f", p=P)[:, bass.ds((j * 2 + b) * CHUNK, CHUNK), :],
                                         to_table[:, b, k, :, :]).then_inc(stored, 16)

                run_rounds(sp, rounds, round_)
                sp.wait_ge(stored, 16 * len(tables) * 2 * rounds)
            if out is not None:
                sp.wait_ge(table_ready, 2 * rounds)
                last_col = NODE_COLS - 1
                sp.dma_start(out[0:last_col * P, :].rearrange("(c p) f -> p c f", p=P), x_sb[:, 0:last_col, :]).then_inc(stored, 16)
                sp.dma_start(out[last_col * P:N, :], x_sb[0:LAST_NODES, last_col, :]).then_inc(stored, 16)
                sp.wait_ge(stored, 32)

        @block.scalar
        def _(act):
            if kind == "first":
                nc.scalar.activation(pair[:, :, D:2 * D], x_sb[:, 0:CHUNK, :], ACT.Copy, scale=0.0)

            def make_pair(j, b):
                chunk = j * 2 + b
                at = bass.ds(chunk * CHUNK, CHUNK)
                if kind == "edge":
                    return
                if sums:
                    act.wait_ge(summed[b], (j + 1) * (16 * CHUNK * of_sums))
                wait_if(act, turned_done, chunk)
                if kind == "directed":
                    for c in range(CHUNK):
                        for k in range(2):
                            last = nc.scalar.activation(pair[:, c, k * D:k * D + D], sum_sb[:, b, k, c, :], ACT.Copy,
                                                        scale=nodes_of[k].inv_root[:, bass.ds(chunk * CHUNK + c, 1)])
                    last.then_inc(pair_ready, 1)
                elif kind == "first":
                    nc.scalar.copy(pair[:, :, 0:D], h_sb[:, at, :]).then_inc(pair_ready, 1)
                else:
                    nc.scalar.copy(pair[:, :, 0:D], h_sb[:, at, :])
                    nc.scalar.copy(pair[:, :, D:2 * D], sum_sb[:, b, 0, :, :]).then_inc(pair_ready, 1)

            make_pair(0, 0)

            def round_(j):
                for b in range(2):
                    chunk = j * 2 + b
                    act.wait_ge(turned_done, chunk + 1)
                    nc.scalar.copy(pair_t[:, :, :], turned[:, 0:CHUNK, :]).then_inc(pair_t_ready, 1)
                    if not (isinstance(j, int) and j == rounds - 1 and b == 1):
                        make_pair(j + b, 1 - b)
                    if normal:
                        act.wait_ge(var_ready, chunk + 1)
                        nc.scalar.activation(t.std[:, :], t.var[:, :], ACT.Sqrt, bias=cst.eps[:, 0:1], scale=1.0 / D).then_inc(std_ready, 1)

            run_rounds(act, rounds, round_)

        @block.tensor
        def _(pe):
            def round_(j):
                for b in range(2):
                    chunk = j * 2 + b
                    pe.wait_ge(pair_ready, chunk + 1)
                    wait_if(pe, pair_t_ready, chunk)
                    for c in range(CHUNK):
                        last = nc.tensor.transpose(turned[:, c, :], pair[:, c, :], cst.ident[:, :])
                    last.then_inc(turned_done, 1)
                    pe.wait_ge(pair_t_ready, chunk + 1)
                    wait_if(pe, product_taken, chunk)
                    for c in range(CHUNK):
                        last = nc.tensor.matmul(product[:, c, :], pair_t[:, c, :], weights[:, :], start=True, stop=True)
                    last.then_inc(product_done, 1)

            run_rounds(pe, rounds, round_)

        @block.vector
        def _(dve):
            link = Link(dve, link_sem)

            def stage_rows(b, at):
                part_wait(dve)
                for k, (order, state) in enumerate(sums):
                    last = nc.vector.tensor_copy(idx[:, b, k, :], nodes_of[order].end_row[:, at])
                last.then_inc(idx_ready, 1)

            if kind == "edge":
                link(nc.vector.tensor_tensor(degree[:, :], nodes_of[0].count[:, :], nodes_of[1].count[:, :], ALU.add))
            if sums:
                for b in range(2):
                    stage_rows(b, slice(b * CHUNK, (b + 1) * CHUNK))

            def chunk_steps(j, b, more):
                chunk = j * 2 + b
                at = bass.ds(chunk * CHUNK, CHUNK)
                if kind == "edge":
                    dve.wait_ge(summed[b], (j + 1) * (16 * CHUNK * 2))
                    wait_if(dve, turned_done, chunk)
                    nc.vector.tensor_tensor(pair[:, :, :], sum_sb[:, b, 0, :, :], sum_sb[:, b, 1, :, :], ALU.add).then_inc(pair_ready, 1)
                dve.wait_ge(pair_ready, chunk + 1)
                if sums and more:
                    stage_rows(b, bass.ds((chunk + 2) * CHUNK, CHUNK))
                by_degree = {"edge": (degree, w.edge_out_bias), "first": (nodes_of[0].count, w.degree_row),
                             "step": (nodes_of[0].count, w.degree_row), "last": (nodes_of[0].count, w.degree_row)}
                if kind in by_degree:
                    count, row = by_degree[kind]
                    link(nc.vector.tensor_tensor(y[:, :, :], row[:, :].unsqueeze(1).to_broadcast(wide),
                                                 count[:, at].unsqueeze(2).to_broadcast(wide), ALU.mult))
                    bias = y[:, :, :]
                else:
                    row = {"conv1": w.conv_bias[0], "conv2": w.conv_bias[1], "directed": w.directed_bias}[kind]
                    bias = row[:, :].unsqueeze(1).to_broadcast(wide)
                dve.wait_ge(product_done, chunk + 1)
                nc.vector.tensor_tensor(y[:, :, :], product[:, 0:CHUNK, :], bias, ALU.add).then_inc(product_taken, 1)
                dve.wait_ge(product_taken, chunk + 1)
                if tables:
                    wait_if(dve, stored, j * (16 * 2 * len(tables)))
                if kind in ("conv1", "first", "step"):
                    ins = nc.vector.tensor_scalar(to_table[:, b, 0, :, :], y[:, :, :], 0.0, None, ALU.max)
                    ins.then_inc(table_ready, 1)
                    dve.wait_ge(table_ready, chunk + 1)
                    if kind == "conv1":
                        part_wait(dve)
                        link(nc.vector.tensor_copy(h_sb[:, at, :], to_table[:, b, 0, :, :]))
                    return
                if kind in ("conv2", "last"):
                    link(nc.vector.tensor_scalar(y[:, :, :], y[:, :, :], 0.0, None, ALU.max))
                ins = nc.vector.tensor_tensor(x_sb[:, at, :], x_sb[:, at, :], y[:, :, :], ALU.add)
                if kind == "last":
                    ins.then_inc(table_ready, 1)
                    dve.wait_ge(table_ready, chunk + 1)
                    return
                link(ins)

                def act_part(ins):
                    ins.then_inc(var_ready, 1)
                    dve.wait_ge(std_ready, chunk + 1)

                normalise(nc, link, act_part, h_sb[:, at, :], x_sb[:, at, :], t)
                if kind == "edge":
                    part_wait(dve)
                    nc.vector.tensor_copy(to_table[:, b, 0, :, :], h_sb[:, at, :]).then_inc(table_ready, 1)
                elif kind == "conv2":
                    for k in range(2):
                        last = nc.vector.tensor_tensor(to_table[:, b, k, :, :], h_sb[:, at, :],
                                                       nodes_of[k].inv_root[:, at].unsqueeze(2).to_broadcast(wide), ALU.mult)
                    last.then_inc(table_ready, 1)

            steps = {"edge": 2 * 8, "conv1": 2, "conv2": 2 * 8, "directed": 2 * 7, "first": 2, "step": 2, "last": 4}[kind]
            link.start_loop()

            def round_(j):
                link.iteration(j, steps)
                for b in range(2):
                    chunk_steps(j, b, not (isinstance(j, int) and j == rounds - 1))

            run_rounds(dve, rounds, round_)
            link.end_loop(rounds, steps)


def graph_layers(nc, x, src, dst, *weights_and_out):
    weights, out = weights_and_out[:-1], weights_and_out[-1]

    def dram(name, shape, dtype=F32):
        return nc.dram_tensor(name, shape, dtype, kind="Internal").ap()

    key_rows = dram("key_rows", [EDGES])
    by_src_edges, by_dst_edges = dram("by_src_edges", [EDGES, 2], I32), dram("by_dst_edges", [EDGES, 2], I32)
    source_table, target_table = dram("source_table", [NODES, H]), dram("target_table", [NODES, H])
    tables = [dram("table0", [NODES, D]), dram("table1", [NODES, D])]
    wide_states = [dram(f"wide_state{k}", [EDGES + P, H]) for k in range(2)]
    states = [dram(f"state{k}", [EDGES + P, D]) for k in range(2)]
    fills = [dram(f"fill{k}", [EDGES, H]) for k in range(2)]

    with ExitStack() as ctx:
        s = Scope(nc, ctx, "")
        cst = Constants(s)
        nodes_of = [Nodes(s, side) for side in ("src", "dst")]
        dst_low, dst_high = s.sb("dst_low", [P, TILES], BF16), s.sb("dst_high", [P, TILES], BF16)
        constants(nc, cst)
        with ExitStack() as raw_ctx:
            r = Scope(nc, raw_ctx, "raw_")
            raw = EdgeColumns(r, dst_low, dst_high)
            load_edges(nc, cst, "ld_", raw, src, dst, key_rows)
            count_edges(nc, cst, raw.low[0], raw.high[0], nodes_of[0])
            place_nodes(nc, cst, "by_src_", nodes_of[0])
            sort_edges(nc, cst, "sort_", raw, nodes_of[0], key_rows, by_src_edges, fills,
                       [(wide_states[0], H), (wide_states[1], H), (states[0], D), (states[1], D)])
        orders = [Order(s, side) for side in ("src", "dst")]
        unsorted = s.sb("unsorted", [P, 1], I32)
        edge_order(nc, cst, "src_order_", orders[0], sorted_edges=by_src_edges)
        edge_order(nc, cst, "dst_order_", orders[1], keys=dst, others=src, unsorted=unsorted)
        w = Weights(s)
        prepare_weights(nc, cst, w, weights)
        x_sb = s.sb("x_sb", [P, NODE_COLS, D], F32)

        first_layer_tables(nc, cst, w, orders[0], nodes_of[0], x, x_sb, source_table, target_table, fills[0])
        sum_mlp_over_edges(nc, cst, "e0_", orders[0], source_table, wide_states[0], fills[0],
                           count=(dst_low, dst_high, nodes_of[1]))
        place_nodes(nc, cst, "by_dst_", nodes_of[1])
        with nc.If(nc.values_load(unsorted[0:1, 0:1], min_val=0, max_val=EDGES) > 0):
            with ExitStack() as raw_ctx:
                raw = EdgeColumns(Scope(nc, raw_ctx, "raw_dst_"), dst_low, dst_high)
                load_edges(nc, cst, "ld_dst_", raw, dst, src, key_rows)
                sort_edges(nc, cst, "sort_dst_", raw, nodes_of[1], key_rows, by_dst_edges)
            edge_order(nc, cst, "sorted_dst_order_", orders[1], sorted_edges=by_dst_edges)
        fill_starts(nc, cst, orders[1], nodes_of[1], target_table, fills[1])
        sum_mlp_over_edges(nc, cst, "e1_", orders[1], source_table, wide_states[1], fills[1])
        h_sb = s.sb("h_sb", [P, NODE_COLS, D], F32)
        update_nodes(nc, cst, "ne_", "edge", [(0, wide_states[0]), (1, wide_states[1])], w.edge_out, nodes_of, w,
                     x_sb, h_sb, tables[:1])
        sum_over_edges(nc, cst, "c1_", orders[1], tables[0], states[1])
        update_nodes(nc, cst, "n1_", "conv1", [(1, states[1])], w.conv[0], nodes_of, w, x_sb, h_sb, tables[:1])
        sum_over_edges(nc, cst, "c2_", orders[1], tables[0], states[1])
        update_nodes(nc, cst, "n2_", "conv2", [(1, states[1])], w.conv[1], nodes_of, w, x_sb, h_sb, tables)
        sum_over_edges(nc, cst, "d0_", orders[0], tables[1], states[0])
        sum_over_edges(nc, cst, "d1_", orders[1], tables[0], states[1])
        update_nodes(nc, cst, "nd_", "directed", [(0, states[0]), (1, states[1])], w.directed, nodes_of, w,
                     x_sb, h_sb, [])
        update_nodes(nc, cst, "s0_", "first", [], w.steps, nodes_of, w, x_sb, h_sb, tables[:1])
        for step in range(1, 4):
            sum_over_edges(nc, cst, f"p{step}_", orders[0], tables[0], states[0])
            update_nodes(nc, cst, f"s{step}_", "last" if step == 3 else "step", [(0, states[0])], w.steps, nodes_of, w,
                         x_sb, h_sb, [] if step == 3 else tables[:1], out if step == 3 else None)


_INS = ['x', 'src', 'dst', 'L0_gnn_W1', 'L0_gnn_b1', 'L0_gnn_W2', 'L0_gnn_b2', 'L1_gnn_W1_root', 'L1_gnn_W1_rel',
        'L1_gnn_b1', 'L1_gnn_W2_root', 'L1_gnn_W2_rel', 'L1_gnn_b2', 'L2_gnn_W_src', 'L2_gnn_b_src', 'L2_gnn_W_dst',
        'L2_gnn_b_dst', 'L3_gnn_W1', 'L3_gnn_W2', 'L3_gnn_W3', 'L3_gnn_W4']


def kernel(**inputs):
    import numpy as _np
    import concourse.bacc as _bacc
    from concourse import mybir as _mybir
    from concourse.bass_utils import run_bass_kernel_spmd as _run

    nc = _bacc.Bacc("TRN2", target_bir_lowering=False, num_devices=1)
    arrays, args = {}, []
    for name in _INS:
        a = _np.ascontiguousarray(inputs[name])
        arrays[f"in_{name}_dram"] = a
        args.append(nc.dram_tensor(f"in_{name}_dram", a.shape, _mybir.dt.from_np(a.dtype), kind="ExternalInput").ap())
    out = nc.dram_tensor("out_0_dram", (N, D), F32, kind="ExternalOutput").ap()
    graph_layers(nc, *args, out)
    r = _run(nc, [arrays], core_ids=[0])
    return r.results[0]["out_0_dram"]
```
